# Optimizing a Trainium2 kernel written in Bass

```python
import numpy as np
import jax
import jax.numpy as jnp

def _softmax(x, axis=-1):
    return jax.nn.softmax(x, axis=axis)

def _gelu(x):
    return jax.nn.gelu(x, approximate=True)

def _silu(x):
    return jax.nn.silu(x)

def _sigmoid(x):
    return jax.nn.sigmoid(x)

def _layernorm(x, axis=-1, eps=1e-05):
    m = jnp.mean(x, axis=axis, keepdims=True)
    v = jnp.var(x, axis=axis, keepdims=True)
    return (x - m) / jnp.sqrt(v + eps)

def _scatter_add(tgt, idx, src, axis=0):
    return tgt.at[idx].add(src)

def _segment_sum(src, seg, n):
    return jax.ops.segment_sum(src, seg, n)
kernel_name = 'mk_vit_tower_cls_d1_tok_img256_r4_f965d7'

def setup_inputs(seed: int=0):
    np.random.seed(seed)
    _w = jnp.asarray

    def _rec_inputs():
        import jax
        import jax.numpy as jnp
        _rk = jax.random.key(seed)
        x = -0.000596345 + 1.00056 * jax.random.normal(jax.random.fold_in(_rk, 1), (32, 64, 64, 3), jnp.float32)
        cls_tok = 0.02 * jax.random.normal(jax.random.fold_in(_rk, 5), (1, 1, 64), jnp.float32)
        return (x, cls_tok)
    x, cls_tok = _rec_inputs()

    def _L0_tok_setup():
        import jax, jax.numpy as jnp
        import numpy as np
        M1 = 20
        M2 = 20

        def _spectral_conv(x, w):
            B, Cin, H, W = x.shape
            x_ft = jnp.fft.rfft2(x, norm='ortho')
            out = jnp.einsum('bixy,ioxy->boxy', x_ft[:, :, :M1, :M2], w.astype(x_ft.dtype))
            out_ft = jnp.zeros((B, w.shape[1], H, W // 2 + 1), dtype=x_ft.dtype)
            out_ft = out_ft.at[:, :, :M1, :M2].set(out)
            return jnp.fft.irfft2(out_ft, s=(H, W), norm='ortho')

        def _gelu(x):
            return jax.nn.gelu(x, approximate=False)
        key = jax.random.key(seed)
        ks = jax.random.split(key, 16)
        B, H, W, width = (16, 64, 64, 32)
        scale = 1.0 / (width * width)
        d = {}
        d['coords'] = jax.random.normal(ks[0], (B, H, W, 3), dtype=jnp.float32)
        d['fc0_w'] = jax.random.normal(ks[1], (3, width), dtype=jnp.float32) * 0.1
        d['fc0_b'] = jnp.zeros((width,), dtype=jnp.float32)
        for i in range(4):
            d[f'sw{i}'] = scale * jax.random.normal(ks[2 + i], (width, width, M1, M2), dtype=jnp.float32)
            d[f'cw{i}'] = jax.random.normal(ks[6 + i], (width, width), dtype=jnp.float32) * 0.1
            d[f'cb{i}'] = jnp.zeros((width,), dtype=jnp.float32)
        d['fc1_w'] = jax.random.normal(ks[10], (width, 64), dtype=jnp.float32) * 0.1
        d['fc1_b'] = jnp.zeros((64,), dtype=jnp.float32)
        d['fc2_w'] = jax.random.normal(ks[11], (64, 1), dtype=jnp.float32) * 0.1
        d['fc2_b'] = jnp.zeros((1,), dtype=jnp.float32)
        return d
    _L0_tok_all = _L0_tok_setup()
    _L0_tok_in = {k: v for k, v in _L0_tok_all.items() if k in ('fc0_w', 'fc0_b', 'sw0', 'cw0', 'cb0', 'sw1', 'cw1', 'cb1', 'sw2', 'cw2', 'cb2', 'sw3', 'cw3', 'cb3', 'fc1_w', 'fc1_b', 'fc2_w', 'fc2_b')}
    del _L0_tok_all

    def _L0_attn_setup():
        import jax, jax.numpy as jnp
        import numpy as np
        import math
        RADIUS = 32
        NUM_HEADS = 8
        B, L, DIM = (2, 2048, 64)
        key = jax.random.key(seed)
        k1, k2, k3, k4, k5 = jax.random.split(key, 5)
        s_in = 1.0 / math.sqrt(DIM)
        return {'x': jax.random.normal(k1, (B, L, DIM), dtype=jnp.float32), 'w_qkv': jax.random.normal(k2, (DIM, 3 * DIM), dtype=jnp.float32) * s_in, 'b_qkv': jax.random.normal(k3, (3 * DIM,), dtype=jnp.float32) * 0.01, 'w_proj': jax.random.normal(k4, (DIM, DIM), dtype=jnp.float32) * s_in, 'b_proj': jax.random.normal(k5, (DIM,), dtype=jnp.float32) * 0.01}
    _L0_attn_all = _L0_attn_setup()
    _L0_attn_in = {k: v for k, v in _L0_attn_all.items() if k in ('w_qkv', 'b_qkv', 'w_proj', 'b_proj')}
    del _L0_attn_all

    def _L0_ffn_setup():
        import jax, jax.numpy as jnp
        import numpy as np
        TOP_K = 6
        LN_EPS = 1e-05
        key = jax.random.key(seed)
        ks = jax.random.split(key, 4)
        B, S, D, E = (2, 64, 64, 64)
        x = jax.random.normal(ks[0], (B, S, D), dtype=jnp.float32)
        gate_w = jax.random.normal(ks[1], (E, D), dtype=jnp.float32) * 0.02
        lattice_weights = jax.random.normal(ks[2], (E, D, D), dtype=jnp.float32) * 0.02
        out_w = jax.random.normal(ks[3], (D, D), dtype=jnp.float32) * 0.02
        out_b = jnp.zeros((D,), dtype=jnp.float32)
        ln_g = jnp.ones((D,), dtype=jnp.float32)
        ln_b = jnp.zeros((D,), dtype=jnp.float32)
        return {'x': x, 'gate_w': gate_w, 'lattice_weights': lattice_weights, 'out_w': out_w, 'out_b': out_b, 'ln_g': ln_g, 'ln_b': ln_b}
    _L0_ffn_all = _L0_ffn_setup()
    _L0_ffn_in = {k: v for k, v in _L0_ffn_all.items() if k in ('gate_w', 'lattice_weights', 'out_w', 'out_b', 'ln_g', 'ln_b')}
    del _L0_ffn_all
    return {'x': x, 'cls_tok': cls_tok, 'L0_tok_fc0_w': _L0_tok_in['fc0_w'], 'L0_tok_fc0_b': _L0_tok_in['fc0_b'], 'L0_tok_sw0': _L0_tok_in['sw0'], 'L0_tok_cw0': _L0_tok_in['cw0'], 'L0_tok_cb0': _L0_tok_in['cb0'], 'L0_tok_sw1': _L0_tok_in['sw1'], 'L0_tok_cw1': _L0_tok_in['cw1'], 'L0_tok_cb1': _L0_tok_in['cb1'], 'L0_tok_sw2': _L0_tok_in['sw2'], 'L0_tok_cw2': _L0_tok_in['cw2'], 'L0_tok_cb2': _L0_tok_in['cb2'], 'L0_tok_sw3': _L0_tok_in['sw3'], 'L0_tok_cw3': _L0_tok_in['cw3'], 'L0_tok_cb3': _L0_tok_in['cb3'], 'L0_tok_fc1_w': _L0_tok_in['fc1_w'], 'L0_tok_fc1_b': _L0_tok_in['fc1_b'], 'L0_tok_fc2_w': _L0_tok_in['fc2_w'], 'L0_tok_fc2_b': _L0_tok_in['fc2_b'], 'L0_attn_w_qkv': _L0_attn_in['w_qkv'], 'L0_attn_b_qkv': _L0_attn_in['b_qkv'], 'L0_attn_w_proj': _L0_attn_in['w_proj'], 'L0_attn_b_proj': _L0_attn_in['b_proj'], 'L0_ffn_gate_w': _L0_ffn_in['gate_w'], 'L0_ffn_lattice_weights': _L0_ffn_in['lattice_weights'], 'L0_ffn_out_w': _L0_ffn_in['out_w'], 'L0_ffn_out_b': _L0_ffn_in['out_b'], 'L0_ffn_ln_g': _L0_ffn_in['ln_g'], 'L0_ffn_ln_b': _L0_ffn_in['ln_b']}

def reference(x, cls_tok, L0_tok_fc0_w, L0_tok_fc0_b, L0_tok_sw0, L0_tok_cw0, L0_tok_cb0, L0_tok_sw1, L0_tok_cw1, L0_tok_cb1, L0_tok_sw2, L0_tok_cw2, L0_tok_cb2, L0_tok_sw3, L0_tok_cw3, L0_tok_cb3, L0_tok_fc1_w, L0_tok_fc1_b, L0_tok_fc2_w, L0_tok_fc2_b, L0_attn_w_qkv, L0_attn_b_qkv, L0_attn_w_proj, L0_attn_b_proj, L0_ffn_gate_w, L0_ffn_lattice_weights, L0_ffn_out_w, L0_ffn_out_b, L0_ffn_ln_g, L0_ffn_ln_b):
    import jax
    import jax.numpy as jnp

    def _L0_tok_ref(coords, fc0_w, fc0_b, sw0, cw0, cb0, sw1, cw1, cb1, sw2, cw2, cb2, sw3, cw3, cb3, fc1_w, fc1_b, fc2_w, fc2_b):
        import jax, jax.numpy as jnp
        import numpy as np
        M1 = 20
        M2 = 20

        def _spectral_conv(x, w):
            B, Cin, H, W = x.shape
            x_ft = jnp.fft.rfft2(x, norm='ortho')
            out = jnp.einsum('bixy,ioxy->boxy', x_ft[:, :, :M1, :M2], w.astype(x_ft.dtype))
            out_ft = jnp.zeros((B, w.shape[1], H, W // 2 + 1), dtype=x_ft.dtype)
            out_ft = out_ft.at[:, :, :M1, :M2].set(out)
            return jnp.fft.irfft2(out_ft, s=(H, W), norm='ortho')

        def _gelu(x):
            return jax.nn.gelu(x, approximate=False)
        x = coords @ fc0_w + fc0_b
        x = jnp.transpose(x, (0, 3, 1, 2))
        for sw, cw, cb in ((sw0, cw0, cb0), (sw1, cw1, cb1), (sw2, cw2, cb2), (sw3, cw3, cb3)):
            x1 = _spectral_conv(x, sw)
            x2 = jnp.einsum('bchw,oc->bohw', x, cw) + cb[None, :, None, None]
            x = _gelu(x1 + x2)
        x = jnp.transpose(x, (0, 2, 3, 1))
        x = _gelu(x @ fc1_w + fc1_b)
        return (x @ fc2_w + fc2_b)[..., 0]

    def _L0_attn_ref(x, w_qkv, b_qkv, w_proj, b_proj):
        import jax, jax.numpy as jnp
        import numpy as np
        import math
        RADIUS = 32
        NUM_HEADS = 8
        B, L, DIM = (2, 2048, 64)
        B, L, dim = x.shape
        H = NUM_HEADS
        hd = dim // H
        R = RADIUS
        W = 2 * R + 1
        scale = math.sqrt(hd)
        qkv = x @ w_qkv + b_qkv
        qkv = qkv.reshape(B, L, 3, H, hd)
        qkv = jnp.transpose(qkv, (2, 0, 3, 1, 4))
        q = qkv[0].reshape(B * H, L, hd)
        k = qkv[1].reshape(B * H, L, hd)
        v = qkv[2].reshape(B * H, L, hd)
        k_p = jnp.pad(k, ((0, 0), (R, R), (0, 0)))
        v_p = jnp.pad(v, ((0, 0), (R, R), (0, 0)))
        idx = jnp.arange(L)[:, None] + jnp.arange(W)[None, :]
        k_w = k_p[:, idx]
        v_w = v_p[:, idx]
        scores = jnp.einsum('bld,blwd->blw', q, k_w) / scale
        attn = jax.nn.softmax(scores, axis=-1)
        out = jnp.einsum('blw,blwd->bld', attn, v_w)
        out = out.reshape(B, H, L, hd)
        out = jnp.transpose(out, (0, 2, 1, 3)).reshape(B, L, dim)
        return out @ w_proj + b_proj

    def _L0_ffn_ref(x, gate_w, lattice_weights, out_w, out_b, ln_g, ln_b):
        import jax, jax.numpy as jnp
        import numpy as np
        TOP_K = 6
        LN_EPS = 1e-05
        logits = jnp.einsum('bsd,ed->bse', x, gate_w)
        top_logits, indices = jax.lax.top_k(logits, TOP_K)
        scores = jax.nn.softmax(top_logits, axis=-1)
        W_sel = lattice_weights[indices]
        xW = jnp.einsum('bsd,bskde->bske', x, W_sel)
        lattice_out = jnp.einsum('bske,bsk->bse', xW, scores)
        proj = jnp.einsum('bsd,ed->bse', lattice_out, out_w) + out_b
        h = x + proj
        mu = jnp.mean(h, axis=-1, keepdims=True)
        var = jnp.mean(jnp.square(h - mu), axis=-1, keepdims=True)
        return (h - mu) * jax.lax.rsqrt(var + LN_EPS) * ln_g + ln_b
    h = _L0_tok_ref(x, L0_tok_fc0_w, L0_tok_fc0_b, L0_tok_sw0, L0_tok_cw0, L0_tok_cb0, L0_tok_sw1, L0_tok_cw1, L0_tok_cb1, L0_tok_sw2, L0_tok_cw2, L0_tok_cb2, L0_tok_sw3, L0_tok_cw3, L0_tok_cb3, L0_tok_fc1_w, L0_tok_fc1_b, L0_tok_fc2_w, L0_tok_fc2_b)
    h = jnp.concatenate([jnp.broadcast_to(cls_tok, (h.shape[0], 1, h.shape[2])), h], axis=1)
    h = h + _L0_attn_ref(_layernorm(h, axis=-1), L0_attn_w_qkv, L0_attn_b_qkv, L0_attn_w_proj, L0_attn_b_proj)
    h = h + _L0_ffn_ref(_layernorm(h, axis=-1), L0_ffn_gate_w, L0_ffn_lattice_weights, L0_ffn_out_w, L0_ffn_out_b, L0_ffn_ln_g, L0_ffn_ln_b)
    return h

_drawn_inputs = setup_inputs


def setup_inputs(seed=0):
    import zlib

    import numpy as np

    out = dict(_drawn_inputs(seed))
    spreads = {'L0_tok_fc0_b': (0.0, 0.1),
     'L0_tok_cb0': (0.0, 0.1),
     'L0_tok_cb1': (0.0, 0.1),
     'L0_tok_cb2': (0.0, 0.1),
     'L0_tok_cb3': (0.0, 0.1),
     'L0_tok_fc1_b': (0.0, 0.1),
     'L0_ffn_out_b': (0.0, 0.1),
     'L0_ffn_ln_g': (1.0, 0.2),
     'L0_ffn_ln_b': (0.0, 0.1)}
    factors = {'L0_tok_sw0': 8.0,
     'L0_tok_sw1': 8.0,
     'L0_tok_sw2': 8.0,
     'L0_tok_sw3': 8.0,
     'L0_ffn_gate_w': 6.68,
     'L0_ffn_lattice_weights': 5.434,
     'L0_ffn_out_w': 5.365}
    for name, (base, spread) in spreads.items():
        noise = np.random.default_rng([zlib.crc32(name.encode()), seed]).standard_normal(out[name].shape)
        drawn = base * np.exp(spread * noise) if base else spread * noise
        out[name] = jnp.asarray(drawn.astype(out[name].dtype))
    for name, factor in factors.items():
        out[name] = (out[name] * factor).astype(out[name].dtype)
    return out
```

```python
from contextlib import ExitStack

import concourse.bass as bass
from concourse import mybir

NIMG, GRID, CH, MODES, LAYERS = 32, 64, 32, 20, 4
FC = 64
RI = 2
B4 = 4
GROUPS = 2
STREAMS = 2
SIMG = B4 * GROUPS
PASSES = NIMG // (STREAMS * SIMG)
H2 = 2
HH = GRID // H2
PIX = GRID * GRID
BANK = 512
KYG = MODES // B4
KXD = MODES // B4
MIXB = KXD * KYG
KOUT = RI * MODES

N_XT = PIX // BANK
N_T1 = N_XT
N_TR = MODES // B4
N_F = 2
N_MIX = (MIXB + 3) // 4
N_G = MODES // B4
N_G2 = HH // 4
N_X = PIX // BANK

TOK = GRID + 1
HEADS, HD = 8, 8
EXPERTS, TOPK = 64, 6
RADIUS = 32
EPS = 1e-5
NT = NIMG * TOK
BC = 4
NC = NIMG // BC
CT = BC * TOK
NZ = 5
ZT = NT // NZ
LW = EXPERTS + 2
SENTINEL = -3.0e38
LAG = 3
TAIL_LOADS = 15

F32 = mybir.dt.float32
ALU = mybir.AluOpType
ACT = mybir.ActivationFunctionType
AX = mybir.AxisListType


class Count:

    def __init__(self, sem, per_turn, unit=1, credit=0):
        self.sem, self.stride, self.unit, self.credit = sem, per_turn * unit, unit, credit


class Turns:

    def __init__(self, eng, name, counts):
        self.eng = eng
        self.base = {n: eng.alloc_register(f"{name}_{n}") for n in sorted({c.stride for c in counts})}
        self.value = eng.alloc_register(f"{name}_value")
        self.second = eng.alloc_register(f"{name}_second")
        for r in self.base.values():
            eng.reg_mov(r, 0)

    def wait(self, count, done):
        self.eng.reg_add(self.value, self.base[count.stride], done * count.unit + count.credit)
        self.eng.wait_ge(count.sem, self.value)

    def wait_both(self, count, done, other, other_done):
        self.eng.reg_add(self.value, self.base[count.stride], done * count.unit + count.credit)
        self.eng.reg_add(self.second, self.base[other.stride], other_done * other.unit + other.credit)
        self.eng.wait_ge(count.sem, self.value)
        self.eng.wait_ge(other.sem, self.second)

    def next(self, counts):
        for n in sorted({c.stride for c in counts}):
            self.eng.reg_add(self.base[n], self.base[n], n)


def vit_kernel(nc, xin, fc0_w, fc0_b, spec_w, conv_wb, fc1_w, fc1_b, fc2_w, fc2_b,
               w_qkv, b_qk, b_v, w_proj, b_proj, gate_w, w_expert, out_w, out_b, ln_g, ln_b, cls_rows,
               head_mask, band, band4, sel_in, dft_w, dft_h, idft_h, idft_w, ident_in,
               spec_scr, hid_scr, out):
    ctx = ExitStack()
    with ctx:
        def sb(name, shape, dt=F32):
            return ctx.enter_context(nc.sbuf_tensor(name, shape, dt))

        def sem(name):
            return ctx.enter_context(nc.semaphore(name))

        X = sb("X", [128, STREAMS, GROUPS, PIX])
        XT = sb("XT", [128, 2, BANK])
        T1 = sb("T1", [128, KOUT, GRID])
        TR = sb("TR", [128, B4, MODES, CH])
        SPEC = sb("SPEC", [128, KYG, MODES, RI * SIMG])
        SW = sb("SW", [128, 2, B4, B4 * KYG * CH])
        MIXED = sb("MIXED", [128, MIXB * 128])
        MODE = sb("MODE", [128, GROUPS, MODES, B4 * CH])
        G = sb("G", [128, GRID * RI, MODES])
        GT = sb("GT", [H2 * KOUT, HH, 128])
        DW = sb("DW", [128, H2 * KOUT])
        DH = sb("DH", [128, KOUT])
        EH = sb("EH", [KOUT, GRID * RI])
        EW = sb("EW", [H2 * KOUT, H2 * GRID])
        ident = sb("ident", [128, 128])
        CWALL = sb("CWALL", [128, LAYERS, 129])
        CW = sb("CW", [128, 129])
        W0 = sb("W0", [3 * B4, 128])
        B0 = sb("B0", [128, 1])
        W1 = sb("W1", [128, 2, 128])
        B1 = sb("B1", [128, 1])
        W2 = sb("W2", [128, CH])
        B2 = sb("B2", [128, 1])
        WQKV, WP = sb("WQKV", [GRID, 3 * GRID]), sb("WP", [GRID, GRID])
        BQK, BV, BP = sb("BQK", [GRID, 2]), sb("BV", [TOK, GRID]), sb("BP", [TOK, GRID])
        GATE, WO, OB = sb("GATE", [GRID, EXPERTS]), sb("WO", [GRID, GRID]), sb("OB", [TOK, GRID])
        LNG, LNB = sb("LNG", [TOK, GRID]), sb("LNB", [TOK, GRID])
        HM = sb("HM", [GRID, HEADS])
        BAND = sb("BAND", [TOK, TOK])
        BAND4 = sb("BAND4", [TOK, 4 * TOK])
        WE = sb("WE", [128, EXPERTS // 2, GRID])
        COIN = sb("COIN", [3 * B4, 2, BANK])
        FH = [MIXED[:, i * BANK:(i + 1) * BANK] for i in range(4)]
        HO = G[:, :, :].rearrange("p a b -> p (a b)")[:, 0:4 * BANK].rearrange("p (a b) -> p a b", a=4)

        PSALL = ctx.enter_context(nc.psum_tensor("PSALL", [128, 8, BANK], F32))
        PS = [PSALL[:, i, :] for i in range(8)]

        xt_bank, t1_bank, tr_bank, sp_bank = PS[0:2], PS[2:4], PS[0:2], PS[2:4]
        mix_bank, g_bank, gt_bank, x_bank = PS[4:6], PS[6:8], PS[4:6], PS[6:8]

        U = STREAMS
        consts = sem("consts_loaded")
        zeroed = sem("psum_and_ring_zeroed")
        credits = sem("credits_given")
        xt_full, xt_ready = Count(sem("xt_full"), U * GROUPS * N_XT), Count(sem("xt_ready"), U * GROUPS * N_XT, credit=2)
        t1_full, t1_ready = Count(sem("t1_full"), U * GROUPS * N_T1, credit=2), Count(sem("t1_ready"), U * GROUPS * N_T1)
        tr_full, tr_ready = Count(sem("tr_full"), U * GROUPS * N_TR, credit=1), Count(sem("tr_ready"), U * GROUPS * N_TR, credit=1)
        sp_full, sp_ready = Count(sem("sp_full"), U * GROUPS * N_F, credit=1), Count(sem("sp_ready"), U * GROUPS * N_F, credit=1)
        mix_full, mix_ready = Count(sem("mix_full"), U * N_MIX, credit=1), Count(sem("mix_ready"), U * N_MIX)
        piece_used = Count(sem("weights_piece_used"), U * KXD, credit=2)
        g_full, g_ready = Count(sem("g_full"), U * GROUPS * N_G, credit=GROUPS * N_G), Count(sem("g_ready"), U * GROUPS * N_G)
        gt_full, gt_ready = Count(sem("gt_full"), U * GROUPS * N_G2, credit=1), Count(sem("gt_ready"), U * GROUPS * N_G2, credit=2)
        x_full, x_ready = Count(sem("x_full"), U * GROUPS * N_X, credit=1), Count(sem("x_ready"), U * GROUPS * N_X, credit=2)
        piece_in = [Count(sem(f"weights_piece_loaded{i}"), U * KXD // 2, unit=64) for i in range(2)]
        stored = Count(sem("spectrum_stored"), U, unit=64, credit=1)
        loaded = [Count(sem(f"modes_loaded{g}"), U, unit=64) for g in range(GROUPS)]
        cw_set = Count(sem("layer_weights_set"), 1)
        N0 = STREAMS * GROUPS * N_X
        NF = 2 * N0
        x0_full, x0_ready = Count(sem("x0_full"), N0), Count(sem("x0_ready"), N0)
        fc1_full, fc1_ready = Count(sem("fc1_full"), NF), Count(sem("fc1_ready"), NF)
        fc2_full, fc2_ready = Count(sem("fc2_full"), NF), Count(sem("fc2_ready"), N0 // 2)
        ho_out = Count(sem("hidden_stored"), STREAMS * GROUPS, unit=64)
        co_in = [Count(sem(f"coords_loaded{i}"), STREAMS * GROUPS * N_X // 2, unit=16) for i in range(2)]
        pass_done = Count(sem("pass_done"), 1)
        LAYER_COUNTS = [xt_full, xt_ready, t1_full, t1_ready, tr_full, tr_ready, sp_full, sp_ready, mix_full, mix_ready,
                        piece_used, g_full, g_ready, gt_full, gt_ready, x_full, x_ready, stored, cw_set] + loaded + piece_in
        PASS_COUNTS = [x0_full, x0_ready, fc1_full, fc1_ready, fc2_full, fc2_ready, ho_out, pass_done] + co_in

        arena = X[:].rearrange("p s g n -> p (s g n)")
        H = arena[0:TOK, 0:2048].rearrange("p (b d) -> p b d", b=NIMG)
        Y = arena[0:TOK, 2048:6144].rearrange("p (b t d) -> p b t d", b=NIMG, t=2)
        TMP = arena[0:TOK, 6144:8192].rearrange("p (b d) -> p b d", b=NIMG)
        YT = arena[:, 8192:8192 + NT]
        QT = arena[0:GRID, 10272:10272 + NT]
        KT = arena[0:GRID, 12352:12352 + NT]
        V = T1[0:TOK].rearrange("p a b -> p (a b)")[:, 0:2048].rearrange("p (b d) -> p b d", b=NIMG)
        O = TR[0:TOK].rearrange("p a b c -> p (a b c)")[:, 0:2048].rearrange("p (b d) -> p b d", b=NIMG)
        modes_mem = MODE[:].rearrange("p a b c -> p (a b c)")
        KM = modes_mem[0:GRID, 0:2 * HEADS * CT].rearrange("p (r h t) -> p r h t", r=2, h=HEADS)
        sw_mem = SW[:].rearrange("p a b c -> p (a b c)")
        HT = HEADS * TOK
        PR = sw_mem[0:TOK, 0:4 * HT].rearrange("p (r h t) -> p r h t", r=4, h=HEADS)
        PM = sw_mem[0:TOK, 4 * HT:7 * HT].rearrange("p (r h t) -> p r h t", r=3, h=HEADS)
        PT = sw_mem[0:TOK, 7 * HT:9 * HT].rearrange("p (r h t) -> p r h t", r=2, h=HEADS)
        OT = MIXED[0:GRID, 0:2 * CT].rearrange("p (r t) -> p r t", r=2)
        LG = arena[0:TOK, 12352:12352 + NIMG * LW].rearrange("p (b e) -> p b e", b=NIMG)
        LR = MIXED[0:TOK, 0:NIMG * LW].rearrange("p (b e) -> p b e", b=NIMG)
        SC = T1[0:TOK].rearrange("p a b -> p (a b)")[:, 0:2048].rearrange("p (b e) -> p b e", b=NIMG)
        ST = arena[0:EXPERTS, 10272:10272 + NT]
        ZX = sw_mem[:, 0:4 * ZT].rearrange("p (r t) -> p r t", r=4)
        LT = modes_mem[0:GRID, 0:NT]
        SEL = GT[0:EXPERTS, :, :]
        M8 = SPEC[0:TOK].rearrange("p a b c -> p (a b c)")[:, 0:NIMG * 8].rearrange("p (b e) -> p b e", b=NIMG)

        smx = sb("smx", [TOK, 4, HEADS])
        den = sb("den", [TOK, NIMG, HEADS])
        rden = sb("rden", [TOK, NIMG, HEADS])
        st = sb("st", [TOK, 4, NIMG])

        h_in, tail_w = sem("tokens_loaded"), sem("tail_weights_loaded")
        dve_step = sem("dve_step")
        var_ready, dev_ready, y_ready = sem("variance_ready"), sem("deviation_ready"), sem("layernorm_ready")
        yt_full, yt_ready = sem("yt_full"), sem("yt_ready")
        q_full, q_ready = sem("q_full"), sem("q_ready")
        k_full, k_ready = sem("k_full"), sem("k_ready")
        v_full, v_ready = sem("v_full"), sem("v_ready")
        km_ready, s_full, s_ready = sem("masked_keys_ready"), sem("scores_full"), sem("scores_ready")
        max_ready, sub_ready, exp_ready = sem("max_ready"), sem("shifted_ready"), sem("exp_ready")
        sum_ready = sem("sum_ready")
        pm_ready, pt_full, pt_ready = sem("windowed_ready"), sem("pt_full"), sem("pt_ready")
        o_full, o_ready = sem("o_full"), sem("o_ready")
        ot_full, ot_ready = sem("ot_full"), sem("ot_ready")
        pj_full, pj_ready = sem("projected_full"), sem("projected_ready")
        lg_full, lg_ready = sem("logits_full"), sem("logits_ready")
        le_ready, lx_ready, sc_ready = sem("shifted_logits_ready"), sem("exp_logits_ready"), sem("expert_scores_ready")
        st_full, st_ready = sem("st_full"), sem("st_ready")
        bc_full, zx_ready, zx_used = sem("broadcast_full"), sem("zx_ready"), sem("zx_used")
        lt_full, lt_ready = sem("lt_full"), sem("lt_ready")
        f_full, f_ready = sem("ffn_full"), sem("ffn_ready")
        out_ready, out_stored = sem("out_ready"), sem("out_stored")

        SPR = [PSALL[:, 2 * i:2 * i + 2, 0:4 * TOK] for i in range(2)]
        PTP = PSALL[:, 4:6, 0:4 * TOK]

        def tail_sync(sp):
            sp.dma_start(H[0:1], cls_rows).then_inc(h_in, 16)
            sp.dma_start(H[1:TOK], hid_scr.rearrange("p s g r b (h w) -> h (p s g r b) w", w=GRID)).then_inc(h_in, 16)
            sp.dma_start(SEL, sel_in).then_inc(tail_w, 16)
            sp.wait_ge(out_ready, 1)
            sp.dma_start(out.rearrange("b t d -> t b d"), TMP).then_inc(out_stored, 16)
            sp.wait_ge(out_stored, 16)

        def tail_tensor(pe):
            pe.wait_ge(tail_w, 16 * TAIL_LOADS)

            def transposes(c, ready, src, width, dst, full):
                for i in range(BC):
                    m = pe.transpose(dst[0:width, i * TOK:(i + 1) * TOK], src(c * BC + i), ident[0:TOK, 0:TOK])
                m.then_inc(full, 1)

            def qkv(c):
                pe.wait_ge(yt_ready, c + 1)
                x = YT[0:GRID, c * CT:(c + 1) * CT]
                if c:
                    pe.wait_ge(q_ready, c)
                pe.matmul(PS[2][0:GRID, 0:CT], WQKV[:, 0:GRID], x, start=True, stop=True).then_inc(q_full, 1)
                if c:
                    pe.wait_ge(k_ready, c)
                pe.matmul(PS[3][0:GRID, 0:CT], WQKV[:, GRID:2 * GRID], x, start=True, stop=True).then_inc(k_full, 1)
                if c:
                    pe.wait_ge(v_ready, c)
                for i in range(BC):
                    b = c * BC + i
                    m = pe.matmul(PS[4][0:TOK, i * GRID:(i + 1) * GRID], YT[0:GRID, b * TOK:(b + 1) * TOK],
                                  WQKV[:, 2 * GRID:3 * GRID], start=True, stop=True)
                m.then_inc(v_full, 1)

            pe.wait_ge(y_ready, 1)
            for c in range(NC + 1):
                if c < NC:
                    if c >= 2:
                        pe.wait_ge(yt_ready, c - 1)
                    transposes(c, None, lambda b: Y[:, b, 0, :], GRID, PS[c % 2], yt_full)
                if c:
                    qkv(c - 1)

            def scores(b):
                if b == 0:
                    pe.wait_ge(q_ready, NC)
                    pe.wait_ge(k_ready, NC)
                    pe.wait_ge(v_ready, NC)
                    pe.wait_ge(yt_ready, NC)
                if b % BC == 0:
                    pe.wait_ge(km_ready, HEADS * (b // BC + 1))
                if b >= 2:
                    pe.wait_ge(s_ready, b - 1)
                for hf in range(2):
                    m = pe.matmul(SPR[b % 2][0:TOK, hf, :], QT[:, b * TOK:(b + 1) * TOK],
                                  KM[:, b // BC % 2, 4 * hf:4 * hf + 4, b % BC * TOK:(b % BC + 1) * TOK],
                                  start=True, stop=True)
                m.then_inc(s_full, 1)

            def turn_probs(b):
                pe.wait_ge(pm_ready, b + 1)
                if b:
                    pe.wait_ge(pt_ready, b)
                for h in range(HEADS):
                    m = pe.transpose(PTP[0:TOK, h // 4, h % 4 * TOK:(h % 4 + 1) * TOK], PM[:, b % 3, h, :],
                                     ident[0:TOK, 0:TOK])
                m.then_inc(pt_full, 1)

            def values(b):
                pe.wait_ge(pt_ready, b + 1)
                if b % BC == 0 and b:
                    pe.wait_ge(o_ready, b // BC)
                for h in range(HEADS):
                    m = pe.matmul(PS[6][0:TOK, b % BC * GRID + h * HD:b % BC * GRID + (h + 1) * HD], PT[:, b % 2, h, :],
                                  V[:, b, h * HD:(h + 1) * HD], start=True, stop=True)
                m.then_inc(o_full, 1)

            def project(c):
                pe.wait_ge(o_ready, c + 1)
                if c:
                    pe.wait_ge(pj_ready, c)
                transposes(c, None, lambda b: O[:, b, :], GRID, PS[7], ot_full)
                pe.wait_ge(ot_ready, c + 1)
                for i in range(BC):
                    m = pe.matmul(PS[7][0:TOK, i * GRID:(i + 1) * GRID], OT[:, c % 2, i * TOK:(i + 1) * TOK], WP[:],
                                  start=True, stop=True)
                m.then_inc(pj_full, 1)

            for i in range(NIMG + LAG + 2):
                if i < NIMG:
                    scores(i)
                if LAG <= i < NIMG + LAG:
                    turn_probs(i - LAG)
                if i >= LAG + 1 and i - LAG - 1 < NIMG:
                    values(i - LAG - 1)
                if i > LAG + 1 and (i - LAG - 2) % BC == BC - 1:
                    project((i - LAG - 2) // BC)

            pe.wait_ge(y_ready, 2)
            for c in range(NC + 1):
                if c < NC:
                    if c >= 2:
                        pe.wait_ge(yt_ready, NC + c - 1)
                    transposes(c, None, lambda b: Y[:, b].rearrange("p t d -> p (t d)"), 128, PS[c % 2], yt_full)
                if c:
                    pe.wait_ge(yt_ready, NC + c)
                    if c >= 3:
                        pe.wait_ge(lg_ready, c - 2)
                    for i in range(BC):
                        b = (c - 1) * BC + i
                        m = pe.matmul(PS[2 + (c - 1) % 2][0:TOK, i * EXPERTS:(i + 1) * EXPERTS],
                                      YT[0:GRID, b * TOK:(b + 1) * TOK], GATE[:], start=True, stop=True)
                    m.then_inc(lg_full, 1)
            pe.wait_ge(sc_ready, 1)
            for c in range(NC):
                if c >= 2:
                    pe.wait_ge(st_ready, c - 1)
                transposes(c, None, lambda b: SC[:, b, :], EXPERTS, PS[c % 2], st_full)
            pe.wait_ge(st_ready, NC)
            pe.wait_ge(lg_ready, NC)
            PAIRS = EXPERTS // 2

            def expert_product(n):
                z, ep = n // PAIRS, n % PAIRS
                pe.wait_ge(zx_ready, n + 1)
                if ep == 0 and z >= 2:
                    pe.wait_ge(lt_ready, z - 1)
                m = pe.matmul(PS[4 + z % 2][0:GRID, 0:ZT], WE[:, ep, :], ZX[:, n % 4, :],
                              start=(ep == 0), stop=(ep == PAIRS - 1))
                m.then_inc(zx_used, 1)

            for n in range(NZ * PAIRS + 2):
                if n < NZ * PAIRS:
                    if n >= 4:
                        pe.wait_ge(zx_ready, n - 3)
                    z, ep = n // PAIRS, n % PAIRS
                    pe.matmul(PS[n % 4][:, 0:ZT], SEL[:, ep, :], ST[:, z * ZT:(z + 1) * ZT],
                              start=True, stop=True).then_inc(bc_full, 1)
                if n >= 2:
                    expert_product(n - 2)
            for c in range(NC):
                pe.wait_ge(lt_ready, -(-(c + 1) * CT // ZT))
                if c >= 2:
                    pe.wait_ge(f_ready, c - 1)
                for i in range(BC):
                    b = c * BC + i
                    m = pe.matmul(PS[6 + c % 2][0:TOK, i * GRID:(i + 1) * GRID], LT[:, b * TOK:(b + 1) * TOK], WO[:],
                                  start=True, stop=True)
                m.then_inc(f_full, 1)

        def tail_scalar(act):
            act.wait_ge(tail_w, 16 * TAIL_LOADS)

            def deviation(n):
                act.wait_ge(var_ready, n + 1)
                nc.scalar.activation(st[:, 2, :], st[:, 1, :], ACT.Sqrt).then_inc(dev_ready, 1)

            deviation(0)
            for c in range(NC):
                act.wait_ge(q_full, c + 1)
                nc.scalar.activation(QT[:, c * CT:(c + 1) * CT], PS[2][0:GRID, 0:CT], ACT.Identity, bias=BQK[:, 0:1]
                                     ).then_inc(q_ready, 1)
                act.wait_ge(k_full, c + 1)
                nc.scalar.activation(KT[:, c * CT:(c + 1) * CT], PS[3][0:GRID, 0:CT], ACT.Identity, bias=BQK[:, 1:2]
                                     ).then_inc(k_ready, 1)
            act.wait_ge(k_ready, NC)
            for i in range(NIMG + LAG + 1):
                if i % BC == 0 and i < NIMG:
                    c = i // BC
                    if c >= 2:
                        act.wait_ge(s_full, (c - 1) * BC)
                    for h in range(HEADS):
                        nc.scalar.activation(KM[:, c % 2, h, :], KT[:, c * CT:(c + 1) * CT], ACT.Copy,
                                             scale=HM[:, h:h + 1]).then_inc(km_ready, 1)
                if 1 <= i <= NIMG:
                    b = i - 1
                    act.wait_ge(sub_ready, b + 1)
                    nc.scalar.activation(PR[:, b % 4], PR[:, b % 4], ACT.Exp).then_inc(exp_ready, 1)
                if i >= LAG and i - LAG < NIMG:
                    b = i - LAG
                    act.wait_ge(pt_full, b + 1)
                    if b >= 2:
                        act.wait_ge(o_full, b - 1)
                    nc.scalar.copy(PT[:, b % 2].rearrange("p (a h) t -> p a (h t)", a=2), PTP[0:TOK]).then_inc(pt_ready, 1)
                if i > LAG + 1 and (i - LAG - 2) % BC == BC - 1:
                    turn_out(act, (i - LAG - 2) // BC)
            turn_out(act, NC - 1)
            deviation(1)
            act.wait_ge(le_ready, 1)
            nc.scalar.activation(SC, SC, ACT.Exp).then_inc(lx_ready, 1)
            for z in range(NZ):
                act.wait_ge(zx_used, (z + 1) * (EXPERTS // 2))
                nc.scalar.copy(LT[:, z * ZT:(z + 1) * ZT], PS[4 + z % 2][0:GRID, 0:ZT]).then_inc(lt_ready, 1)
            deviation(2)

        def turn_out(act, c):
            act.wait_ge(ot_full, c + 1)
            nc.scalar.copy(OT[:, c % 2, :], PS[7][0:GRID, 0:CT]).then_inc(ot_ready, 1)

        def tail_pool(pool):
            pool.wait_ge(tail_w, 16 * TAIL_LOADS)
            for i in range(NIMG + 2):
                if i < NIMG:
                    pool.wait_ge(max_ready, i + 1)
                    nc.gpsimd.tensor_tensor(PR[:, i % 4], PR[:, i % 4],
                                            smx[:, i % 4, :].unsqueeze(2).broadcast_to([TOK, HEADS, TOK]),
                                            ALU.subtract).then_inc(sub_ready, 1)
                if i >= 2:
                    b = i - 2
                    pool.wait_ge(exp_ready, b + 1)
                    if b >= 3:
                        pool.wait_ge(pt_full, b - 2)
                    nc.gpsimd.tensor_tensor(PM[:, b % 3], PR[:, b % 4],
                                            BAND[:].unsqueeze(1).broadcast_to([TOK, HEADS, TOK]), ALU.mult
                                            ).then_inc(pm_ready, 1)

        def tail_vector(dve):
            steps = [0]

            def link(ins):
                steps[0] += 1
                ins.then_inc(dve_step, 1)
                dve.wait_ge(dve_step, steps[0])

            def over(x, n=GRID):
                return x.unsqueeze(2).broadcast_to([TOK, NIMG, n])

            def rows(x, n=NIMG):
                return x.unsqueeze(1).broadcast_to([TOK, n, GRID])

            def normalise(src, n):
                link(nc.vector.reduce_sum(st[:, 0, :], src, AX.X))
                link(nc.vector.tensor_scalar(st[:, 0, :], st[:, 0, :], 1.0 / GRID, None, ALU.mult))
                link(nc.vector.tensor_tensor(TMP, src, over(st[:, 0, :]), ALU.subtract))
                link(nc.vector.tensor_tensor(Y[:, :, 1, :], TMP, TMP, ALU.mult))
                link(nc.vector.reduce_sum(st[:, 1, :], Y[:, :, 1, :], AX.X))
                nc.vector.tensor_scalar(st[:, 1, :], st[:, 1, :], 1.0 / GRID, EPS, ALU.mult, ALU.add).then_inc(var_ready, 1)
                dve.wait_ge(dev_ready, n + 1)
                link(nc.vector.reciprocal(st[:, 3, :], st[:, 2, :]))

            dve.wait_ge(tail_w, 16 * TAIL_LOADS)
            dve.wait_ge(h_in, 32)
            normalise(H, 0)
            nc.vector.tensor_tensor(Y[:, :, 0, :], TMP, over(st[:, 3, :]), ALU.mult).then_inc(y_ready, 1)
            link(nc.vector.tensor_tensor(H, H, rows(BP[:]), ALU.add))
            for c in range(NC + 1):
                if c < NC:
                    dve.wait_ge(yt_full, c + 1)
                    nc.vector.tensor_copy(YT[0:GRID, c * CT:(c + 1) * CT], PS[c % 2][0:GRID, 0:CT]).then_inc(yt_ready, 1)
                if c:
                    dve.wait_ge(v_full, c)
                    nc.vector.tensor_tensor(V[:, (c - 1) * BC:c * BC, :],
                                            PS[4][0:TOK, 0:BC * GRID].rearrange("p (b d) -> p b d", b=BC),
                                            rows(BV[:], BC), ALU.add).then_inc(v_ready, 1)

            def attended(c):
                a = slice(c * BC, (c + 1) * BC)
                dve.wait_ge(o_full, (c + 1) * BC)
                link(nc.vector.reciprocal(rden[:, a, :], den[:, a, :]))
                nc.vector.tensor_tensor(
                    O[:, a, :].rearrange("p b (h e) -> p (b h) e", h=HEADS),
                    PS[6][0:TOK, 0:BC * GRID].rearrange("p (n e) -> p n e", e=HD),
                    rden[:, a, :].rearrange("p b h -> p (b h)").unsqueeze(2).broadcast_to([TOK, BC * HEADS, HD]),
                    ALU.mult).then_inc(o_ready, 1)

            def residual(c):
                a = slice(c * BC, (c + 1) * BC)
                dve.wait_ge(pj_full, c + 1)
                nc.vector.tensor_tensor(H[:, a, :], PS[7][0:TOK, 0:BC * GRID].rearrange("p (b d) -> p b d", b=BC),
                                        H[:, a, :], ALU.add).then_inc(pj_ready, 1)

            for i in range(NIMG + LAG + 3):
                if i < NIMG:
                    dve.wait_ge(s_full, i + 1)
                    if i >= 4:
                        dve.wait_ge(pm_ready, i - 3)
                        dve.wait_ge(sum_ready, i - 3)
                    nc.vector.tensor_tensor(
                        PR[:, i % 4].rearrange("p (a h) t -> p a (h t)", a=2), SPR[i % 2][0:TOK],
                        BAND4[:].unsqueeze(1).broadcast_to([TOK, 2, 4 * TOK]), ALU.mult).then_inc(s_ready, 1)
                    dve.wait_ge(s_ready, i + 1)
                    nc.vector.reduce_max(smx[:, i % 4, :], PR[:, i % 4], AX.X).then_inc(max_ready, 1)
                if 2 <= i < NIMG + 2:
                    b = i - 2
                    dve.wait_ge(exp_ready, b + 1)
                    nc.vector.reduce_sum(den[:, b, :], PR[:, b % 4], AX.X).then_inc(sum_ready, 1)
                    dve.wait_ge(sum_ready, b + 1)
                if i >= LAG + 1 and (i - LAG - 1) % BC == BC - 1:
                    attended((i - LAG - 1) // BC)
                if i > LAG + 2 and (i - LAG - 2) % BC == BC - 1:
                    residual((i - LAG - 2) // BC)
            dve.wait_ge(pj_ready, NC)
            normalise(H, 1)
            link(nc.vector.tensor_tensor(Y[:, :, 0, :], TMP, over(st[:, 3, :]), ALU.mult))
            nc.vector.tensor_copy(Y[:, :, 1, :], Y[:, :, 0, :]).then_inc(y_ready, 1)
            link(nc.vector.memset(LG[:, :, EXPERTS:LW], SENTINEL))
            for c in range(NC + 1):
                if c < NC:
                    dve.wait_ge(yt_full, NC + c + 1)
                    nc.vector.tensor_copy(YT[:, c * CT:(c + 1) * CT], PS[c % 2][:, 0:CT]).then_inc(yt_ready, 1)
                if c:
                    a = slice((c - 1) * BC, c * BC)
                    dve.wait_ge(lg_full, c)
                    nc.vector.tensor_copy(LG[:, a, 0:EXPERTS],
                                          PS[2 + (c - 1) % 2][0:TOK, 0:BC * EXPERTS].rearrange("p (b e) -> p b e", b=BC)
                                          ).then_inc(lg_ready, 1)
            dve.wait_ge(lg_ready, NC)
            for b in range(NIMG):
                m = nc.vector.max(M8[:, b, :], LG[:, b, 0:EXPERTS])
            link(m)
            link(nc.vector.tensor_tensor(SC, LG[:, :, 0:EXPERTS],
                                         M8[:, :, 0:1].broadcast_to([TOK, NIMG, EXPERTS]), ALU.subtract))
            dve.sem_inc(le_ready, 1)
            link(nc.vector.memset(M8[:, :, TOPK:8], SENTINEL))
            for b in range(NIMG):
                m = nc.vector.match_replace(LR[:, b, :], M8[:, b, :], LG[:, b, :], -SENTINEL)
            link(m)
            link(nc.vector.tensor_tensor(TMP, LR[:, :, 0:EXPERTS], LG[:, :, 0:EXPERTS], ALU.not_equal))
            dve.wait_ge(lx_ready, 1)
            link(nc.vector.tensor_tensor(SC, SC, TMP, ALU.mult))
            link(nc.vector.reduce_sum(st[:, 0, :], SC, AX.X))
            link(nc.vector.reciprocal(st[:, 3, :], st[:, 0, :]))
            nc.vector.tensor_tensor(SC, SC, over(st[:, 3, :]), ALU.mult).then_inc(sc_ready, 1)
            for c in range(NC):
                dve.wait_ge(st_full, c + 1)
                nc.vector.tensor_copy(ST[:, c * CT:(c + 1) * CT], PS[c % 2][0:EXPERTS, 0:CT]).then_inc(st_ready, 1)
            for n in range(NZ * EXPERTS // 2):
                z = n // (EXPERTS // 2)
                dve.wait_ge(bc_full, n + 1)
                if n >= 4:
                    dve.wait_ge(zx_used, n - 3)
                nc.vector.tensor_tensor(ZX[:, n % 4, :], PS[n % 4][:, 0:ZT], YT[:, z * ZT:(z + 1) * ZT], ALU.mult
                                        ).then_inc(zx_ready, 1)
            F = SC
            link(nc.vector.tensor_tensor(F, Y[:, :, 0, :], rows(OB[:]), ALU.add))
            for c in range(NC):
                a = slice(c * BC, (c + 1) * BC)
                dve.wait_ge(f_full, c + 1)
                nc.vector.tensor_tensor(F[:, a, :], PS[6 + c % 2][0:TOK, 0:BC * GRID].rearrange("p (b d) -> p b d", b=BC),
                                        F[:, a, :], ALU.add).then_inc(f_ready, 1)
            dve.wait_ge(f_ready, NC)
            normalise(F, 2)
            link(nc.vector.tensor_tensor(TMP, TMP, over(st[:, 3, :]), ALU.mult))
            link(nc.vector.tensor_tensor(TMP, TMP, rows(LNG[:]), ALU.mult))
            link(nc.vector.tensor_tensor(TMP, TMP, rows(LNB[:]), ALU.add))
            nc.vector.tensor_tensor(TMP, TMP, H, ALU.add).then_inc(out_ready, 1)

        block = ctx.enter_context(nc.Block())


        @block.sync
        def _(sp):
            loads = [(DW, dft_w), (DH, dft_h), (EH, idft_h), (EW, idft_w), (ident, ident_in),
                     (CWALL, conv_wb), (W0, fc0_w), (B0, fc0_b), (W1, fc1_w), (B1, fc1_b), (W2, fc2_w), (B2, fc2_b)]
            for dst, src in loads:
                sp.dma_start(dst[:], src).then_inc(consts, 16)

            def load_piece(s, kxd, layer):
                sp_turn.wait(piece_used, s * KXD + kxd + 1 - 2)
                slot = (s * KXD + kxd) % 2
                for j in range(B4):
                    sp.dma_start(SW[j * CH:(j + 1) * CH, slot, j, :],
                                 spec_w[bass.ds(layer, 1), kxd, j].rearrange("l c n -> (l c) n")
                                 ).then_inc(piece_in[slot].sem, 16)

            sp.wait_ge(zeroed, 2)
            sp.sem_inc(stored.sem, stored.credit)
            sp_turn, sp_pass = Turns(sp, "layer", LAYER_COUNTS), Turns(sp, "pass", PASS_COUNTS)
            with sp.Fori(0, PASSES) as p:
                for n in range(N0):
                    s, g, q = n // (GROUPS * N_X), n // N_X % GROUPS, n % N_X
                    if n >= 2:
                        sp_pass.wait(x0_full, n - 1)
                    else:
                        sp.wait_ge(credits, 1)
                        sp_pass.wait(pass_done, 1)
                    sp.dma_start(COIN[:, n % 2, :],
                                 xin[bass.ds(p, 1), s, g, :, q * BANK:(q + 1) * BANK].rearrange("o r n -> (o r) n")
                                 ).then_inc(co_in[n % 2].sem, 16)
                with sp.Fori(0, LAYERS) as l:
                    for kxd in range(KXD):
                        load_piece(0, kxd, l)
                    for s in range(STREAMS):
                        sp_turn.wait(mix_ready, (s + 1) * N_MIX)
                        for q in range(B4):
                            sp.dma_start(
                                spec_scr[s].rearrange("(d q) r b n -> q (r b) d n", q=B4)[q],
                                MIXED[q * 32:q * 32 + SIMG * RI, :].rearrange("p (d n) -> p d n", d=KXD)
                            ).then_inc(stored.sem, 16)
                        if s == 0:
                            for kxd in range(KXD):
                                load_piece(1, kxd, l)
                        for g in range(GROUPS):
                            sp_turn.wait_both(stored, s + 1, g_full, (s * GROUPS + g + 1 - GROUPS) * N_G)
                            modes = spec_scr[s].rearrange("k r b (y o) -> (k r) y b o", y=MODES)
                            for b in range(B4):
                                sp.dma_start(MODE[0:KOUT, g].rearrange("p y (b o) -> p y b o", b=B4)[:, :, b], modes[:, :, g * B4 + b]
                                             ).then_inc(loaded[g].sem, 16)
                    sp_turn.next(LAYER_COUNTS)
                for s in range(STREAMS):
                    for g in range(GROUPS):
                        n = s * GROUPS + g
                        sp_pass.wait(fc2_ready, 4 * (n + 1))
                        for tile in range(4):
                            qp, pr = tile // 2, tile % 2
                            sp.dma_start(
                                hid_scr[bass.ds(p, 1), s, g, pr].rearrange("o b (d q n) -> q (o b) d n", d=4, q=2)[qp],
                                HO[32 * tile:32 * tile + 2]).then_inc(ho_out.sem, 16)
                sp_pass.next(PASS_COUNTS)
            sp.wait_ge(ho_out.sem, PASSES * STREAMS * GROUPS * 64)
            tail_sync(sp)

        @block.tensor
        def _(pe):
            pe.wait_ge(consts, 16 * 12)
            pe.wait_ge(zeroed, 2)
            pe.wait_ge(credits, 1)
            pe.sem_inc(t1_full.sem, t1_full.credit)
            pe.sem_inc(tr_full.sem, tr_full.credit)
            pe.sem_inc(sp_full.sem, sp_full.credit)
            pe.sem_inc(mix_full.sem, mix_full.credit)
            pe.sem_inc(piece_used.sem, piece_used.credit)
            pe.sem_inc(g_full.sem, g_full.credit)
            pe.sem_inc(gt_full.sem, gt_full.credit)
            pe.sem_inc(x_full.sem, x_full.credit)

            def transpose_x(s, g, j):
                n = (s * GROUPS + g) * N_XT + j
                pe_turn.wait(xt_ready, n + 1 - 2)
                if j == 0:
                    pe_turn.wait(tr_ready, (s * GROUPS + g) * N_TR)
                for i in range(4):
                    c = (4 * j + i) * 128
                    m = pe.transpose(xt_bank[j % 2][:, i * 128:(i + 1) * 128], X[:, s, g, c:c + 128], ident[:])
                m.then_inc(xt_full.sem, 1)

            def dft_columns(s, g, j):
                n = (s * GROUPS + g) * N_T1 + j
                pe_turn.wait(xt_ready, n + 1)
                if j < 2:
                    pe_turn.wait(sp_ready, (s * GROUPS + g) * N_F)
                else:
                    pe_turn.wait(t1_ready, n + 1 - 2)
                for i in range(4):
                    m = pe.matmul(t1_bank[j % 2][:, i * H2 * KOUT:(i + 1) * H2 * KOUT],
                                  XT[:, j % 2, i * 128:(i + 1) * 128], DW[:], start=True, stop=True)
                m.then_inc(t1_full.sem, 1)

            def front(s):
                for g in range(GROUPS):
                    sg = s * GROUPS + g
                    for j in range(N_XT + 1):
                        if j < N_XT:
                            transpose_x(s, g, j)
                        if j:
                            dft_columns(s, g, j - 1)
                    pe_turn.wait(t1_ready, (sg + 1) * N_T1)
                    pe_turn.wait(xt_ready, (sg + 1) * N_XT)
                    for j in range(N_TR):
                        if j >= 2:
                            pe_turn.wait(tr_ready, sg * N_TR + j - 1)
                        for i in range(4):
                            ky = 4 * j + i
                            m = pe.transpose(tr_bank[j % 2][:, i * 128:(i + 1) * 128],
                                             T1[:, RI * ky:RI * (ky + 1), :].rearrange("p r h -> p (r h)"), ident[:])
                        m.then_inc(tr_full.sem, 1)
                    pe_turn.wait(tr_ready, (sg + 1) * N_TR)
                    for j in range(N_F):
                        for ki, kyg in enumerate(range(3 * j, min(3 * j + 3, KYG))):
                            for b in range(B4):
                                m = pe.matmul(sp_bank[j][:, (ki * B4 + b) * KOUT:(ki * B4 + b + 1) * KOUT],
                                              TR[:, b, 4 * kyg:4 * kyg + 4, :].rearrange("p k c -> p (k c)"), DH[:], start=True, stop=True)
                        m.then_inc(sp_full.sem, 1)
                pe_turn.wait(sp_ready, (s + 1) * GROUPS * N_F)
                pe_turn.wait(gt_ready, 0)
                for blk in range(MIXB):
                    kxd, kyg, job = blk // KYG, blk % KYG, blk // 4
                    if kyg == 0:
                        n = s * KXD + kxd
                        pe_turn.wait(piece_in[n % 2], n // 2 + 1)
                    if blk % 4 == 0 and (job >= 2 or s):
                        pe_turn.wait(mix_ready, s * N_MIX + job - 1)
                    for q in range(B4):
                        c = (q * KYG + kyg) * CH
                        m = pe.matmul(mix_bank[(s * N_MIX + job) % 2][32 * q:32 * q + SIMG * RI, (blk % 4) * 128:(blk % 4 + 1) * 128],
                                      SPEC[:, kyg, 4 * kxd + q, :],
                                      SW[:, (s * KXD + kxd) % 2, :, c:c + CH],
                                      start=True, stop=True, tile_position=(0, 32 * q))
                    if kyg == KYG - 1:
                        m.then_inc(piece_used.sem, 1)
                    if blk % 4 == 3 or blk == MIXB - 1:
                        if kyg == KYG - 1:
                            m = pe.matmul(mix_bank[(s * N_MIX + job) % 2][96:96 + SIMG * RI, (blk % 4) * 128:(blk % 4 + 1) * 128],
                                          SPEC[:, kyg, 4 * kxd + 3, :],
                                          SW[:, (s * KXD + kxd) % 2, :, c:c + CH],
                                          start=True, stop=True, tile_position=(0, 96))
                        m.then_inc(mix_full.sem, 1)

            def back(s):
                for g in range(GROUPS):
                    sg = s * GROUPS + g
                    pe_turn.wait(loaded[g], s + 1)
                    pe_turn.wait(x_ready, sg * N_X)
                    for j in range(N_G):
                        if j >= 2:
                            pe_turn.wait(g_ready, sg * N_G + j - 1)
                        for i in range(4):
                            m = pe.matmul(g_bank[j % 2][:, i * 128:(i + 1) * 128],
                                          MODE[0:KOUT, g, 4 * j + i, :], EH[:], start=True, stop=True)
                        m.then_inc(g_full.sem, 1)
                    pe_turn.wait(g_ready, (sg + 1) * N_G)
                    if g == 0:
                        pe_turn.wait(mix_ready, STREAMS * N_MIX)
                    if s == 0 and g == 0:
                        pe_turn.wait(cw_set, 1)
                    for j in range(N_G2 + 1):
                        if j < N_G2:
                            pe_turn.wait(gt_ready, sg * N_G2 + j - 1)
                            for i in range(4):
                                hh = 4 * j + i
                                m = pe.transpose(gt_bank[j % 2][0:H2 * KOUT, i * 128:(i + 1) * 128],
                                                 G[:, H2 * RI * hh:H2 * RI * (hh + 1), :].rearrange("p a b -> p (a b)"), ident[:])
                            m.then_inc(gt_full.sem, 1)
                        if j:
                            q = j - 1
                            pe_turn.wait(gt_ready, sg * N_G2 + q + 1)
                            pe_turn.wait(x_ready, sg * N_X + q - 1)
                            pe.matmul(x_bank[q % 2][:, :], CW[:, 0:128], X[:, s, g, q * BANK:(q + 1) * BANK],
                                      start=True, stop=True, skip_group_check=True)
                            for i in range(4):
                                m = pe.matmul(x_bank[q % 2][:, i * 128:(i + 1) * 128], GT[:, 4 * q + i, :], EW[:],
                                              start=False, stop=True, skip_group_check=True)
                            m.then_inc(x_full.sem, 1)

            pe_turn, pe_pass = Turns(pe, "layer", LAYER_COUNTS), Turns(pe, "pass", PASS_COUNTS)
            with pe.Fori(0, PASSES) as p:
                for n in range(N0):
                    pe_pass.wait(co_in[n % 2], n // 2 + 1)
                    if n >= 2:
                        pe_pass.wait(x0_ready, n - 1)
                    pe.matmul(xt_bank[n % 2][:, :], W0[:], COIN[:, n % 2, :], start=True, stop=True).then_inc(x0_full.sem, 1)
                with pe.Fori(0, LAYERS) as l:
                    pe_pass.wait(x0_ready, N0)
                    pe_turn.wait(x_ready, 0)
                    for s in range(STREAMS):
                        front(s)
                    for s in range(STREAMS):
                        back(s)
                    pe_turn.next(LAYER_COUNTS)
                pe_turn.wait(x_ready, 0)
                pe_turn.wait(gt_ready, 0)
                for n in range(N0 + 1):
                    if n < N0:
                        s, g, q = n // (GROUPS * N_X), n // N_X % GROUPS, n % N_X
                        for pr in range(2):
                            k = 2 * n + pr
                            if k >= 4:
                                pe_pass.wait(fc1_ready, k - 3)
                            pe.matmul(PS[4 + k % 4][:, :], W1[:, pr, :], X[:, s, g, q * BANK:(q + 1) * BANK],
                                      start=True, stop=True).then_inc(fc1_full.sem, 1)
                    if n:
                        m0 = n - 1
                        if m0 % 2 == 0 and m0 >= 4:
                            pe_pass.wait(fc2_ready, m0 // 2 - 1)
                        for pr in range(2):
                            k = 2 * m0 + pr
                            tile = 2 * (m0 % 2) + pr
                            pe_pass.wait(fc1_ready, k + 1)
                            pe.matmul(PS[m0 // 2 % 2][32 * tile:32 * tile + 32, :], W2[:], FH[k % 4],
                                      start=True, stop=True, tile_position=(0, 32 * tile)).then_inc(fc2_full.sem, 1)
                pe_pass.wait(fc2_ready, N0 // 2)
                pe_pass.next(PASS_COUNTS)
            tail_tensor(pe)

        @block.scalar
        def _(act):
            for dst, src in [(WQKV, w_qkv), (BQK, b_qk), (BV, b_v), (WP, w_proj), (BP, b_proj), (GATE, gate_w),
                             (WE, w_expert), (WO, out_w), (OB, out_b), (LNG, ln_g), (LNB, ln_b), (HM, head_mask),
                             (BAND, band), (BAND4, band4)]:
                act.dma_start(dst[:], src).then_inc(tail_w, 16)
            act.wait_ge(consts, 16 * 12)
            act.sem_inc(sp_ready.sem, sp_ready.credit)
            act.sem_inc(gt_ready.sem, gt_ready.credit)
            act.sem_inc(x_ready.sem, x_ready.credit)
            act_turn, act_pass = Turns(act, "layer", LAYER_COUNTS), Turns(act, "pass", PASS_COUNTS)
            with act.Fori(0, PASSES) as p:
                with act.Fori(0, LAYERS) as l:
                    for s in range(STREAMS):
                        for g in range(GROUPS):
                            for j in range(N_F):
                                act_turn.wait(sp_full, (s * GROUPS + g) * N_F + j + 1)
                                if g == 0 and j == 0:
                                    act_turn.wait(mix_full, s * N_MIX)
                                ks = min(3, KYG - 3 * j)
                                nc.scalar.copy(
                                    SPEC[:, 3 * j:3 * j + ks].rearrange("p k x (r b) -> p k (x r) b", r=RI)[:, :, :, g * B4:(g + 1) * B4],
                                    sp_bank[j][:, 0:ks * B4 * KOUT].rearrange("p (k b n) -> p k n b", k=ks, b=B4)
                                ).then_inc(sp_ready.sem, 1)
                        for j in range(N_MIX):
                            act_turn.wait(mix_full, s * N_MIX + j + 1)
                            if j == 0:
                                act_turn.wait(stored, s)
                            w = min(BANK, MIXB * 128 - j * BANK)
                            nc.scalar.copy(MIXED[:, j * BANK:j * BANK + w], mix_bank[(s * N_MIX + j) % 2][:, 0:w]
                                           ).then_inc(mix_ready.sem, 1)
                    for s in range(STREAMS):
                        for g in range(GROUPS):
                            sg = s * GROUPS + g
                            for j in range(N_G2 + 1):
                                if j < N_G2:
                                    act_turn.wait(gt_full, sg * N_G2 + j + 1)
                                    act_turn.wait(x_full, (sg - 1) * N_X + j + 1 if sg else 0)
                                    nc.scalar.copy(GT[:, 4 * j:4 * j + 4, :].rearrange("p h n -> p (h n)"),
                                                   gt_bank[j % 2][0:H2 * KOUT, :]).then_inc(gt_ready.sem, 1)
                                if j:
                                    q = j - 1
                                    act_turn.wait(x_full, sg * N_X + q + 1)
                                    nc.scalar.activation(X[:, s, g, q * BANK:(q + 1) * BANK], x_bank[q % 2][:, :],
                                                         ACT.Gelu, bias=CW[:, 128:129]).then_inc(x_ready.sem, 1)
                    act_turn.next(LAYER_COUNTS)
                act_turn.wait(stored, 0)
                for k in range(NF):
                    act_pass.wait(fc1_full, k + 1)
                    if k >= 4:
                        act_pass.wait(fc2_full, k - 3)
                    nc.scalar.activation(FH[k % 4], PS[4 + k % 4][:, :], ACT.Gelu, bias=B1[:, 0:1]).then_inc(fc1_ready.sem, 1)
                act_pass.next(PASS_COUNTS)
            tail_scalar(act)

        @block.vector
        def _(dve):
            for i in range(8):
                z = nc.vector.memset(PS[i][:, :], 0.0)
            z.then_inc(zeroed, 1)
            nc.vector.memset(SW[:], 0.0).then_inc(zeroed, 1)
            dve.sem_inc(credits, 1)
            dve.sem_inc(pass_done.sem, 1)
            dve.sem_inc(xt_ready.sem, xt_ready.credit)
            dve.sem_inc(tr_ready.sem, tr_ready.credit)
            dve.wait_ge(consts, 16 * 12)
            dve_turn, dve_pass = Turns(dve, "layer", LAYER_COUNTS), Turns(dve, "pass", PASS_COUNTS)
            with dve.Fori(0, PASSES) as p:
                for n in range(N0):
                    s, g, q = n // (GROUPS * N_X), n // N_X % GROUPS, n % N_X
                    dve_pass.wait(x0_full, n + 1)
                    nc.vector.tensor_scalar(X[:, s, g, q * BANK:(q + 1) * BANK], xt_bank[n % 2][:, :],
                                            B0[:, 0:1], None, ALU.add).then_inc(x0_ready.sem, 1)
                with dve.Fori(0, LAYERS) as l:
                    for s in range(STREAMS):
                        for g in range(GROUPS):
                            sg = s * GROUPS + g
                            for j in range(N_XT + 1):
                                if j < N_XT:
                                    n = sg * N_XT + j
                                    dve_turn.wait(xt_full, n + 1)
                                    dve_turn.wait(t1_full, n + 1 - 2)
                                    nc.vector.tensor_copy(XT[:, j % 2, :], xt_bank[j % 2][:, :]).then_inc(xt_ready.sem, 1)
                                if j:
                                    jj = j - 1
                                    dve_turn.wait(t1_full, sg * N_T1 + jj + 1)
                                    if jj == 0:
                                        dve_turn.wait(tr_full, sg * N_TR)
                                    nc.vector.tensor_copy(
                                        T1[:, :, 8 * jj:8 * jj + 8],
                                        t1_bank[jj % 2][:, 0:8 * KOUT].rearrange("p (h k) -> p k h", k=KOUT)
                                    ).then_inc(t1_ready.sem, 1)
                            for j in range(N_TR):
                                dve_turn.wait(tr_full, sg * N_TR + j + 1)
                                if j == 0:
                                    dve_turn.wait(sp_full, sg * N_F)
                                nc.vector.tensor_copy(TR[:, :, 4 * j:4 * j + 4, :].rearrange("p b k c -> p k b c"),
                                                      tr_bank[j % 2][:, :].rearrange("p (k b c) -> p k b c", k=4, b=B4)).then_inc(tr_ready.sem, 1)
                    dve_turn.wait(x_ready, 0)
                    nc.vector.tensor_copy(CW[:], CWALL[:, bass.ds(l, 1), :].rearrange("p o n -> p (o n)")).then_inc(cw_set.sem, 1)
                    for s in range(STREAMS):
                        for g in range(GROUPS):
                            sg = s * GROUPS + g
                            for j in range(N_G):
                                dve_turn.wait(g_full, sg * N_G + j + 1)
                                if j == 0:
                                    dve_turn.wait(gt_full, sg * N_G2)
                                nc.vector.tensor_copy(
                                    G[:, :, 4 * j:4 * j + 4],
                                    g_bank[j % 2][:, :].rearrange("p (k r) -> p r k", k=4)
                                ).then_inc(g_ready.sem, 1)
                    dve_turn.next(LAYER_COUNTS)
                dve_turn.wait(gt_full, 0)
                for m in range(N0 // 2):
                    if m % 4 == 0:
                        n = m // 4
                        if n:
                            dve_pass.wait(ho_out, n)
                    dve_pass.wait(fc2_full, 4 * (m + 1))
                    nc.vector.tensor_scalar(HO[:, m % 4, :], PS[m % 2][:, :], B2[:, 0:1], None, ALU.add
                                            ).then_inc(fc2_ready.sem, 1)
                dve_pass.wait(ho_out, STREAMS * GROUPS)
                dve.sem_inc(pass_done.sem, 1)
                dve_pass.next(PASS_COUNTS)
            tail_vector(dve)

        @block.gpsimd
        def _(pool):
            tail_pool(pool)


def constants():
    import numpy as np
    w = np.arange(GRID)
    k = np.arange(MODES)
    th = 2 * np.pi * np.outer(w, k) / GRID
    cos, sin = np.cos(th) / 8, np.sin(th) / 8
    fw = np.stack([cos, -sin], 2).reshape(GRID, KOUT)
    dft_w = np.zeros((H2, GRID, H2, KOUT))
    for i in range(H2):
        dft_w[i, :, i] = fw
    dft_h = np.zeros((RI, GRID, MODES, RI))
    dft_h[0, :, :, 0], dft_h[1, :, :, 0] = cos, sin
    dft_h[0, :, :, 1], dft_h[1, :, :, 1] = -sin, cos
    idft_h = np.zeros((MODES, RI, GRID, RI))
    idft_h[:, 0, :, 0], idft_h[:, 1, :, 0] = cos.T, -sin.T
    idft_h[:, 0, :, 1], idft_h[:, 1, :, 1] = sin.T, cos.T
    twice = np.where(k == 0, 1.0, 2.0)[:, None]
    bw = np.stack([twice * cos.T, -twice * sin.T], 0).reshape(KOUT, GRID)
    idft_w = np.zeros((H2, KOUT, H2, GRID))
    for i in range(H2):
        idft_w[i, :, i] = bw
    f = np.float32
    band = (np.abs(np.subtract.outer(np.arange(TOK), np.arange(TOK))) <= RADIUS).astype(f)
    return {
        "dft_w": dft_w.reshape(128, H2 * KOUT).astype(f), "dft_h": dft_h.reshape(128, KOUT).astype(f),
        "idft_h": idft_h.reshape(KOUT, GRID * RI).astype(f),
        "head_mask": np.kron(np.eye(HEADS, dtype=f), np.ones((HD, 1), f)),
        "band": band, "band4": np.tile(band * f(HD ** -0.5), (1, 4)),
        "sel": np.repeat(np.eye(EXPERTS, dtype=f), GRID, 1).reshape(EXPERTS, EXPERTS // 2, 128),
        "idft_w": idft_w.reshape(H2 * KOUT, H2 * GRID).astype(f), "ident": np.eye(128, dtype=f),
    }


def block_diagonal(w, n):
    import numpy as np
    k, m = w.shape
    out = np.zeros((n * k, n * m), w.dtype)
    for i in range(n):
        out[i * k:(i + 1) * k, i * m:(i + 1) * m] = w
    return out


def layout(inputs):
    import numpy as np
    a = {k: np.asarray(v) for k, v in inputs.items()}
    tok = {k[len("L0_tok_"):]: v for k, v in a.items() if k.startswith("L0_tok_")}
    d = constants()
    x = a["x"].reshape(PASSES, STREAMS, GROUPS, B4, PIX, 3).transpose(0, 1, 2, 3, 5, 4)
    d["x"] = x.reshape(PASSES, STREAMS, GROUPS, B4 * 3, PIX)
    d["fc0_w"] = block_diagonal(tok["fc0_w"], B4)
    d["fc0_b"] = np.tile(tok["fc0_b"], B4)[:, None]
    sw = np.stack([tok[f"sw{i}"] for i in range(LAYERS)])
    sw = sw.reshape(LAYERS, CH, CH, KXD, B4, KYG, B4)
    d["spec_w"] = sw.transpose(0, 3, 6, 1, 4, 5, 2).reshape(LAYERS, KXD, B4, CH, B4 * KYG * CH)
    d["conv_wb"] = np.stack([np.concatenate([block_diagonal(tok[f"cw{i}"].T, B4), np.tile(tok[f"cb{i}"], B4)[:, None]], 1)
                             for i in range(LAYERS)], 1)
    w1 = np.zeros((2, 2, CH, 2, 2, FC), np.float32)
    for pr in range(2):
        for b in range(2):
            w1[pr, b, :, pr, b] = tok["fc1_w"]
    d["fc1_w"] = w1.reshape(128, 2, 128)
    d["fc1_b"] = np.tile(tok["fc1_b"], 2)[:, None]
    w2 = np.zeros((128, CH), np.float32)
    w2[0:FC, 0], w2[FC:128, 1] = tok["fc2_w"][:, 0], tok["fc2_w"][:, 0]
    d["fc2_w"] = w2
    d["fc2_b"] = np.repeat(tok["fc2_b"], 128)[:, None]
    att = {k[len("L0_attn_"):]: v for k, v in a.items() if k.startswith("L0_attn_")}
    ffn = {k[len("L0_ffn_"):]: v for k, v in a.items() if k.startswith("L0_ffn_")}
    d["w_qkv"], d["w_proj"] = att["w_qkv"], att["w_proj"]
    d["b_qk"] = att["b_qkv"][0:2 * GRID].reshape(2, GRID).T
    every = lambda v: np.tile(v, (TOK, 1))
    d["b_v"], d["b_proj"] = every(att["b_qkv"][2 * GRID:]), every(att["b_proj"])
    d["gate_w"], d["out_w"] = ffn["gate_w"].T, ffn["out_w"].T
    d["w_expert"] = ffn["lattice_weights"].reshape(EXPERTS // 2, 128, GRID).transpose(1, 0, 2)
    d["out_b"], d["ln_g"], d["ln_b"] = every(ffn["out_b"]), every(ffn["ln_g"]), every(ffn["ln_b"])
    d["cls_rows"] = np.tile(a["cls_tok"].reshape(1, 1, GRID), (1, NIMG, 1))
    return {k: np.ascontiguousarray(v) for k, v in d.items()}


INS = ["x", "fc0_w", "fc0_b", "spec_w", "conv_wb", "fc1_w", "fc1_b", "fc2_w", "fc2_b",
       "w_qkv", "b_qk", "b_v", "w_proj", "b_proj", "gate_w", "w_expert", "out_w", "out_b", "ln_g", "ln_b", "cls_rows",
       "head_mask", "band", "band4", "sel", "dft_w", "dft_h", "idft_h", "idft_w", "ident"]


def program(nc, arrays):
    args = [nc.dram_tensor(f"in_{n}", arrays[n].shape, F32, kind="ExternalInput").ap() for n in INS]
    args.append(nc.dram_tensor("spec_scr", (STREAMS, MODES, RI, SIMG, MODES * CH), F32).ap())
    args.append(nc.dram_tensor("hid_scr", (PASSES, STREAMS, GROUPS, 2, 2, PIX), F32).ap())
    args.append(nc.dram_tensor("out", (NIMG, TOK, GRID), F32, kind="ExternalOutput").ap())
    vit_kernel(nc, *args)


def kernel(**inputs):
    import concourse.bacc as bacc
    from concourse.bass_utils import run_bass_kernel_spmd
    nc = bacc.Bacc("TRN2", target_bir_lowering=False, num_devices=1)
    arrays = layout(inputs)
    program(nc, arrays)
    r = run_bass_kernel_spmd(nc, [{f"in_{n}": arrays[n] for n in INS}], core_ids=[0])
    return r.results[0]["out"]
```

```python
from contextlib import ExitStack

import concourse.bass as bass
from concourse import mybir

NIMG, GRID, CH, MODES, LAYERS = 32, 64, 32, 20, 4
FC = 64
RI = 2
B4 = 4
NG = 4
GIMG = B4 * NG
PASSES = NIMG // GIMG
H2 = 2
HH = GRID // H2
PIX = GRID * GRID
BANK = 512
KYG = MODES // B4
KXD = MODES // B4
MIXB = KXD * KYG
KOUT = RI * MODES

N_XT = PIX // BANK
N_TR = MODES // B4
SPK = 3
N_F = -(-KYG // SPK)
N_MIX = (MIXB + 3) // 4
N_G = MODES // B4
N_X = PIX // BANK

AHEAD = 4
SLOTS = 3
FB = 4

TOK = GRID + 1
HEADS, HD = 8, 8
EXPERTS, TOPK = 64, 6
RADIUS = 32
EPS = 1e-5
NT = NIMG * TOK
BC = 4
NC = NIMG // BC
CT = BC * TOK
NZ = 5
ZT = NT // NZ
LW = EXPERTS + 2
SENTINEL = -3.0e38
LAG = 3
TAIL_LOADS = 13
CONST_LOADS = 11

F32 = mybir.dt.float32
ALU = mybir.AluOpType
ACT = mybir.ActivationFunctionType
AX = mybir.AxisListType


class Count:

    def __init__(self, sem, per_turn, unit=1, credit=0):
        self.sem, self.stride, self.unit, self.credit = sem, per_turn * unit, unit, credit


class Halves:

    def __init__(self, v, a, per_turn, credit=0):
        self.counts = [Count(v, per_turn // 2, credit=credit), Count(a, per_turn // 2, credit=credit)]

    def sem(self, n):
        return self.counts[n % 2].sem


class Turns:

    def __init__(self, eng, name, counts):
        self.eng, self.strides = eng, sorted({c.stride for c in counts})
        self.base = {n: eng.alloc_register(f"{name}_{n}") for n in self.strides}
        self.value = eng.alloc_register(f"{name}_value")
        self.second = eng.alloc_register(f"{name}_second")
        for r in self.base.values():
            eng.reg_mov(r, 0)

    def wait(self, count, done):
        self.eng.reg_add(self.value, self.base[count.stride], done * count.unit + count.credit)
        self.eng.wait_ge(count.sem, self.value)

    def wait_both(self, count, done, other, other_done):
        self.eng.reg_add(self.value, self.base[count.stride], done * count.unit + count.credit)
        self.eng.reg_add(self.second, self.base[other.stride], other_done * other.unit + other.credit)
        self.eng.wait_ge(count.sem, self.value)
        self.eng.wait_ge(other.sem, self.second)

    def wait_job(self, halves, n):
        self.wait(halves.counts[n % 2], n // 2 + 1)

    def wait_jobs(self, halves, n):
        self.wait_both(halves.counts[0], (n + 1) // 2, halves.counts[1], n // 2)

    def next(self):
        for n in self.strides:
            self.eng.reg_add(self.base[n], self.base[n], n)


def forward_steps(lead):
    steps = []
    for k in range(NG * N_XT + lead + N_TR + 3):
        if k < NG * N_XT:
            steps.append(("transpose", k))
        if 1 <= k <= NG * N_XT:
            steps.append(("columns", k - 1))
        for stage, delay in (("turn", 1), ("rows", 3)):
            n, j = divmod(k - lead - delay, N_XT)
            if 0 <= n < NG and j < N_TR:
                steps.append((stage, (n, j)))
    return steps


def inverse_steps():
    steps = [("pointwise", u) for u in range(AHEAD)] + [("modes", (0, j)) for j in range(N_G)]
    for u in range(NG * N_X + 1):
        if u < NG * N_X:
            steps.append(("turn_back", u))
        if u:
            steps.append(("inverse", u - 1))
        n, j = divmod(u - 1, N_X)
        if n + 1 < NG and 0 <= j < N_G:
            steps.append(("modes", (n + 1, j)))
        if AHEAD <= u + 2 < NG * N_X:
            steps.append(("pointwise", u + 2))
    return steps


FIRST_FORWARD, FORWARD, INVERSE = forward_steps(0), forward_steps(N_XT), inverse_steps()


def vit_kernel(nc, xall, fc0_all, spec_w, conv_wb, fc1_w, fc1_b, fc2_w, fc2_b,
               w_qkv, b_qk, b_v, w_proj, b_proj, gate_w, w_expert, out_w, out_b, ln_g, ln_b, cls_rows,
               head_mask, band, band4, sel_in, dft_w, dft_h, idft_h, idft_w, ident_in,
               spec_scr, hid_scr, out):
    ctx = ExitStack()
    with ctx:
        def sb(name, shape, dt=F32):
            return ctx.enter_context(nc.sbuf_tensor(name, shape, dt))

        def sem(name):
            return ctx.enter_context(nc.semaphore(name))

        X = sb("X", [128, NG, PIX])
        XT = sb("XT", [128, 2, BANK])
        T1 = sb("T1", [128, 2, KOUT, GRID])
        T1C = sb("T1C", [128, KOUT, GRID])
        TR = sb("TR", [128, 2, B4, MODES, CH])
        SPEC = sb("SPEC", [128, KYG, MODES, RI * GIMG])
        SW = sb("SW", [128, SLOTS, B4, B4 * KYG * CH])
        MIXED = sb("MIXED", [128, MIXB * 128])
        spec_mem = SPEC[:].rearrange("p a b c -> p (a b c)")
        MODE = spec_mem[:, 0:MODES * B4 * CH].rearrange("p (y n) -> p y n", y=MODES)
        G = T1[:].rearrange("p s a b -> p s (a b)").rearrange("p s (h k) -> p s h k", k=MODES)
        GT = TR[:, 0].rearrange("p a b c -> p (a b c)")[0:H2 * KOUT, 0:4 * 4 * 128].rearrange("p (s h n) -> p s h n", s=4, h=4)
        DW = sb("DW", [128, H2 * KOUT])
        DH = sb("DH", [128, KOUT])
        EH = sb("EH", [128, GRID * RI])
        EW = sb("EW", [H2 * KOUT, H2 * GRID])
        ident = sb("ident", [128, 128])
        CWALL = sb("CWALL", [128, LAYERS, 129])
        CW = sb("CW", [128, 129])
        W0 = sb("W0", [128, NG, 128])
        W1 = sb("W1", [128, 2, 128])
        B1 = sb("B1", [128, 1])
        W2 = sb("W2", [128, CH])
        B2 = sb("B2", [128, 1])
        WQKV, WP = sb("WQKV", [GRID, 3 * GRID]), sb("WP", [GRID, GRID])
        BQK, BV, BP = sb("BQK", [GRID, 2]), sb("BV", [TOK, GRID]), sb("BP", [TOK, GRID])
        GATE, WO, OB = sb("GATE", [GRID, EXPERTS]), sb("WO", [GRID, GRID]), sb("OB", [TOK, GRID])
        LNG, LNB = sb("LNG", [TOK, GRID]), sb("LNB", [TOK, GRID])
        HM = sb("HM", [GRID, HEADS])
        BAND = sb("BAND", [TOK, TOK])
        BAND4 = sb("BAND4", [TOK, 4 * TOK])
        COIN = T1[:, 0].rearrange("p a b -> p (a b)")[:, 0:2 * BANK].rearrange("p (r n) -> p r n", r=2)
        FH = TR[:].rearrange("p r a b c -> p (r a b c)")[:, 0:2 * FB * BANK].rearrange("p (r n) -> p r n", n=BANK)
        HO = T1[:, 0].rearrange("p a b -> p (a b)")[:, 0:4 * BANK].rearrange("p (a b) -> p a b", a=4)

        PSALL = ctx.enter_context(nc.psum_tensor("PSALL", [128, 8, BANK], F32))
        PS = [PSALL[:, i, :] for i in range(8)]

        xt_bank, t1_bank, tr_bank, sp_bank = PS[0:2], PS[2:4], PS[4:6], PS[6:8]
        mix_bank, g_bank, gt_bank, x_bank = PS[2:4], PS[6:8], PS[4:6], PS[0:4]

        consts = sem("consts_loaded")
        zeroed = sem("psum_and_ring_zeroed")
        credits = sem("credits_given")
        NP = NG * N_X
        NF = 2 * NP
        xt_full = Count(sem("xt_full"), NP, credit=N_XT)
        xt_ready = Halves(sem("xt_ready_v"), sem("xt_ready_a"), NP, credit=1 + N_XT // 2)
        t1_full, t1_ready = Count(sem("t1_full"), NP, credit=2 + N_XT), Count(sem("t1_ready"), NP, credit=N_XT)
        tr_full, tr_ready = Count(sem("tr_full"), NG * N_TR, credit=2 * N_TR), Halves(sem("tr_ready_v"), sem("tr_ready_a"), NG * N_TR, credit=1)
        sp_full, sp_ready = Count(sem("sp_full"), NG * N_F, credit=2 * N_F), Count(sem("sp_ready"), NG * N_F)
        mix_full, mix_ready = Count(sem("mix_full"), N_MIX), Count(sem("mix_ready"), N_MIX)
        piece_used = Count(sem("weights_piece_used"), KXD, credit=SLOTS)
        g_full, g_ready = Count(sem("g_full"), NG * N_G), Count(sem("g_ready"), NG * N_G, credit=2)
        gt_full, gt_ready = Count(sem("gt_full"), NP, credit=1), Count(sem("gt_ready"), NP, credit=2)
        x_full, x_ready = Count(sem("x_full"), NP, credit=4), Count(sem("x_ready"), NP, credit=4)
        piece_in = [Count(sem(f"weights_piece_loaded{i}"), len(range(i, KXD, SLOTS)), unit=64) for i in range(SLOTS)]
        stored = Count(sem("spectrum_stored"), KXD, unit=16, credit=1)
        loaded = [Count(sem(f"modes_loaded{g}"), NG // 2, unit=64) for g in range(2)]
        cw_set = Count(sem("layer_weights_set"), 1)
        x0_full = Count(sem("x0_full"), NP)
        x0_ready = Halves(sem("x0_ready_v"), sem("x0_ready_a"), NP)
        fc1_full, fc1_ready = Count(sem("fc1_full"), NF), Count(sem("fc1_ready"), NF)
        fc2_full, fc2_ready = Count(sem("fc2_full"), NP // 2), Count(sem("fc2_ready"), NP // 2)
        ho_out = Count(sem("hidden_stored"), NG, unit=64)
        co_in = [Count(sem(f"coords_loaded{i}"), N_X // 2, unit=16) for i in range(2)]
        w0_in = Count(sem("fc0_loaded"), 1, unit=16)
        pass_done = Count(sem("pass_done"), 1)
        c4_in = sem("input_loaded")
        COLUMN_COUNTS = [xt_full, t1_full, t1_ready] + xt_ready.counts
        LAYER_COUNTS = [tr_full, sp_full, sp_ready, mix_full, mix_ready, piece_used, g_full, g_ready, gt_full, gt_ready,
                        x_full, x_ready, stored, cw_set] + tr_ready.counts + loaded + piece_in
        PASS_COUNTS = [x0_full, fc1_full, fc1_ready, fc2_full, fc2_ready, ho_out, pass_done, w0_in] + x0_ready.counts + co_in

        arena = X[:].rearrange("p g n -> p (g n)")
        H = arena[0:TOK, 0:2048].rearrange("p (b d) -> p b d", b=NIMG)
        Y = arena[0:TOK, 2048:6144].rearrange("p (b t d) -> p b t d", b=NIMG, t=2)
        TMP = arena[0:TOK, 6144:8192].rearrange("p (b d) -> p b d", b=NIMG)
        YT = arena[:, 8192:8192 + NT]
        QT = arena[0:GRID, 10272:10272 + NT]
        KT = arena[0:GRID, 12352:12352 + NT]
        V = T1[0:TOK, 0].rearrange("p a b -> p (a b)")[:, 0:2048].rearrange("p (b d) -> p b d", b=NIMG)
        O = T1[0:TOK, 1].rearrange("p a b -> p (a b)")[:, 0:2048].rearrange("p (b d) -> p b d", b=NIMG)
        modes_mem = TR[:].rearrange("p r a b c -> p (r a b c)")
        KM = modes_mem[0:GRID, 0:2 * HEADS * CT].rearrange("p (r h t) -> p r h t", r=2, h=HEADS)
        sw_mem = SW[:].rearrange("p a b c -> p (a b c)")
        HT = HEADS * TOK
        PR = sw_mem[0:TOK, 0:4 * HT].rearrange("p (r h t) -> p r h t", r=4, h=HEADS)
        PM = sw_mem[0:TOK, 4 * HT:7 * HT].rearrange("p (r h t) -> p r h t", r=3, h=HEADS)
        PT = sw_mem[0:TOK, 7 * HT:9 * HT].rearrange("p (r h t) -> p r h t", r=2, h=HEADS)
        OT = MIXED[0:GRID, 0:2 * CT].rearrange("p (r t) -> p r t", r=2)
        LG = arena[0:TOK, 12352:12352 + NIMG * LW].rearrange("p (b e) -> p b e", b=NIMG)
        LR = MIXED[0:TOK, 0:NIMG * LW].rearrange("p (b e) -> p b e", b=NIMG)
        SC = T1[0:TOK, 0].rearrange("p a b -> p (a b)")[:, 0:2048].rearrange("p (b e) -> p b e", b=NIMG)
        ST = arena[0:EXPERTS, 10272:10272 + NT]
        ZX = T1[:, 1].rearrange("p a b -> p (a b)")[:, 0:4 * ZT].rearrange("p (r t) -> p r t", r=4)
        LT = modes_mem[0:GRID, 0:NT]
        WE = spec_mem[:, 0:EXPERTS // 2 * GRID].rearrange("p (e d) -> p e d", d=GRID)
        SEL = sw_mem[0:EXPERTS, 0:EXPERTS // 2 * 128].rearrange("p (e n) -> p e n", n=128)
        M8 = spec_mem[0:TOK, MODES * B4 * CH:MODES * B4 * CH + NIMG * 8].rearrange("p (b e) -> p b e", b=NIMG)

        smx = sb("smx", [TOK, 4, HEADS])
        den = sb("den", [TOK, NIMG, HEADS])
        rden = sb("rden", [TOK, NIMG, HEADS])
        st = sb("st", [TOK, 4, NIMG])

        h_in, tail_w = sem("tokens_loaded"), sem("tail_weights_loaded")
        we_in, sel_loaded = sem("expert_weights_loaded"), sem("selector_loaded")
        dve_step = sem("dve_step")
        var_ready, dev_ready, y_ready = sem("variance_ready"), sem("deviation_ready"), sem("layernorm_ready")
        yt_full, yt_ready = sem("yt_full"), sem("yt_ready")
        q_full, q_ready = sem("q_full"), sem("q_ready")
        k_full, k_ready = sem("k_full"), sem("k_ready")
        v_full, v_ready = sem("v_full"), sem("v_ready")
        km_ready, s_full, s_ready = sem("masked_keys_ready"), sem("scores_full"), sem("scores_ready")
        max_ready, sub_ready, exp_ready = sem("max_ready"), sem("shifted_ready"), sem("exp_ready")
        sum_ready = sem("sum_ready")
        pm_ready, pt_full, pt_ready = sem("windowed_ready"), sem("pt_full"), sem("pt_ready")
        o_full, o_ready = sem("o_full"), sem("o_ready")
        ot_full, ot_ready = sem("ot_full"), sem("ot_ready")
        pj_full, pj_ready = sem("projected_full"), sem("projected_ready")
        lg_full, lg_ready = sem("logits_full"), sem("logits_ready")
        le_ready, lx_ready, sc_ready = sem("shifted_logits_ready"), sem("exp_logits_ready"), sem("expert_scores_ready")
        st_full, st_ready = sem("st_full"), sem("st_ready")
        bc_full, zx_ready, zx_used = sem("broadcast_full"), sem("zx_ready"), sem("zx_used")
        lt_full, lt_ready = sem("lt_full"), sem("lt_ready")
        f_full, f_ready = sem("ffn_full"), sem("ffn_ready")
        out_ready, out_stored = sem("out_ready"), sem("out_stored")

        SPR = [PSALL[:, 2 * i:2 * i + 2, 0:4 * TOK] for i in range(2)]
        PTP = PSALL[:, 4:6, 0:4 * TOK]

        def tail_sync(sp):
            sp.dma_start(H[0:1], cls_rows).then_inc(h_in, 16)
            sp.dma_start(H[1:TOK], hid_scr.rearrange("p g r b (h w) -> h (p g r b) w", w=GRID)).then_inc(h_in, 16)
            sp.dma_start(WE, w_expert).then_inc(we_in, 16)
            sp.wait_ge(y_ready, 2)
            sp.dma_start(SEL, sel_in).then_inc(sel_loaded, 16)
            sp.wait_ge(out_ready, 1)
            sp.dma_start(out.rearrange("b t d -> t b d"), TMP).then_inc(out_stored, 16)
            sp.wait_ge(out_stored, 16)

        def tail_tensor(pe):
            pe.wait_ge(tail_w, 16 * TAIL_LOADS)

            def transposes(c, ready, src, width, dst, full):
                for i in range(BC):
                    m = pe.transpose(dst[0:width, i * TOK:(i + 1) * TOK], src(c * BC + i), ident[0:TOK, 0:TOK])
                m.then_inc(full, 1)

            def qkv(c):
                pe.wait_ge(yt_ready, c + 1)
                x = YT[0:GRID, c * CT:(c + 1) * CT]
                if c:
                    pe.wait_ge(q_ready, c)
                pe.matmul(PS[2][0:GRID, 0:CT], WQKV[:, 0:GRID], x, start=True, stop=True).then_inc(q_full, 1)
                if c:
                    pe.wait_ge(k_ready, c)
                pe.matmul(PS[3][0:GRID, 0:CT], WQKV[:, GRID:2 * GRID], x, start=True, stop=True).then_inc(k_full, 1)
                if c:
                    pe.wait_ge(v_ready, c)
                for i in range(BC):
                    b = c * BC + i
                    m = pe.matmul(PS[4][0:TOK, i * GRID:(i + 1) * GRID], YT[0:GRID, b * TOK:(b + 1) * TOK],
                                  WQKV[:, 2 * GRID:3 * GRID], start=True, stop=True)
                m.then_inc(v_full, 1)

            pe.wait_ge(y_ready, 1)
            for c in range(NC + 1):
                if c < NC:
                    if c >= 2:
                        pe.wait_ge(yt_ready, c - 1)
                    transposes(c, None, lambda b: Y[:, b, 0, :], GRID, PS[c % 2], yt_full)
                if c:
                    qkv(c - 1)

            def scores(b):
                if b == 0:
                    pe.wait_ge(q_ready, NC)
                    pe.wait_ge(k_ready, NC)
                    pe.wait_ge(v_ready, NC)
                    pe.wait_ge(yt_ready, NC)
                if b % BC == 0:
                    pe.wait_ge(km_ready, HEADS * (b // BC + 1))
                if b >= 2:
                    pe.wait_ge(s_ready, b - 1)
                for hf in range(2):
                    m = pe.matmul(SPR[b % 2][0:TOK, hf, :], QT[:, b * TOK:(b + 1) * TOK],
                                  KM[:, b // BC % 2, 4 * hf:4 * hf + 4, b % BC * TOK:(b % BC + 1) * TOK],
                                  start=True, stop=True)
                m.then_inc(s_full, 1)

            def turn_probs(b):
                pe.wait_ge(pm_ready, b + 1)
                if b:
                    pe.wait_ge(pt_ready, b)
                for h in range(HEADS):
                    m = pe.transpose(PTP[0:TOK, h // 4, h % 4 * TOK:(h % 4 + 1) * TOK], PM[:, b % 3, h, :],
                                     ident[0:TOK, 0:TOK])
                m.then_inc(pt_full, 1)

            def values(b):
                pe.wait_ge(pt_ready, b + 1)
                if b % BC == 0 and b:
                    pe.wait_ge(o_ready, b // BC)
                for h in range(HEADS):
                    m = pe.matmul(PS[6][0:TOK, b % BC * GRID + h * HD:b % BC * GRID + (h + 1) * HD], PT[:, b % 2, h, :],
                                  V[:, b, h * HD:(h + 1) * HD], start=True, stop=True)
                m.then_inc(o_full, 1)

            def project(c):
                pe.wait_ge(o_ready, c + 1)
                if c:
                    pe.wait_ge(pj_ready, c)
                transposes(c, None, lambda b: O[:, b, :], GRID, PS[7], ot_full)
                pe.wait_ge(ot_ready, c + 1)
                for i in range(BC):
                    m = pe.matmul(PS[7][0:TOK, i * GRID:(i + 1) * GRID], OT[:, c % 2, i * TOK:(i + 1) * TOK], WP[:],
                                  start=True, stop=True)
                m.then_inc(pj_full, 1)

            for i in range(NIMG + LAG + 2):
                if i < NIMG:
                    scores(i)
                if LAG <= i < NIMG + LAG:
                    turn_probs(i - LAG)
                if i >= LAG + 1 and i - LAG - 1 < NIMG:
                    values(i - LAG - 1)
                if i > LAG + 1 and (i - LAG - 2) % BC == BC - 1:
                    project((i - LAG - 2) // BC)

            pe.wait_ge(y_ready, 2)
            for c in range(NC + 1):
                if c < NC:
                    if c >= 2:
                        pe.wait_ge(yt_ready, NC + c - 1)
                    transposes(c, None, lambda b: Y[:, b].rearrange("p t d -> p (t d)"), 128, PS[c % 2], yt_full)
                if c:
                    pe.wait_ge(yt_ready, NC + c)
                    if c >= 3:
                        pe.wait_ge(lg_ready, c - 2)
                    for i in range(BC):
                        b = (c - 1) * BC + i
                        m = pe.matmul(PS[2 + (c - 1) % 2][0:TOK, i * EXPERTS:(i + 1) * EXPERTS],
                                      YT[0:GRID, b * TOK:(b + 1) * TOK], GATE[:], start=True, stop=True)
                    m.then_inc(lg_full, 1)
            pe.wait_ge(sc_ready, 1)
            for c in range(NC):
                if c >= 2:
                    pe.wait_ge(st_ready, c - 1)
                transposes(c, None, lambda b: SC[:, b, :], EXPERTS, PS[c % 2], st_full)
            pe.wait_ge(st_ready, NC)
            pe.wait_ge(lg_ready, NC)
            pe.wait_ge(we_in, 16)
            pe.wait_ge(sel_loaded, 16)
            PAIRS = EXPERTS // 2

            def expert_product(n):
                z, ep = n // PAIRS, n % PAIRS
                pe.wait_ge(zx_ready, n + 1)
                if ep == 0 and z >= 2:
                    pe.wait_ge(lt_ready, z - 1)
                m = pe.matmul(PS[4 + z % 2][0:GRID, 0:ZT], WE[:, ep, :], ZX[:, n % 4, :],
                              start=(ep == 0), stop=(ep == PAIRS - 1))
                m.then_inc(zx_used, 1)

            for n in range(NZ * PAIRS + 2):
                if n < NZ * PAIRS:
                    if n >= 4:
                        pe.wait_ge(zx_ready, n - 3)
                    z, ep = n // PAIRS, n % PAIRS
                    pe.matmul(PS[n % 4][:, 0:ZT], SEL[:, ep, :], ST[:, z * ZT:(z + 1) * ZT],
                              start=True, stop=True).then_inc(bc_full, 1)
                if n >= 2:
                    expert_product(n - 2)
            for c in range(NC):
                pe.wait_ge(lt_ready, -(-(c + 1) * CT // ZT))
                if c >= 2:
                    pe.wait_ge(f_ready, c - 1)
                for i in range(BC):
                    b = c * BC + i
                    m = pe.matmul(PS[6 + c % 2][0:TOK, i * GRID:(i + 1) * GRID], LT[:, b * TOK:(b + 1) * TOK], WO[:],
                                  start=True, stop=True)
                m.then_inc(f_full, 1)

        def tail_scalar(act):
            act.wait_ge(tail_w, 16 * TAIL_LOADS)

            def deviation(n):
                act.wait_ge(var_ready, n + 1)
                nc.scalar.activation(st[:, 2, :], st[:, 1, :], ACT.Sqrt).then_inc(dev_ready, 1)

            deviation(0)
            for c in range(NC):
                act.wait_ge(q_full, c + 1)
                nc.scalar.activation(QT[:, c * CT:(c + 1) * CT], PS[2][0:GRID, 0:CT], ACT.Identity, bias=BQK[:, 0:1]
                                     ).then_inc(q_ready, 1)
                act.wait_ge(k_full, c + 1)
                nc.scalar.activation(KT[:, c * CT:(c + 1) * CT], PS[3][0:GRID, 0:CT], ACT.Identity, bias=BQK[:, 1:2]
                                     ).then_inc(k_ready, 1)
            act.wait_ge(k_ready, NC)
            for i in range(NIMG + LAG + 1):
                if i % BC == 0 and i < NIMG:
                    c = i // BC
                    if c >= 2:
                        act.wait_ge(s_full, (c - 1) * BC)
                    for h in range(HEADS):
                        nc.scalar.activation(KM[:, c % 2, h, :], KT[:, c * CT:(c + 1) * CT], ACT.Copy,
                                             scale=HM[:, h:h + 1]).then_inc(km_ready, 1)
                if 1 <= i <= NIMG:
                    b = i - 1
                    act.wait_ge(sub_ready, b + 1)
                    nc.scalar.activation(PR[:, b % 4], PR[:, b % 4], ACT.Exp).then_inc(exp_ready, 1)
                if i >= LAG and i - LAG < NIMG:
                    b = i - LAG
                    act.wait_ge(pt_full, b + 1)
                    if b >= 2:
                        act.wait_ge(o_full, b - 1)
                    nc.scalar.copy(PT[:, b % 2].rearrange("p (a h) t -> p a (h t)", a=2), PTP[0:TOK]).then_inc(pt_ready, 1)
                if i > LAG + 1 and (i - LAG - 2) % BC == BC - 1:
                    turn_out(act, (i - LAG - 2) // BC)
            turn_out(act, NC - 1)
            deviation(1)
            act.wait_ge(le_ready, 1)
            nc.scalar.activation(SC, SC, ACT.Exp).then_inc(lx_ready, 1)
            for z in range(NZ):
                act.wait_ge(zx_used, (z + 1) * (EXPERTS // 2))
                nc.scalar.copy(LT[:, z * ZT:(z + 1) * ZT], PS[4 + z % 2][0:GRID, 0:ZT]).then_inc(lt_ready, 1)
            deviation(2)

        def turn_out(act, c):
            act.wait_ge(ot_full, c + 1)
            nc.scalar.copy(OT[:, c % 2, :], PS[7][0:GRID, 0:CT]).then_inc(ot_ready, 1)

        def tail_pool(pool):
            pool.wait_ge(tail_w, 16 * TAIL_LOADS)
            for i in range(NIMG + 2):
                if i < NIMG:
                    pool.wait_ge(max_ready, i + 1)
                    nc.gpsimd.tensor_tensor(PR[:, i % 4], PR[:, i % 4],
                                            smx[:, i % 4, :].unsqueeze(2).broadcast_to([TOK, HEADS, TOK]),
                                            ALU.subtract).then_inc(sub_ready, 1)
                if i >= 2:
                    b = i - 2
                    pool.wait_ge(exp_ready, b + 1)
                    if b >= 3:
                        pool.wait_ge(pt_full, b - 2)
                    nc.gpsimd.tensor_tensor(PM[:, b % 3], PR[:, b % 4],
                                            BAND[:].unsqueeze(1).broadcast_to([TOK, HEADS, TOK]), ALU.mult
                                            ).then_inc(pm_ready, 1)

        def tail_vector(dve):
            steps = [0]

            def link(ins):
                steps[0] += 1
                ins.then_inc(dve_step, 1)
                dve.wait_ge(dve_step, steps[0])

            def over(x, n=GRID):
                return x.unsqueeze(2).broadcast_to([TOK, NIMG, n])

            def rows(x, n=NIMG):
                return x.unsqueeze(1).broadcast_to([TOK, n, GRID])

            def normalise(src, n):
                link(nc.vector.reduce_sum(st[:, 0, :], src, AX.X))
                link(nc.vector.tensor_scalar(st[:, 0, :], st[:, 0, :], 1.0 / GRID, None, ALU.mult))
                link(nc.vector.tensor_tensor(TMP, src, over(st[:, 0, :]), ALU.subtract))
                link(nc.vector.tensor_tensor(Y[:, :, 1, :], TMP, TMP, ALU.mult))
                link(nc.vector.reduce_sum(st[:, 1, :], Y[:, :, 1, :], AX.X))
                nc.vector.tensor_scalar(st[:, 1, :], st[:, 1, :], 1.0 / GRID, EPS, ALU.mult, ALU.add).then_inc(var_ready, 1)
                dve.wait_ge(dev_ready, n + 1)
                link(nc.vector.reciprocal(st[:, 3, :], st[:, 2, :]))

            dve.wait_ge(tail_w, 16 * TAIL_LOADS)
            dve.wait_ge(h_in, 32)
            normalise(H, 0)
            nc.vector.tensor_tensor(Y[:, :, 0, :], TMP, over(st[:, 3, :]), ALU.mult).then_inc(y_ready, 1)
            link(nc.vector.tensor_tensor(H, H, rows(BP[:]), ALU.add))
            for c in range(NC + 1):
                if c < NC:
                    dve.wait_ge(yt_full, c + 1)
                    nc.vector.tensor_copy(YT[0:GRID, c * CT:(c + 1) * CT], PS[c % 2][0:GRID, 0:CT]).then_inc(yt_ready, 1)
                if c:
                    dve.wait_ge(v_full, c)
                    nc.vector.tensor_tensor(V[:, (c - 1) * BC:c * BC, :],
                                            PS[4][0:TOK, 0:BC * GRID].rearrange("p (b d) -> p b d", b=BC),
                                            rows(BV[:], BC), ALU.add).then_inc(v_ready, 1)

            def attended(c):
                a = slice(c * BC, (c + 1) * BC)
                dve.wait_ge(o_full, (c + 1) * BC)
                link(nc.vector.reciprocal(rden[:, a, :], den[:, a, :]))
                nc.vector.tensor_tensor(
                    O[:, a, :].rearrange("p b (h e) -> p (b h) e", h=HEADS),
                    PS[6][0:TOK, 0:BC * GRID].rearrange("p (n e) -> p n e", e=HD),
                    rden[:, a, :].rearrange("p b h -> p (b h)").unsqueeze(2).broadcast_to([TOK, BC * HEADS, HD]),
                    ALU.mult).then_inc(o_ready, 1)

            def residual(c):
                a = slice(c * BC, (c + 1) * BC)
                dve.wait_ge(pj_full, c + 1)
                nc.vector.tensor_tensor(H[:, a, :], PS[7][0:TOK, 0:BC * GRID].rearrange("p (b d) -> p b d", b=BC),
                                        H[:, a, :], ALU.add).then_inc(pj_ready, 1)

            for i in range(NIMG + LAG + 3):
                if i < NIMG:
                    dve.wait_ge(s_full, i + 1)
                    if i >= 4:
                        dve.wait_ge(pm_ready, i - 3)
                        dve.wait_ge(sum_ready, i - 3)
                    nc.vector.tensor_tensor(
                        PR[:, i % 4].rearrange("p (a h) t -> p a (h t)", a=2), SPR[i % 2][0:TOK],
                        BAND4[:].unsqueeze(1).broadcast_to([TOK, 2, 4 * TOK]), ALU.mult).then_inc(s_ready, 1)
                    dve.wait_ge(s_ready, i + 1)
                    nc.vector.reduce_max(smx[:, i % 4, :], PR[:, i % 4], AX.X).then_inc(max_ready, 1)
                if 2 <= i < NIMG + 2:
                    b = i - 2
                    dve.wait_ge(exp_ready, b + 1)
                    nc.vector.reduce_sum(den[:, b, :], PR[:, b % 4], AX.X).then_inc(sum_ready, 1)
                    dve.wait_ge(sum_ready, b + 1)
                if i >= LAG + 1 and (i - LAG - 1) % BC == BC - 1:
                    attended((i - LAG - 1) // BC)
                if i > LAG + 2 and (i - LAG - 2) % BC == BC - 1:
                    residual((i - LAG - 2) // BC)
            dve.wait_ge(pj_ready, NC)
            normalise(H, 1)
            link(nc.vector.tensor_tensor(Y[:, :, 0, :], TMP, over(st[:, 3, :]), ALU.mult))
            nc.vector.tensor_copy(Y[:, :, 1, :], Y[:, :, 0, :]).then_inc(y_ready, 1)
            link(nc.vector.memset(LG[:, :, EXPERTS:LW], SENTINEL))
            for c in range(NC + 1):
                if c < NC:
                    dve.wait_ge(yt_full, NC + c + 1)
                    nc.vector.tensor_copy(YT[:, c * CT:(c + 1) * CT], PS[c % 2][:, 0:CT]).then_inc(yt_ready, 1)
                if c:
                    a = slice((c - 1) * BC, c * BC)
                    dve.wait_ge(lg_full, c)
                    nc.vector.tensor_copy(LG[:, a, 0:EXPERTS],
                                          PS[2 + (c - 1) % 2][0:TOK, 0:BC * EXPERTS].rearrange("p (b e) -> p b e", b=BC)
                                          ).then_inc(lg_ready, 1)
            dve.wait_ge(lg_ready, NC)
            for b in range(NIMG):
                m = nc.vector.max(M8[:, b, :], LG[:, b, 0:EXPERTS])
            link(m)
            link(nc.vector.tensor_tensor(SC, LG[:, :, 0:EXPERTS],
                                         M8[:, :, 0:1].broadcast_to([TOK, NIMG, EXPERTS]), ALU.subtract))
            dve.sem_inc(le_ready, 1)
            link(nc.vector.memset(M8[:, :, TOPK:8], SENTINEL))
            for b in range(NIMG):
                m = nc.vector.match_replace(LR[:, b, :], M8[:, b, :], LG[:, b, :], -SENTINEL)
            link(m)
            link(nc.vector.tensor_tensor(TMP, LR[:, :, 0:EXPERTS], LG[:, :, 0:EXPERTS], ALU.not_equal))
            dve.wait_ge(lx_ready, 1)
            link(nc.vector.tensor_tensor(SC, SC, TMP, ALU.mult))
            link(nc.vector.reduce_sum(st[:, 0, :], SC, AX.X))
            link(nc.vector.reciprocal(st[:, 3, :], st[:, 0, :]))
            nc.vector.tensor_tensor(SC, SC, over(st[:, 3, :]), ALU.mult).then_inc(sc_ready, 1)
            for c in range(NC):
                dve.wait_ge(st_full, c + 1)
                nc.vector.tensor_copy(ST[:, c * CT:(c + 1) * CT], PS[c % 2][0:EXPERTS, 0:CT]).then_inc(st_ready, 1)
            for n in range(NZ * EXPERTS // 2):
                z = n // (EXPERTS // 2)
                dve.wait_ge(bc_full, n + 1)
                if n >= 4:
                    dve.wait_ge(zx_used, n - 3)
                nc.vector.tensor_tensor(ZX[:, n % 4, :], PS[n % 4][:, 0:ZT], YT[:, z * ZT:(z + 1) * ZT], ALU.mult
                                        ).then_inc(zx_ready, 1)
            F = SC
            link(nc.vector.tensor_tensor(F, Y[:, :, 0, :], rows(OB[:]), ALU.add))
            for c in range(NC):
                a = slice(c * BC, (c + 1) * BC)
                dve.wait_ge(f_full, c + 1)
                nc.vector.tensor_tensor(F[:, a, :], PS[6 + c % 2][0:TOK, 0:BC * GRID].rearrange("p (b d) -> p b d", b=BC),
                                        F[:, a, :], ALU.add).then_inc(f_ready, 1)
            dve.wait_ge(f_ready, NC)
            normalise(F, 2)
            link(nc.vector.tensor_tensor(TMP, TMP, over(st[:, 3, :]), ALU.mult))
            link(nc.vector.tensor_tensor(TMP, TMP, rows(LNG[:]), ALU.mult))
            link(nc.vector.tensor_tensor(TMP, TMP, rows(LNB[:]), ALU.add))
            nc.vector.tensor_tensor(TMP, TMP, H, ALU.add).then_inc(out_ready, 1)

        block = ctx.enter_context(nc.Block())

        @block.sync
        def _(sp):
            sp.dma_start(X[:, 0, :], xall).then_inc(c4_in, 16)
            for dst, src in [(DW, dft_w), (ident, ident_in), (DH, dft_h), (EH[0:KOUT], idft_h), (EH[64:64 + KOUT], idft_h),
                             (EW, idft_w), (CWALL, conv_wb), (W1, fc1_w), (B1, fc1_b), (W2, fc2_w), (B2, fc2_b)]:
                sp.dma_start(dst[:], src).then_inc(consts, 16)
            sp.wait_ge(zeroed, 2)
            sp.sem_inc(stored.sem, stored.credit)
            turn, passes = Turns(sp, "layer", LAYER_COUNTS), Turns(sp, "pass", PASS_COUNTS)

            def load_piece(kxd, layer):
                before = kxd - SLOTS if kxd >= SLOTS else max(range(kxd, KXD, SLOTS)) - KXD
                turn.wait(piece_used, before + 1)
                slot = kxd % SLOTS
                for j in range(B4):
                    sp.dma_start(SW[j * CH:(j + 1) * CH, slot, j, :],
                                 spec_w[bass.ds(layer, 1), kxd, j].rearrange("l c n -> (l c) n")
                                 ).then_inc(piece_in[slot].sem, 16)

            def load_coords(p):
                passes.wait(pass_done, 1)
                sp.dma_start(W0[:], fc0_all[:, bass.ds(p * NG, NG), :]).then_inc(w0_in.sem, 16)
                for q in range(N_X):
                    if q >= 2:
                        passes.wait(x0_full, NG * (q - 1))
                    sp.dma_start(COIN[:, q % 2, :], xall[:, q * BANK:(q + 1) * BANK]).then_inc(co_in[q % 2].sem, 16)

            def layer(p, l, first):
                for kxd in range(SLOTS):
                    load_piece(kxd, l)
                if first:
                    load_coords(p)
                for d in range(KXD):
                    if d + SLOTS < KXD:
                        load_piece(d + SLOTS, l)
                    turn.wait(mix_ready, -(-(d + 1) * KYG // 4))
                    sp.dma_start(spec_scr[B4 * d:B4 * (d + 1)].rearrange("k r b n -> (k r b) n"),
                                 MIXED[:, d * MODES * CH:(d + 1) * MODES * CH]).then_inc(stored.sem, 16)
                modes = spec_scr.rearrange("k r b (y o) -> (k r) y b o", y=MODES)
                for n in range(NG):
                    if n == 0:
                        turn.wait(stored, KXD)
                    if n >= 2:
                        turn.wait(g_full, (n - 1) * N_G)
                    r = 64 * (n % 2)
                    for b in range(B4):
                        sp.dma_start(MODE[r:r + KOUT].rearrange("p y (b o) -> p y b o", b=B4)[:, :, b],
                                     modes[:, :, n * B4 + b]).then_inc(loaded[n % 2].sem, 16)

            with sp.Fori(0, PASSES) as p:
                layer(p, 0, True)
                turn.next()
                with sp.Fori(1, LAYERS) as l:
                    layer(p, l, False)
                    turn.next()
                for n in range(NG):
                    passes.wait(fc2_ready, 4 * (n + 1))
                    for tile in range(4):
                        qp, pr = tile // 2, tile % 2
                        sp.dma_start(
                            hid_scr[bass.ds(p, 1), n, pr].rearrange("o b (d q n) -> q (o b) d n", d=4, q=2)[qp],
                            HO[32 * tile:32 * tile + 2]).then_inc(ho_out.sem, 16)
                passes.next()
            sp.wait_ge(ho_out.sem, PASSES * NG * 64)
            tail_sync(sp)

        @block.tensor
        def _(pe):
            pe.wait_ge(consts, 16 * CONST_LOADS)
            pe.wait_ge(c4_in, 16)
            pe.wait_ge(zeroed, 2)
            pe.wait_ge(credits, 1)
            pe.sem_inc(t1_full.sem, t1_full.credit - N_XT)
            for c in (tr_full, sp_full, piece_used, gt_full, x_full):
                pe.sem_inc(c.sem, c.credit)

            def transpose_x(bank, x, q):
                for i in range(4):
                    c = q * BANK + i * 128
                    m = pe.transpose(bank[:, i * 128:(i + 1) * 128], x[:, c:c + 128], ident[:])
                m.then_inc(xt_full.sem, 1)

            def dft_columns(k):
                for i in range(4):
                    m = pe.matmul(t1_bank[k % 2][:, i * H2 * KOUT:(i + 1) * H2 * KOUT],
                                  XT[:, k % 2, i * 128:(i + 1) * 128], DW[:], start=True, stop=True)
                m.then_inc(t1_full.sem, 1)

            for j in range(N_XT + 1):
                if j < N_XT:
                    if j >= 2:
                        pe.wait_ge(xt_ready.sem(j), 1 + j // 2)
                    transpose_x(xt_bank[j % 2], X[:, 0, :], j)
                if j:
                    pe.wait_ge(xt_ready.sem(j - 1), 2 + (j - 1) // 2)
                    if j >= 3:
                        pe.wait_ge(t1_ready.sem, j - 2)
                    dft_columns(j - 1)
            pe.wait_ge(t1_ready.sem, N_XT)

            turn, cols, passes = Turns(pe, "layer", LAYER_COUNTS), Turns(pe, "cols", COLUMN_COUNTS), Turns(pe, "pass", PASS_COUNTS)

            def fc0(m):
                q, n = m // NG, m % NG
                if m == 0:
                    passes.wait(w0_in, 1)
                if n == 0:
                    passes.wait(co_in[q % 2], q // 2 + 1)
                if m >= 2:
                    passes.wait_job(x0_ready, m - 2)
                pe.matmul(xt_bank[m % 2][:, :], W0[:, n, :], COIN[:, q % 2, :], start=True, stop=True).then_inc(x0_full.sem, 1)

            def transpose(k):
                if k < 2:
                    turn.wait(x_ready, k - 3)
                cols.wait_job(xt_ready, k - 2)
                transpose_x(xt_bank[k % 2], X[:, k // N_XT, :], k % N_XT)

            def columns(k):
                cols.wait_job(xt_ready, k)
                if k < 2:
                    turn.wait(x_ready, k - 1)
                else:
                    cols.wait(t1_ready, k - 1)
                dft_columns(k)

            def rows_onto_partitions(n, j, first):
                m0 = n * N_TR + j
                if m0 < 2:
                    turn.wait(gt_ready, m0 - 1)
                else:
                    turn.wait_job(tr_ready, m0 - 2)
                if j == 0 and not first:
                    cols.wait(t1_ready, (n + 1) * N_XT)
                for i in range(4):
                    ky = 4 * j + i
                    dst = tr_bank[m0 % 2][:, i * 128:(i + 1) * 128]
                    if first:
                        m = pe.matmul(dst, T1C[:, RI * ky:RI * (ky + 1), :].rearrange("p r h -> p (r h)"),
                                      W0[:, n, :], start=True, stop=True)
                    else:
                        m = pe.transpose(dst, T1[:, n % 2, RI * ky:RI * (ky + 1), :].rearrange("p r h -> p (r h)"), ident[:])
                m.then_inc(tr_full.sem, 1)

            def dft_rows(n, kyg):
                j, ki = kyg // SPK, kyg % SPK
                turn.wait_job(tr_ready, n * N_TR + kyg)
                if ki == 0:
                    if n:
                        turn.wait(sp_ready, (n - 1) * N_F + j + 1)
                    else:
                        turn.wait(g_ready, j - 1)
                for b in range(B4):
                    m = pe.matmul(sp_bank[j][:, (ki * B4 + b) * KOUT:(ki * B4 + b + 1) * KOUT],
                                  TR[:, n % 2, b, 4 * kyg:4 * kyg + 4, :].rearrange("p k c -> p (k c)"), DH[:],
                                  start=True, stop=True)
                if ki == SPK - 1 or kyg == KYG - 1:
                    m.then_inc(sp_full.sem, 1)

            def mix():
                for blk in range(MIXB):
                    kxd, kyg, job = blk // KYG, blk % KYG, blk // 4
                    if blk == 0:
                        turn.wait(sp_ready, (NG - 1) * N_F + 1)
                    if blk == SPK:
                        turn.wait(sp_ready, NG * N_F)
                    if kyg == 0:
                        turn.wait(piece_in[kxd % SLOTS], kxd // SLOTS + 1)
                    if blk % 4 == 0 and job >= 2:
                        turn.wait(mix_ready, job - 1)
                    for q in range(B4):
                        c = (q * KYG + kyg) * CH
                        m = pe.matmul(mix_bank[job % 2][32 * q:32 * q + RI * GIMG, (blk % 4) * 128:(blk % 4 + 1) * 128],
                                      SPEC[:, kyg, 4 * kxd + q, :], SW[:, kxd % SLOTS, :, c:c + CH],
                                      start=True, stop=True, tile_position=(0, 32 * q))
                    if kyg == KYG - 1:
                        m.then_inc(piece_used.sem, 1)
                    if blk % 4 == 3 or blk == MIXB - 1:
                        if kyg == KYG - 1:
                            m = pe.matmul(mix_bank[job % 2][32 * q:32 * q + RI * GIMG, (blk % 4) * 128:(blk % 4 + 1) * 128],
                                          SPEC[:, kyg, 4 * kxd + q, :], SW[:, kxd % SLOTS, :, c:c + CH],
                                          start=True, stop=True, tile_position=(0, 32 * q))
                        m.then_inc(mix_full.sem, 1)

            def pointwise(u, first):
                if u == 0:
                    if first:
                        passes.wait_jobs(x0_ready, NP)
                    turn.wait(cw_set, 1)
                elif u == 2:
                    turn.wait(mix_ready, N_MIX)
                elif u >= AHEAD:
                    turn.wait(x_ready, u + 1 - AHEAD)
                pe.matmul(x_bank[u % 4][:, :], CW[:, 0:128], X[:, u // N_X, u % N_X * BANK:(u % N_X + 1) * BANK],
                          start=True, stop=True, skip_group_check=True)

            def inverse_rows(n, j):
                m0, r = n * N_G + j, 64 * (n % 2)
                if j == 0:
                    turn.wait(loaded[n % 2], n // 2 + 1)
                if m0 >= 2:
                    turn.wait(g_ready, m0 - 1)
                for i in range(4):
                    m = pe.matmul(g_bank[m0 % 2][:, i * 128:(i + 1) * 128], MODE[r:r + KOUT, 4 * j + i, :],
                                  EH[r:r + KOUT, :], start=True, stop=True)
                m.then_inc(g_full.sem, 1)

            def turn_back(u):
                n, q = u // N_X, u % N_X
                if q == 0:
                    turn.wait(g_ready, (n + 1) * N_G)
                if u >= 2:
                    turn.wait(gt_ready, u - 1)
                for i in range(4):
                    hh = 4 * q + i
                    m = pe.transpose(gt_bank[u % 2][0:H2 * KOUT, i * 128:(i + 1) * 128],
                                     G[:, n % 2, H2 * RI * hh:H2 * RI * (hh + 1), :].rearrange("p a b -> p (a b)"), ident[:])
                m.then_inc(gt_full.sem, 1)

            def inverse_columns(u):
                turn.wait(gt_ready, u + 1)
                for i in range(4):
                    m = pe.matmul(x_bank[u % 4][:, i * 128:(i + 1) * 128], GT[:, u % 4, i, :], EW[:],
                                  start=False, stop=True, skip_group_check=True)
                m.then_inc(x_full.sem, 1)

            def layer(first):
                for stage, k in FIRST_FORWARD if first else FORWARD:
                    if stage == "transpose":
                        fc0(k) if first else transpose(k)
                    elif stage == "columns" and not first:
                        columns(k)
                    elif stage == "turn":
                        rows_onto_partitions(*k, first)
                    elif stage == "rows":
                        dft_rows(*k)
                mix()
                for stage, u in INVERSE:
                    if stage == "pointwise":
                        pointwise(u, first)
                    elif stage == "modes":
                        inverse_rows(*u)
                    elif stage == "turn_back":
                        turn_back(u)
                    else:
                        inverse_columns(u)

            with pe.Fori(0, PASSES) as p:
                layer(True)
                turn.next()
                with pe.Fori(1, LAYERS) as l:
                    layer(False)
                    turn.next()
                    cols.next()
                turn.wait(x_ready, 0)
                turn.wait(gt_ready, 0)
                turn.wait(g_ready, 0)
                for m0 in range(NP // 2 + 1):
                    if m0 < NP // 2:
                        for i in range(FB):
                            k = FB * m0 + i
                            u, pr = k // 2, k % 2
                            if k >= 4:
                                passes.wait(fc1_ready, k - 3)
                            pe.matmul(PS[4 + k % 4][:, :], W1[:, pr, :], X[:, u // N_X, u % N_X * BANK:(u % N_X + 1) * BANK],
                                      start=True, stop=True).then_inc(fc1_full.sem, 1)
                    if m0:
                        if m0 >= 3:
                            passes.wait(fc2_ready, m0 - 2)
                        passes.wait(fc1_ready, FB * m0)
                        for i in range(FB):
                            m = pe.matmul(PS[(m0 - 1) % 2][32 * i:32 * i + 32, :], W2[:], FH[:, (m0 - 1) % 2 * FB + i, :],
                                          start=True, stop=True, tile_position=(0, 32 * i))
                        m.then_inc(fc2_full.sem, 1)
                passes.wait(fc2_ready, NP // 2)
                passes.next()
            tail_tensor(pe)

        @block.scalar
        def _(act):
            for dst, src in [(WQKV, w_qkv), (BQK, b_qk), (BV, b_v), (WP, w_proj), (BP, b_proj), (GATE, gate_w),
                             (WO, out_w), (OB, out_b), (LNG, ln_g), (LNB, ln_b), (HM, head_mask),
                             (BAND, band), (BAND4, band4)]:
                act.dma_start(dst[:], src).then_inc(tail_w, 16)
            act.wait_ge(consts, 16 * CONST_LOADS)
            act.sem_inc(xt_ready.sem(1), 1)
            act.sem_inc(tr_ready.sem(1), 1)
            for c in (gt_ready, x_ready):
                act.sem_inc(c.sem, c.credit)
            for j in range(1, N_XT, 2):
                act.wait_ge(xt_full.sem, j + 1)
                if j >= 2:
                    act.wait_ge(t1_full.sem, 2 + j - 1)
                nc.scalar.copy(XT[:, j % 2, :], xt_bank[j % 2][:, :]).then_inc(xt_ready.sem(1), 1)
            turn, cols, passes = Turns(act, "layer", LAYER_COUNTS), Turns(act, "cols", COLUMN_COUNTS), Turns(act, "pass", PASS_COUNTS)

            def fc0_out(m):
                passes.wait(x0_full, m + 1)
                q, n = m // NG, m % NG
                nc.scalar.copy(X[:, n, q * BANK:(q + 1) * BANK], xt_bank[m % 2][:, :]).then_inc(x0_ready.sem(1), 1)

            def transposed(k):
                cols.wait(xt_full, k + 1)
                cols.wait(t1_full, k - 1)
                nc.scalar.copy(XT[:, k % 2, :], xt_bank[k % 2][:, :]).then_inc(xt_ready.sem(1), 1)

            def turned(n, j):
                m = n * N_TR + j
                turn.wait(tr_full, m + 1)
                turn.wait(sp_full, (n - 1) * N_F)
                nc.scalar.copy(TR[:, n % 2, :, 4 * j:4 * j + 4, :].rearrange("p b k c -> p k b c"),
                               tr_bank[m % 2][:, :].rearrange("p (k b c) -> p k b c", k=4, b=B4)
                               ).then_inc(tr_ready.sem(1), 1)

            def spectrum(n, j):
                turn.wait(sp_full, n * N_F + j + 1)
                ks = min(SPK, KYG - SPK * j)
                nc.scalar.copy(
                    SPEC[:, SPK * j:SPK * j + ks].rearrange("p k x (r b) -> p k (x r) b", r=RI)[:, :, :, n * B4:(n + 1) * B4],
                    sp_bank[j][:, 0:ks * B4 * KOUT].rearrange("p (k b n) -> p k n b", k=ks, b=B4)
                ).then_inc(sp_ready.sem, 1)

            def mixed():
                for j in range(N_MIX):
                    turn.wait(mix_full, j + 1)
                    if j == 0:
                        turn.wait(stored, 0)
                    w = min(BANK, MIXB * 128 - j * BANK)
                    nc.scalar.copy(MIXED[:, j * BANK:j * BANK + w], mix_bank[j % 2][:, 0:w]).then_inc(mix_ready.sem, 1)

            def turned_back(u):
                turn.wait(gt_full, u + 1)
                turn.wait(x_full, u + 1 - 4)
                nc.scalar.copy(GT[:, u % 4].rearrange("p h n -> p (h n)"),
                               gt_bank[u % 2][0:H2 * KOUT, :]).then_inc(gt_ready.sem, 1)

            def activated(u):
                turn.wait(x_full, u + 1)
                nc.scalar.activation(X[:, u // N_X, u % N_X * BANK:(u % N_X + 1) * BANK], x_bank[u % 4][:, :],
                                     ACT.Gelu, bias=CW[:, 128:129]).then_inc(x_ready.sem, 1)

            def layer(first):
                for stage, k in FIRST_FORWARD if first else FORWARD:
                    if stage == "transpose" and k % 2:
                        fc0_out(k) if first else transposed(k)
                    elif stage == "turn" and (k[0] * N_TR + k[1]) % 2:
                        turned(*k)
                    elif stage == "rows" and (k[1] % SPK == SPK - 1 or k[1] == KYG - 1):
                        spectrum(k[0], k[1] // SPK)
                mixed()
                turn.wait(cw_set, 1)
                for stage, u in INVERSE:
                    if stage == "turn_back":
                        turned_back(u)
                    elif stage == "inverse":
                        activated(u)

            with act.Fori(0, PASSES) as p:
                layer(True)
                turn.next()
                with act.Fori(1, LAYERS) as l:
                    layer(False)
                    turn.next()
                    cols.next()
                for k in range(NF):
                    passes.wait(fc1_full, k + 1)
                    if k >= 2 * FB and k % FB == 0:
                        passes.wait(fc2_full, k // FB - 1)
                    nc.scalar.activation(FH[:, k % (2 * FB), :], PS[4 + k % 4][:, :], ACT.Gelu, bias=B1[:, 0:1]
                                         ).then_inc(fc1_ready.sem, 1)
                passes.next()
            tail_scalar(act)

        @block.vector
        def _(dve):
            for i in range(8):
                z = nc.vector.memset(PS[i], 0.0)
            z.then_inc(zeroed, 1)
            nc.vector.memset(SW[:], 0.0).then_inc(zeroed, 1)
            dve.sem_inc(credits, 1)
            dve.sem_inc(pass_done.sem, 1)
            dve.sem_inc(xt_ready.sem(0), 1)
            dve.sem_inc(tr_ready.sem(0), 1)
            dve.sem_inc(g_ready.sem, g_ready.credit)
            dve.wait_ge(consts, 16 * CONST_LOADS)

            def columns_out(j, q, dst):
                nc.vector.tensor_copy(dst[:, :, 8 * q:8 * q + 8],
                                      t1_bank[j % 2][:, 0:8 * KOUT].rearrange("p (h k) -> p k h", k=KOUT)
                                      ).then_inc(t1_ready.sem, 1)

            for j in range(N_XT + 1):
                if j < N_XT and j % 2 == 0:
                    dve.wait_ge(xt_full.sem, j + 1)
                    if j >= 2:
                        dve.wait_ge(t1_full.sem, 2 + j - 1)
                    nc.vector.tensor_copy(XT[:, 0, :], xt_bank[0][:, :]).then_inc(xt_ready.sem(0), 1)
                if j:
                    dve.wait_ge(t1_full.sem, 2 + j)
                    columns_out(j - 1, j - 1, T1C)
            turn, cols, passes = Turns(dve, "layer", LAYER_COUNTS), Turns(dve, "cols", COLUMN_COUNTS), Turns(dve, "pass", PASS_COUNTS)

            def fc0_out(m):
                passes.wait(x0_full, m + 1)
                q, n = m // NG, m % NG
                nc.vector.tensor_copy(X[:, n, q * BANK:(q + 1) * BANK], xt_bank[m % 2][:, :]).then_inc(x0_ready.sem(0), 1)

            def transposed(k):
                cols.wait(xt_full, k + 1)
                cols.wait(t1_full, k - 1)
                nc.vector.tensor_copy(XT[:, 0, :], xt_bank[0][:, :]).then_inc(xt_ready.sem(0), 1)

            def transformed(k):
                n, q = k // N_XT, k % N_XT
                cols.wait(t1_full, k + 1)
                if q == 0:
                    turn.wait(tr_full, (n - 1) * N_TR)
                columns_out(k, q, T1[:, n % 2])

            def turned(n, j):
                m = n * N_TR + j
                turn.wait(tr_full, m + 1)
                turn.wait(sp_full, (n - 1) * N_F)
                nc.vector.tensor_copy(TR[:, n % 2, :, 4 * j:4 * j + 4, :].rearrange("p b k c -> p k b c"),
                                      tr_bank[m % 2][:, :].rearrange("p (k b c) -> p k b c", k=4, b=B4)
                                      ).then_inc(tr_ready.sem(0), 1)

            def inverse_rows_out(n, j):
                m = n * N_G + j
                turn.wait(g_full, m + 1)
                if j == 0 and n >= 2:
                    turn.wait(gt_full, (n - 1) * N_X)
                nc.vector.tensor_copy(G[:, n % 2, :, 4 * j:4 * j + 4], g_bank[m % 2][:, :].rearrange("p (k r) -> p r k", k=4)
                                      ).then_inc(g_ready.sem, 1)

            def layer(l, first):
                for stage, k in FIRST_FORWARD if first else FORWARD:
                    if stage == "transpose" and k % 2 == 0:
                        fc0_out(k) if first else transposed(k)
                    elif stage == "columns" and not first:
                        transformed(k)
                    elif stage == "turn" and (k[0] * N_TR + k[1]) % 2 == 0:
                        turned(*k)
                turn.wait(x_ready, 0)
                nc.vector.tensor_copy(CW[:], CWALL[:, bass.ds(l, 1), :].rearrange("p o n -> p (o n)")).then_inc(cw_set.sem, 1)
                for stage, k in INVERSE:
                    if stage == "modes":
                        inverse_rows_out(*k)

            with dve.Fori(0, PASSES) as p:
                layer(0, True)
                turn.next()
                with dve.Fori(1, LAYERS) as l:
                    layer(l, False)
                    turn.next()
                    cols.next()
                turn.wait(gt_full, 0)
                for m in range(NP // 2):
                    if m % 4 == 0 and m:
                        passes.wait(ho_out, m // 4)
                    passes.wait(fc2_full, m + 1)
                    nc.vector.tensor_scalar(HO[:, m % 4, :], PS[m % 2], B2[:, 0:1], None, ALU.add
                                            ).then_inc(fc2_ready.sem, 1)
                passes.wait(ho_out, NG)
                dve.sem_inc(pass_done.sem, 1)
                passes.next()
            tail_vector(dve)

        @block.gpsimd
        def _(pool):
            tail_pool(pool)


def constants():
    import numpy as np
    w = np.arange(GRID)
    k = np.arange(MODES)
    th = 2 * np.pi * np.outer(w, k) / GRID
    cos, sin = np.cos(th) / 8, np.sin(th) / 8
    fw = np.stack([cos, -sin], 2).reshape(GRID, KOUT)
    dft_w = np.zeros((H2, GRID, H2, KOUT))
    for i in range(H2):
        dft_w[i, :, i] = fw
    dft_h = np.zeros((RI, GRID, MODES, RI))
    dft_h[0, :, :, 0], dft_h[1, :, :, 0] = cos, sin
    dft_h[0, :, :, 1], dft_h[1, :, :, 1] = -sin, cos
    idft_h = np.zeros((MODES, RI, GRID, RI))
    idft_h[:, 0, :, 0], idft_h[:, 1, :, 0] = cos.T, -sin.T
    idft_h[:, 0, :, 1], idft_h[:, 1, :, 1] = sin.T, cos.T
    twice = np.where(k == 0, 1.0, 2.0)[:, None]
    bw = np.stack([twice * cos.T, -twice * sin.T], 0).reshape(KOUT, GRID)
    idft_w = np.zeros((H2, KOUT, H2, GRID))
    for i in range(H2):
        idft_w[i, :, i] = bw
    f = np.float32
    band = (np.abs(np.subtract.outer(np.arange(TOK), np.arange(TOK))) <= RADIUS).astype(f)
    return {
        "dft_w": dft_w.reshape(128, H2 * KOUT).astype(f), "dft_h": dft_h.reshape(128, KOUT).astype(f),
        "idft_h": idft_h.reshape(KOUT, GRID * RI).astype(f),
        "head_mask": np.kron(np.eye(HEADS, dtype=f), np.ones((HD, 1), f)),
        "band": band, "band4": np.tile(band * f(HD ** -0.5), (1, 4)),
        "sel": np.repeat(np.eye(EXPERTS, dtype=f), GRID, 1).reshape(EXPERTS, EXPERTS // 2, 128),
        "idft_w": idft_w.reshape(H2 * KOUT, H2 * GRID).astype(f), "ident": np.eye(128, dtype=f),
    }


def block_diagonal(w, n):
    import numpy as np
    k, m = w.shape
    out = np.zeros((n * k, n * m), w.dtype)
    for i in range(n):
        out[i * k:(i + 1) * k, i * m:(i + 1) * m] = w
    return out


def layout(inputs):
    import numpy as np
    a = {k: np.asarray(v) for k, v in inputs.items()}
    tok = {k[len("L0_tok_"):]: v for k, v in a.items() if k.startswith("L0_tok_")}
    d = constants()
    xa = np.ones((NIMG, 4, PIX), np.float32)
    xa[:, 0:3] = a["x"].reshape(NIMG, PIX, 3).transpose(0, 2, 1)
    d["xall"] = xa.reshape(128, PIX)
    w0a = np.zeros((NIMG, 4, NIMG // B4, B4, CH), np.float32)
    for b in range(NIMG):
        w0a[b, 0:3, b // B4, b % B4], w0a[b, 3, b // B4, b % B4] = tok["fc0_w"], tok["fc0_b"]
    d["fc0_all"] = w0a.reshape(128, NIMG // B4, 128)
    sw = np.stack([tok[f"sw{i}"] for i in range(LAYERS)])
    sw = sw.reshape(LAYERS, CH, CH, KXD, B4, KYG, B4)
    d["spec_w"] = sw.transpose(0, 3, 6, 1, 4, 5, 2).reshape(LAYERS, KXD, B4, CH, B4 * KYG * CH)
    d["conv_wb"] = np.stack([np.concatenate([block_diagonal(tok[f"cw{i}"].T, B4), np.tile(tok[f"cb{i}"], B4)[:, None]], 1)
                             for i in range(LAYERS)], 1)
    w1 = np.zeros((2, 2, CH, 2, 2, FC), np.float32)
    for pr in range(2):
        for b in range(2):
            w1[pr, b, :, pr, b] = tok["fc1_w"]
    d["fc1_w"] = w1.reshape(128, 2, 128)
    d["fc1_b"] = np.tile(tok["fc1_b"], 2)[:, None]
    w2 = np.zeros((128, CH), np.float32)
    w2[0:FC, 0], w2[FC:128, 1] = tok["fc2_w"][:, 0], tok["fc2_w"][:, 0]
    d["fc2_w"] = w2
    d["fc2_b"] = np.repeat(tok["fc2_b"], 128)[:, None]
    att = {k[len("L0_attn_"):]: v for k, v in a.items() if k.startswith("L0_attn_")}
    ffn = {k[len("L0_ffn_"):]: v for k, v in a.items() if k.startswith("L0_ffn_")}
    d["w_qkv"], d["w_proj"] = att["w_qkv"], att["w_proj"]
    d["b_qk"] = att["b_qkv"][0:2 * GRID].reshape(2, GRID).T
    every = lambda v: np.tile(v, (TOK, 1))
    d["b_v"], d["b_proj"] = every(att["b_qkv"][2 * GRID:]), every(att["b_proj"])
    d["gate_w"], d["out_w"] = ffn["gate_w"].T, ffn["out_w"].T
    d["w_expert"] = ffn["lattice_weights"].reshape(EXPERTS // 2, 128, GRID).transpose(1, 0, 2)
    d["out_b"], d["ln_g"], d["ln_b"] = every(ffn["out_b"]), every(ffn["ln_g"]), every(ffn["ln_b"])
    d["cls_rows"] = np.tile(a["cls_tok"].reshape(1, 1, GRID), (1, NIMG, 1))
    return {k: np.ascontiguousarray(v) for k, v in d.items()}


INS = ["xall", "fc0_all", "spec_w", "conv_wb", "fc1_w", "fc1_b", "fc2_w", "fc2_b",
       "w_qkv", "b_qk", "b_v", "w_proj", "b_proj", "gate_w", "w_expert", "out_w", "out_b", "ln_g", "ln_b", "cls_rows",
       "head_mask", "band", "band4", "sel", "dft_w", "dft_h", "idft_h", "idft_w", "ident"]


def program(nc, arrays):
    args = [nc.dram_tensor(f"in_{n}", arrays[n].shape, F32, kind="ExternalInput").ap() for n in INS]
    args.append(nc.dram_tensor("spec_scr", (MODES, RI, GIMG, MODES * CH), F32).ap())
    args.append(nc.dram_tensor("hid_scr", (PASSES, NG, 2, 2, PIX), F32).ap())
    args.append(nc.dram_tensor("out", (NIMG, TOK, GRID), F32, kind="ExternalOutput").ap())
    vit_kernel(nc, *args)


def kernel(**inputs):
    import concourse.bacc as bacc
    from concourse.bass_utils import run_bass_kernel_spmd
    nc = bacc.Bacc("TRN2", target_bir_lowering=False, num_devices=1)
    arrays = layout(inputs)
    program(nc, arrays)
    r = run_bass_kernel_spmd(nc, [{f"in_{n}": arrays[n] for n in INS}], core_ids=[0])
    return r.results[0]["out"]
```

```python
from contextlib import ExitStack

import concourse.bass as bass
from concourse import mybir

NIMG, GRID, CH, MODES, LAYERS = 32, 64, 32, 20, 4
FC = 64
RI = 2
B4 = 4
NG = 4
GIMG = B4 * NG
PASSES = NIMG // GIMG
H2 = 2
HH = GRID // H2
PIX = GRID * GRID
BANK = 512
KYG = MODES // B4
KXD = MODES // B4
MIXB = KYG * KXD
KOUT = RI * MODES

N_XT = PIX // BANK
N_TR = MODES // B4
SPK = 3
N_F = -(-KYG // SPK)
N_MIX = (MIXB + 3) // 4
N_G = MODES // B4
N_X = PIX // BANK

AHEAD = 2
RING = 3
SLOT = [0, 1, 2, RING, 0]
CLEARS = 4
PARTS = [(0, 3), (3, KYG)]
FB = 4

TOK = GRID + 1
HEADS, HD = 8, 8
EXPERTS, TOPK = 64, 6
RADIUS = 32
EPS = 1e-5
NT = NIMG * TOK
BC = 4
NC = NIMG // BC
CT = BC * TOK
NZ = 5
ZT = NT // NZ
VH = HD + 1
LW = EXPERTS + 2
SENTINEL = -3.0e38
LB = 8
LK = NIMG // LB
PAIRS = EXPERTS // 2
PROJECT_AT = [(k + 2) * PAIRS + 8 + 2 * i for k in range(LK - 1) for i in range(LB // BC)]
ADD_AT = [n + 2 for n in PROJECT_AT]
CENTRE_AT = [(k + 2) * PAIRS + 14 for k in range(LK - 1)]
FINISH_AT = [(k + 2) * PAIRS + 20 for k in range(LK - 1)]
ZR = 6
LN_STEP = 13
SELECTED = EXPERTS // 8
LAG = 3
TAIL_LOADS = 13
CONST_LOADS = 9

F32, BF16 = mybir.dt.float32, mybir.dt.bfloat16
ALU = mybir.AluOpType
ACT = mybir.ActivationFunctionType
AX = mybir.AxisListType


class Count:

    def __init__(self, sem, per_turn, unit=1, credit=0):
        self.sem, self.stride, self.unit, self.credit = sem, per_turn * unit, unit, credit


class Halves:

    def __init__(self, v, a, per_turn, credit=0):
        self.counts = [Count(v, per_turn // 2, credit=credit), Count(a, per_turn // 2, credit=credit)]

    def sem(self, n):
        return self.counts[n % 2].sem


class Turns:

    def __init__(self, eng, name, counts):
        self.eng, self.strides = eng, sorted({c.stride for c in counts})
        self.base = {n: eng.alloc_register(f"{name}_{n}") for n in self.strides}
        self.value = eng.alloc_register(f"{name}_value")
        self.second = eng.alloc_register(f"{name}_second")
        for r in self.base.values():
            eng.reg_mov(r, 0)

    def wait(self, count, done):
        self.eng.reg_add(self.value, self.base[count.stride], done * count.unit + count.credit)
        self.eng.wait_ge(count.sem, self.value)

    def wait_both(self, count, done, other, other_done):
        self.eng.reg_add(self.value, self.base[count.stride], done * count.unit + count.credit)
        self.eng.reg_add(self.second, self.base[other.stride], other_done * other.unit + other.credit)
        self.eng.wait_ge(count.sem, self.value)
        self.eng.wait_ge(other.sem, self.second)

    def wait_job(self, halves, n):
        self.wait(halves.counts[n % 2], n // 2 + 1)

    def wait_jobs(self, halves, n):
        self.wait_both(halves.counts[0], (n + 1) // 2, halves.counts[1], n // 2)

    def next(self):
        for n in self.strides:
            self.eng.reg_add(self.base[n], self.base[n], n)


def forward_steps(first):
    steps = []
    banks, step, lead = (0, N_TR, 0) if first else (NG * N_XT, N_XT, N_XT)
    for k in range(NG * step + lead + 3):
        if k < banks:
            steps.append(("transpose", k))
        if 2 <= k < banks + 2:
            steps.append(("columns", k - 2))
        for stage, delay in (("turn", lead and 2), ("rows", lead and 5 or 2)):
            n, j = divmod(k - lead - delay, step)
            if 0 <= n < NG and j < N_TR:
                steps.append((stage, (n, j)))
        j = k - (NG - 1) * step - lead + 2 if lead else k - (NG - 1) * step - 2
        if 0 <= j < CLEARS:
            steps.append(("clear", j))
    return steps


def inverse_steps():
    steps = [("pointwise", u) for u in range(AHEAD)] + [("modes", (0, j)) for j in range(N_G)]
    for u in range(NG * N_X + 1):
        if u < NG * N_X:
            steps.append(("turn_back", u))
        if u:
            steps.append(("inverse", u - 1))
        n, j = divmod(u - 2, N_X)
        if u >= 2 and n + 1 < NG and 0 <= j < N_G:
            steps.append(("modes", (n + 1, j)))
        if AHEAD <= u + 2 < NG * N_X:
            steps.append(("pointwise", u + 2))
    return steps


FIRST_FORWARD, FORWARD, INVERSE = forward_steps(True), forward_steps(False), inverse_steps()


def vit_kernel(nc, xall, fc0_all, fc0_t, spec_w, conv_wb, fc1_w, fc1_b, fc2_w, fc2_b,
               w_qkv, b_qk, b_v, w_proj, b_proj, gate_w, w_expert, out_w, out_b, ln_g, ln_b, cls_rows,
               head_mask, outside, band4, dft_w, dft_h, idft_h, idft_w, ident_in,
               spec_scr, hid_scr, out):
    ctx = ExitStack()
    with ctx:
        def sb(name, shape, dt=F32):
            return ctx.enter_context(nc.sbuf_tensor(name, shape, dt))

        def sem(name):
            return ctx.enter_context(nc.semaphore(name))

        X = sb("X", [128, NG, PIX])
        XT = sb("XT", [128, 2, BANK])
        T1 = sb("T1", [128, 2, KOUT, GRID])
        T1C = sb("T1C", [128, KOUT, GRID])
        TR = sb("TR", [128, 2, B4, MODES, CH])
        SPEC = sb("SPEC", [128, KYG, MODES, RI * GIMG])
        SW = sb("SW", [128, RING, B4, MODES * CH])
        MIXED = sb("MIXED", [128, MIXB * 128])
        spec_mem = SPEC[:].rearrange("p a b c -> p (a b c)")
        pieces = [SW[:, i] for i in range(RING)] + [T1[:, 0].rearrange("p a b -> p (a b)").rearrange("p (j n) -> p j n", j=B4)]
        MODE = spec_mem[:, 0:MODES * B4 * CH].rearrange("p (y n) -> p y n", y=MODES)
        G = T1[:].rearrange("p s a b -> p s (a b)").rearrange("p s (h k) -> p s h k", k=MODES)
        GT = TR[:, 0].rearrange("p a b c -> p (a b c)")[0:H2 * KOUT, 0:4 * 4 * 128].rearrange("p (s h n) -> p s h n", s=4, h=4)
        DW = sb("DW", [128, H2 * KOUT])
        DH = sb("DH", [128, KOUT])
        EH = sb("EH", [128, GRID * RI])
        EW = sb("EW", [H2 * KOUT, H2 * GRID])
        ident = sb("ident", [128, 128])
        CWALL = sb("CWALL", [128, LAYERS, 129])
        CW = sb("CW", [128, 129])
        W0 = sb("W0", [128, NG, 128])
        W0T, W0C = XT[:, 0].rearrange("p (n k) -> p n k", n=NG), XT[:, 1].rearrange("p (n k) -> p n k", n=NG)
        W1 = sb("W1", [128, 2, 128])
        B1 = sb("B1", [128, 1])
        W2 = sb("W2", [128, CH])
        B2 = sb("B2", [128, 1])
        WQKV, WP = sb("WQKV", [GRID, 3 * GRID]), sb("WP", [GRID, GRID])
        BQK, BV, BP = sb("BQK", [GRID, 2]), sb("BV", [TOK, GRID]), sb("BP", [TOK, GRID])
        GATE, WO, OB = sb("GATE", [GRID, EXPERTS]), sb("WO", [128, GRID]), sb("OB", [TOK, GRID])
        LNG, LNB = sb("LNG", [TOK, GRID]), sb("LNB", [TOK, GRID])
        HM = sb("HM", [GRID, HEADS])
        OUTSIDE = sb("OUTSIDE", [TOK, TOK])
        BAND4 = sb("BAND4", [TOK, 4 * TOK])
        XALL = X[:, NG - 1, :]
        FH = TR[:].rearrange("p r a b c -> p (r a b c)")[:, 0:2 * FB * BANK].rearrange("p (r n) -> p r n", n=BANK)
        HO = T1[:, 0].rearrange("p a b -> p (a b)")[:, 0:4 * BANK].rearrange("p (a b) -> p a b", a=4)

        PSALL = ctx.enter_context(nc.psum_tensor("PSALL", [128, 8, BANK], F32))
        PS = [PSALL[:, i, :] for i in range(8)]

        xt_bank, t1_bank, tr_bank, sp_bank = PS[0:2], PS[2:4], PS[4:6], PS[6:8]
        mix_bank, g_bank, gt_bank, x_bank = PS[2:4], PS[6:8], PS[4:6], PS[0:4]

        first_consts, consts = sem("identity_and_columns_dft_loaded"), sem("consts_loaded")
        psum_zeroed, ring_zeroed = sem("psum_zeroed"), sem("weights_ring_zeroed")
        credits = sem("credits_given")
        NP = NG * N_X
        NF = 2 * NP
        xt_full = Count(sem("xt_full"), NP, credit=N_XT)
        xt_ready = Halves(sem("xt_ready_v"), sem("xt_ready_a"), NP, credit=1 + N_XT // 2)
        t1_full, t1_ready = Count(sem("t1_full"), NP, credit=2 + N_XT), Count(sem("t1_ready"), NP, credit=N_XT)
        tr_full, tr_ready = Count(sem("tr_full"), NG * N_TR, credit=2 * N_TR), Halves(sem("tr_ready_v"), sem("tr_ready_a"), NG * N_TR, credit=1)
        sp_full, sp_ready = Count(sem("sp_full"), NG * N_F, credit=2 * N_F), Count(sem("sp_ready"), NG * N_F)
        mix_full, mix_ready = Count(sem("mix_full"), N_MIX), Count(sem("mix_ready"), N_MIX)
        piece_used = Count(sem("weights_piece_used"), KYG, credit=KYG - 1)
        g_full, g_ready = Count(sem("g_full"), NG * N_G), Count(sem("g_ready"), NG * N_G, credit=2)
        gt_full, gt_ready = Count(sem("gt_full"), NP, credit=1), Count(sem("gt_ready"), NP, credit=2)
        x_full, x_ready = Count(sem("x_full"), NP, credit=4), Count(sem("x_ready"), NP, credit=4)
        piece_in = [Count(sem(f"weights_piece_loaded{i}"), SLOT.count(i), unit=64) for i in range(RING + 1)]
        cleared = Count(sem("last_slot_cleared"), CLEARS)
        stored = [Count(sem(f"spectrum_stored{i}"), 1, unit=16 * (b - a), credit=1) for i, (a, b) in enumerate(PARTS)]
        loaded_first = [Count(sem(f"first_modes_loaded{i}"), 1, unit=64) for i in range(len(PARTS))]
        loaded = [None] + [Count(sem(f"modes_loaded{g}"), 1, unit=64) for g in range(1, NG)]
        cw_set = Count(sem("layer_weights_set"), 1)
        fc1_full, fc1_ready = Count(sem("fc1_full"), NF), Count(sem("fc1_ready"), NF)
        fc2_full, fc2_ready = Count(sem("fc2_full"), NP // 2), Count(sem("fc2_ready"), NP // 2)
        ho_out = Count(sem("hidden_stored"), NG, unit=64)
        co_in = Count(sem("coords_loaded"), 1, unit=16)
        w0_in, w0t_in = Count(sem("fc0_loaded"), 1, unit=16), Count(sem("fc0_transposed_loaded"), 1, unit=16)
        w0c_full, w0c_ready = Count(sem("fc0_pointwise_full"), 1), Count(sem("fc0_pointwise_ready"), 1)
        pass_done = Count(sem("pass_done"), 1)
        input_in = [sem(f"input_half_loaded{i}") for i in range(2)]
        COLUMN_COUNTS = [xt_full, t1_full, t1_ready] + xt_ready.counts
        LAYER_COUNTS = [tr_full, sp_full, sp_ready, mix_full, mix_ready, piece_used, g_full, g_ready, gt_full, gt_ready,
                        x_full, x_ready, cw_set, cleared] + tr_ready.counts + stored + loaded_first + loaded[1:] + piece_in
        PASS_COUNTS = [w0c_full, w0c_ready, co_in, fc1_full, fc1_ready, fc2_full, fc2_ready, ho_out, pass_done, w0_in, w0t_in]

        arena = X[:].rearrange("p g n -> p (g n)")
        H = arena[0:TOK, 0:2048].rearrange("p (b d) -> p b d", b=NIMG)
        Y = arena[0:TOK, 2048:6144].rearrange("p (b t d) -> p b t d", b=NIMG, t=2)
        TMP = arena[0:TOK, 6144:8192].rearrange("p (b d) -> p b d", b=NIMG)
        YT = arena[:, 8192:8192 + NT]
        QT = arena[0:GRID, 10272:10272 + NT]
        KT = arena[0:GRID, 12352:12352 + NT]
        V = T1[0:TOK, 0].rearrange("p a b -> p (a b)")[:, 0:NIMG * HEADS * VH].rearrange("p (b h e) -> p b h e", b=NIMG, h=HEADS)
        O = T1[0:TOK, 1].rearrange("p a b -> p (a b)")[:, 0:2048].rearrange("p (b d) -> p b d", b=NIMG)
        modes_mem = TR[:].rearrange("p r a b c -> p (r a b c)")
        KM = modes_mem[0:GRID, 0:2 * HEADS * CT].rearrange("p (r h t) -> p r h t", r=2, h=HEADS)
        sw_mem = SW[:].rearrange("p a b c -> p (a b c)")
        HT = HEADS * TOK
        PR = sw_mem[0:TOK, 0:4 * HT].rearrange("p (r h t) -> p r h t", r=4, h=HEADS)
        PT = sw_mem[0:TOK, 4 * HT:6 * HT].rearrange("p (r h t) -> p r h t", r=2, h=HEADS)
        NV = TMP
        OT = MIXED[0:GRID, 0:2 * CT].rearrange("p (r t) -> p r t", r=2)
        LG = arena[0:TOK, 12352:12352 + NIMG * LW].rearrange("p (b e) -> p b e", b=NIMG)
        LR = MIXED[0:TOK, 0:NIMG * LW].rearrange("p (b e) -> p b e", b=NIMG)
        SC = arena[0:TOK, 10272:10272 + NIMG * EXPERTS].rearrange("p (b e) -> p b e", b=NIMG)
        SC2 = T1[0:TOK].rearrange("p s a b -> p (s a b)")[:, 0:2 * NIMG * EXPERTS].rearrange("p (b t e) -> p b t e", b=NIMG, t=2)
        ZX = modes_mem[:, NT:NT + ZR * ZT].rearrange("p (r t) -> p r t", r=ZR)
        LT = modes_mem[:, 0:NT]
        SHM = sw_mem[:, 0:NT // 2].bitcast(BF16)
        SLO = sw_mem[0:EXPERTS, NT // 2:NT].bitcast(BF16)
        REST = sw_mem[:, 6 * HT + 2048:6 * HT + 2048 + NT]
        WE = spec_mem[:, 0:EXPERTS // 2 * GRID].rearrange("p (e d) -> p e d", d=GRID)
        SEL = sw_mem[:, 6 * HT:6 * HT + 2048].bitcast(BF16).rearrange("p (e n) -> p e n", n=128)
        SQ = T1[0:TOK].rearrange("p s a b -> p (s a b)")[:, 0:NIMG * GRID].rearrange("p (b d) -> p b d", b=NIMG)
        M8 = spec_mem[0:TOK, MODES * B4 * CH:MODES * B4 * CH + NIMG * 8].rearrange("p (b e) -> p b e", b=NIMG)

        smx = sb("smx", [TOK, NIMG, HEADS])
        emx = sb("emx", [TOK, NIMG, HEADS])
        rden = sb("rden", [TOK, NIMG, HEADS])
        st = sb("st", [TOK, 4, NIMG])

        h_in, last_h_in, tail_w = sem("tokens_loaded"), sem("last_tokens_loaded"), sem("tail_weights_loaded")
        hidden_tokens = hid_scr.rearrange("p g r b (h w) -> h (p g r b) w", w=GRID)
        we_in, sel_ready = sem("expert_weights_loaded"), sem("selector_ready")
        nv_full, nv_ready, em_ready, nw_ready = sem("outside_full"), sem("outside_ready"), sem("exp_max_ready"), sem("outside_weighed")
        ones_set = sem("ones_set")
        high_ready, rest_ready, mid_ready, lo_ready = sem("high_ready"), sem("rest_ready"), sem("middle_ready"), sem("low_ready")
        dve_step = sem("dve_step")
        var_ready, dev_ready = sem("variance_ready"), sem("deviation_ready")
        centred, squared, y_ready = sem("centred"), sem("squared"), sem("layernorm_ready")
        hb_ready, hl_ready, ob_ready = sem("residual_and_bias_ready"), sem("residual_and_shift_ready"), sem("output_bias_ready")
        chosen, weighed, ln_ready, scaled = sem("chosen"), sem("chosen_weighed"), sem("last_layernorm_ready"), sem("last_scaled")
        yt_full, yt_ready = sem("yt_full"), sem("yt_ready")
        q_full, q_ready = sem("q_full"), sem("q_ready")
        k_full, k_ready = sem("k_full"), sem("k_ready")
        v_full, v_ready = sem("v_full"), sem("v_ready")
        km_ready, s_full, s_ready = sem("masked_keys_ready"), sem("scores_full"), sem("scores_ready")
        max_ready, sub_ready, exp_ready = sem("max_ready"), sem("shifted_ready"), sem("exp_ready")
        pt_full, pt_ready = sem("pt_full"), sem("pt_ready")
        o_full, o_ready = sem("o_full"), sem("o_ready")
        ot_full, ot_ready = sem("ot_full"), sem("ot_ready")
        pj_full, pj_ready = sem("projected_full"), sem("projected_ready")
        lg_full, lg_ready = sem("logits_full"), sem("logits_ready")
        le_ready, lx_ready, sc_ready = sem("shifted_logits_ready"), sem("exp_logits_ready"), sem("expert_scores_ready")
        st_full, lo_copied = sem("st_full"), sem("low_rest_copied")
        bc_full, zx_ready, zx_used = sem("broadcast_full"), sem("zx_ready"), sem("zx_used")
        lt_full, lt_ready = sem("lt_full"), sem("lt_ready")
        f_full, f_ready = sem("ffn_full"), sem("ffn_ready")
        out_ready, last_ready, out_stored = sem("out_ready"), sem("last_chunk_ready"), sem("out_stored")

        SPR = [PSALL[:, 2 * i:2 * i + 2, 0:4 * TOK] for i in range(2)]
        PTP = PSALL[:, 4:6, 0:4 * TOK]

        def tail_sync(sp):
            sp.dma_start(H[1:TOK, NIMG - B4:], hidden_tokens[:, NIMG - B4:]).then_inc(last_h_in, 16)
            sp.dma_start(WE, w_expert).then_inc(we_in, 16)
            for k in range(LK):
                a = slice(k * LB, (k + 1) * LB)
                if k < LK - 1:
                    sp.wait_ge(out_ready, k + 1)
                else:
                    sp.wait_ge(last_ready, 1)
                sp.dma_start(out.rearrange("b t d -> t b d")[:, a], TMP[:, a]).then_inc(out_stored, 16)
            sp.wait_ge(out_stored, 16 * LK)

        def tail_tensor(pe):
            pe.wait_ge(tail_w, 16 * TAIL_LOADS)

            def transposes(c, src, width, dst, full):
                for i in range(BC):
                    m = pe.transpose(dst[0:width, i * TOK:(i + 1) * TOK], src(c * BC + i), ident[0:TOK, 0:TOK])
                m.then_inc(full, 1)

            def qkv(c):
                pe.wait_ge(yt_ready, c + 1)
                x = YT[0:GRID, c * CT:(c + 1) * CT]
                if c:
                    pe.wait_ge(q_ready, c)
                pe.matmul(PS[2][0:GRID, 0:CT], WQKV[:, 0:GRID], x, start=True, stop=True).then_inc(q_full, 1)
                if c:
                    pe.wait_ge(k_ready, c)
                pe.matmul(PS[3][0:GRID, 0:CT], WQKV[:, GRID:2 * GRID], x, start=True, stop=True).then_inc(k_full, 1)
                if c:
                    pe.wait_ge(v_ready, c)
                for i in range(BC):
                    b = c * BC + i
                    m = pe.matmul(PS[4][0:TOK, i * GRID:(i + 1) * GRID], YT[0:GRID, b * TOK:(b + 1) * TOK],
                                  WQKV[:, 2 * GRID:3 * GRID], start=True, stop=True)
                m.then_inc(v_full, 1)

            def outside_sums(c):
                pe.wait_ge(v_ready, c + 1)
                if c >= 2:
                    pe.wait_ge(nv_ready, c - 1)
                pe.matmul(PS[5 + c % 2][0:TOK, 0:BC * GRID].rearrange("p (b h e) -> p b h e", b=BC, h=HEADS), OUTSIDE[:],
                          V[:, c * BC:(c + 1) * BC, :, 0:HD], start=True, stop=True).then_inc(nv_full, 1)

            for c in range(NC + 2):
                if c < NC:
                    pe.wait_ge(y_ready, c * BC // LB + 1)
                    if c >= 2:
                        pe.wait_ge(yt_ready, c - 1)
                    transposes(c, lambda b: Y[:, b, 0, :], GRID, PS[c % 2], yt_full)
                if 1 <= c <= NC:
                    qkv(c - 1)
                if c >= 2:
                    outside_sums(c - 2)

            def scores(b):
                if b == 0:
                    pe.wait_ge(q_ready, NC)
                    pe.wait_ge(k_ready, NC)
                    pe.wait_ge(v_ready, NC)
                    pe.wait_ge(yt_ready, NC)
                    pe.wait_ge(nv_ready, NC)
                    pe.wait_ge(ones_set, 1)
                if b % BC == 0:
                    pe.wait_ge(km_ready, HEADS * (b // BC + 1))
                if b >= 2:
                    pe.wait_ge(s_ready, b - 1)
                for hf in range(2):
                    m = pe.matmul(SPR[b % 2][0:TOK, hf, :], QT[:, b * TOK:(b + 1) * TOK],
                                  KM[:, b // BC % 2, 4 * hf:4 * hf + 4, b % BC * TOK:(b % BC + 1) * TOK],
                                  start=True, stop=True)
                m.then_inc(s_full, 1)

            def turn_probs(b):
                pe.wait_ge(exp_ready, b + 1)
                if b:
                    pe.wait_ge(pt_ready, b)
                for h in range(HEADS):
                    m = pe.transpose(PTP[0:TOK, h // 4, h % 4 * TOK:(h % 4 + 1) * TOK], PR[:, b % 4, h, :],
                                     ident[0:TOK, 0:TOK])
                m.then_inc(pt_full, 1)

            def values(b):
                pe.wait_ge(pt_ready, b + 1)
                if b % BC == 0 and b:
                    pe.wait_ge(o_ready, b // BC)
                for h in range(HEADS):
                    m = pe.matmul(PS[6][0:TOK, (b % BC * HEADS + h) * VH:(b % BC * HEADS + h + 1) * VH], PT[:, b % 2, h, :],
                                  V[:, b, h, :], start=True, stop=True)
                m.then_inc(o_full, 1)

            def turn_attended(c):
                pe.wait_ge(o_ready, c + 1)
                if c:
                    pe.wait_ge(pj_ready, c)
                transposes(c, lambda b: O[:, b, :], GRID, PS[7], ot_full)

            def project(c):
                pe.wait_ge(ot_ready, c + 1)
                for i in range(BC):
                    m = pe.matmul(PS[7][0:TOK, i * GRID:(i + 1) * GRID], OT[:, c % 2, i * TOK:(i + 1) * TOK], WP[:],
                                  start=True, stop=True)
                m.then_inc(pj_full, 1)

            for i in range(NIMG + LAG + 3):
                if i < NIMG:
                    scores(i)
                if LAG <= i < NIMG + LAG:
                    turn_probs(i - LAG)
                if i >= LAG + 1 and i - LAG - 1 < NIMG:
                    values(i - LAG - 1)
                if i > LAG + 2 and (i - LAG - 3) % BC == BC - 1:
                    project((i - LAG - 3) // BC)
                if i > LAG + 1 and (i - LAG - 2) % BC == BC - 1:
                    turn_attended((i - LAG - 2) // BC)

            for c in range(NC + 1):
                if c < NC:
                    pe.wait_ge(y_ready, LK + c * BC // LB + 1)
                    if c >= 2:
                        pe.wait_ge(yt_ready, NC + c - 1)
                    transposes(c, lambda b: Y[:, b].rearrange("p t d -> p (t d)"), 128, PS[c % 2], yt_full)
                if c:
                    pe.wait_ge(yt_ready, NC + c)
                    if c >= 3:
                        pe.wait_ge(lg_ready, c - 2)
                    for i in range(BC):
                        b = (c - 1) * BC + i
                        m = pe.matmul(PS[2 + (c - 1) % 2][0:TOK, i * EXPERTS:(i + 1) * EXPERTS],
                                      YT[0:GRID, b * TOK:(b + 1) * TOK], GATE[:], start=True, stop=True)
                    m.then_inc(lg_full, 1)
            for c in range(NC):
                pe.wait_ge(sc_ready, c + 1)
                if c >= 2:
                    pe.wait_ge(rest_ready, c - 1)
                transposes(c, lambda b: SC2[:, b].rearrange("p t e -> p (t e)"), 2 * EXPERTS, PS[6 + c % 2], st_full)
            pe.wait_ge(yt_ready, 2 * NC)
            pe.wait_ge(lg_ready, NC)
            pe.wait_ge(we_in, 16)
            pe.wait_ge(sel_ready, 2 * SELECTED)
            def broadcast(n):
                z, ep = n // PAIRS, n % PAIRS
                if ep == 0:
                    chunks = -(-(z + 1) * ZT // CT)
                    pe.wait_ge(mid_ready, chunks)
                    pe.wait_ge(lo_ready, chunks)
                if n >= 4:
                    pe.wait_ge(zx_ready, n - 3)
                pe.matmul(PS[n % 4][:, 0:ZT], SEL[:, ep, :], SHM[:, z * ZT:(z + 1) * ZT], start=True, stop=False)
                pe.matmul(PS[n % 4][:, 0:ZT], SEL[0:EXPERTS, ep, :], SLO[:, z * ZT:(z + 1) * ZT],
                          start=False, stop=True).then_inc(bc_full, 1)

            def expert_products(n):
                z, ep = n // PAIRS, n % PAIRS
                pe.wait_ge(zx_ready, n + 2)
                if ep == 0 and z >= 2:
                    pe.wait_ge(lt_ready, z - 1)
                for i in range(2):
                    m = pe.matmul(PS[4 + z % 2][64 * i:64 * i + GRID, 0:ZT], WE[:, ep + i, :], ZX[:, (n + i) % ZR, :],
                                  start=(ep == 0), stop=(ep == PAIRS - 2), tile_position=(0, 64 * i), skip_group_check=True)
                m.then_inc(zx_used, 1)

            def output_projection(c):
                pe.wait_ge(lt_ready, -(-(c + 1) * CT // ZT))
                if c == 0:
                    pe.wait_ge(rest_ready, NC)
                if c >= 2:
                    pe.wait_ge(f_ready, c - 1)
                for i in range(BC):
                    b = c * BC + i
                    m = pe.matmul(PS[6 + c % 2][0:TOK, i * GRID:(i + 1) * GRID], LT[:, b * TOK:(b + 1) * TOK], WO[:],
                                  start=True, stop=True)
                m.then_inc(f_full, 1)

            for n in range(0, NZ * PAIRS + 4, 2):
                if n in PROJECT_AT:
                    output_projection(PROJECT_AT.index(n))
                if n < NZ * PAIRS:
                    broadcast(n)
                    broadcast(n + 1)
                if n >= 4:
                    expert_products(n - 4)
            for c in range(len(PROJECT_AT), NC):
                output_projection(c)

        def tail_scalar(act):
            act.wait_ge(ho_out.sem, (PASSES * NG - 1) * ho_out.stride // NG)
            act.dma_start(H[0:1], cls_rows).then_inc(h_in, 16)
            act.dma_start(H[1:TOK, 0:NIMG - B4], hidden_tokens[:, 0:NIMG - B4]).then_inc(h_in, 16)
            act.wait_ge(tail_w, 16 * TAIL_LOADS)

            def feature_rows(c, rows, done):
                act.wait_ge(yt_full, done + c + 1)
                nc.scalar.copy(YT[0:rows, c * CT:(c + 1) * CT], PS[c % 2][0:rows, 0:CT]).then_inc(yt_ready, 1)

            def deviation(n, k):
                a = slice(k * LB, (k + 1) * LB)
                act.wait_ge(var_ready, n * LK + k + 1)
                nc.scalar.activation(st[:, 2, a], st[:, 1, a], ACT.Sqrt).then_inc(dev_ready, 1)

            deviation(0, 0)
            deviation(0, 1)
            feature_rows(0, GRID, 0)
            for k in range(2, LK):
                deviation(0, k)
            for c in range(NC):
                if c + 1 < NC:
                    feature_rows(c + 1, GRID, 0)
                act.wait_ge(q_full, c + 1)
                nc.scalar.activation(QT[:, c * CT:(c + 1) * CT], PS[2][0:GRID, 0:CT], ACT.Identity, bias=BQK[:, 0:1]
                                     ).then_inc(q_ready, 1)
                act.wait_ge(k_full, c + 1)
                nc.scalar.activation(KT[:, c * CT:(c + 1) * CT], PS[3][0:GRID, 0:CT], ACT.Identity, bias=BQK[:, 1:2]
                                     ).then_inc(k_ready, 1)
                if c:
                    outside_sums_out(act, c - 1)
            outside_sums_out(act, NC - 1)
            act.wait_ge(k_ready, NC)

            def mask_keys(c, heads):
                for h in heads:
                    nc.scalar.activation(KM[:, c % 2, h, :], KT[:, c * CT:(c + 1) * CT], ACT.Copy,
                                         scale=HM[:, h:h + 1]).then_inc(km_ready, 1)

            mask_keys(0, range(HEADS))
            for i in range(LN_STEP + (LK - 1) * LB + 3):
                if i < NIMG - BC:
                    c, r = i // BC, i % BC
                    if r == 0 and c:
                        act.wait_ge(s_full, c * BC)
                    mask_keys(c + 1, range(2 * r, 2 * r + 2))
                if 1 <= i <= NIMG:
                    b = i - 1
                    act.wait_ge(sub_ready, b + 1)
                    nc.scalar.activation(PR[:, b % 4], PR[:, b % 4], ACT.Exp).then_inc(exp_ready, 1)
                    if b % BC == BC - 1:
                        a = slice(b - BC + 1, b + 1)
                        nc.scalar.activation(emx[:, a], smx[:, a], ACT.Exp, scale=-1.0).then_inc(em_ready, 1)
                if i >= LAG and i - LAG < NIMG:
                    b = i - LAG
                    act.wait_ge(pt_full, b + 1)
                    if b >= 2:
                        act.wait_ge(o_full, b - 1)
                    nc.scalar.copy(PT[:, b % 2].rearrange("p (a h) t -> p a (h t)", a=2), PTP[0:TOK]).then_inc(pt_ready, 1)
                if i > LAG + 1 and (i - LAG - 2) % BC == BC - 1:
                    turn_out(act, (i - LAG - 2) // BC)
                if i >= LN_STEP + 2 and (i - LN_STEP - 2) % LB == 0:
                    deviation(1, (i - LN_STEP - 2) // LB)
            def exp_logits(k):
                a = slice(k * LB, (k + 1) * LB)
                act.wait_ge(le_ready, k + 1)
                nc.scalar.activation(SC[:, a], SC[:, a], ACT.Exp).then_inc(lx_ready, 1)

            for c in range(NC + 1):
                if c < NC:
                    feature_rows(c, 128, NC)
                if c:
                    a = slice((c - 1) * BC, c * BC)
                    act.wait_ge(lg_full, c)
                    nc.scalar.copy(LG[:, a, 0:EXPERTS],
                                   PS[2 + (c - 1) % 2][0:TOK, 0:BC * EXPERTS].rearrange("p (b e) -> p b e", b=BC)
                                   ).then_inc(lg_ready, 1)
                if c >= 4 and c % 2 == 0:
                    exp_logits(c // 2 - 2)

            def high_part(c):
                act.wait_ge(st_full, c + 1)
                nc.scalar.copy(SHM[:, c * CT:(c + 1) * CT], PS[6 + c % 2][:, 0:CT]).then_inc(high_ready, 1)

            high_part(0)
            high_part(1)
            exp_logits(LK - 1)
            for c in range(NC):
                if c + 2 < NC:
                    high_part(c + 2)
                act.wait_ge(rest_ready, c + 1)
                nc.scalar.copy(SLO[:, c * CT:(c + 1) * CT], REST[0:EXPERTS, c * CT:(c + 1) * CT]).then_inc(lo_copied, 1)
            for z in range(NZ):
                if z >= 2:
                    deviation(2, z - 2)
                act.wait_ge(zx_used, (z + 1) * PAIRS // 2)
                nc.scalar.copy(LT[:, z * ZT:(z + 1) * ZT], PS[4 + z % 2][:, 0:ZT]).then_inc(lt_ready, 1)
            deviation(2, LK - 1)

        def outside_sums_out(act, c):
            act.wait_ge(nv_full, c + 1)
            nc.scalar.copy(NV[:, c * BC:(c + 1) * BC, :], PS[5 + c % 2][0:TOK, 0:BC * GRID].rearrange("p (b d) -> p b d", b=BC)
                           ).then_inc(nv_ready, 1)

        def turn_out(act, c):
            act.wait_ge(ot_full, c + 1)
            nc.scalar.copy(OT[:, c % 2, :], PS[7][0:GRID, 0:CT]).then_inc(ot_ready, 1)

        def tail_pool(pool):
            pool.wait_ge(tail_w, 16 * TAIL_LOADS)

            def square(n, k):
                a = slice(k * LB, (k + 1) * LB)
                pool.wait_ge(centred, n * LK + k + 1)
                nc.gpsimd.tensor_tensor(Y[:, a, 1, :] if n < 2 else SQ[:, a], TMP[:, a], TMP[:, a], ALU.mult).then_inc(squared, 1)

            for k in range(LK):
                square(0, k)
            nc.gpsimd.tensor_tensor(H, H, BP[:].unsqueeze(1).broadcast_to([TOK, NIMG, GRID]), ALU.add).then_inc(hb_ready, 1)

            def weigh_outside(c):
                a = slice(c * BC, (c + 1) * BC)
                pool.wait_ge(em_ready, c + 1)
                nc.gpsimd.tensor_tensor(NV[:, a].rearrange("p b (h e) -> p (b h) e", h=HEADS),
                                        NV[:, a].rearrange("p b (h e) -> p (b h) e", h=HEADS),
                                        emx[:, a].rearrange("p b h -> p (b h)").unsqueeze(2).broadcast_to([TOK, BC * HEADS, HD]),
                                        ALU.mult).then_inc(nw_ready, 1)

            pool.wait_ge(nv_ready, NC)
            for i in range(LN_STEP + (LK - 1) * LB + 2):
                if i < NIMG:
                    pool.wait_ge(max_ready, i + 1)
                    nc.gpsimd.tensor_tensor(PR[:, i % 4], PR[:, i % 4],
                                            smx[:, i, :].unsqueeze(2).broadcast_to([TOK, HEADS, TOK]),
                                            ALU.subtract).then_inc(sub_ready, 1)
                if i < 2 * SELECTED:
                    r, e = 64 * (i // SELECTED), i % SELECTED * 8
                    pool.wait_ge(sub_ready, i + 1)
                    nc.gpsimd.tensor_copy(SEL[r:r + EXPERTS].rearrange("p a n -> p (a n)").rearrange("p (e n) -> p e n", e=EXPERTS)[:, e:e + 8],
                                          ident[r:r + EXPERTS, r + e:r + e + 8].unsqueeze(2).broadcast_to([EXPERTS, 8, GRID])
                                          ).then_inc(sel_ready, 1)
                    pool.wait_ge(sel_ready, i + 1)
                if BC <= i <= NIMG and i % BC == min(1, NIMG - i):
                    weigh_outside(i // BC - 1)
                if i > LN_STEP and (i - LN_STEP - 1) % LB == 0:
                    square(1, (i - LN_STEP - 1) // LB)
            for k in range(LK):
                a = slice(k * LB, (k + 1) * LB)
                pool.wait_ge(chosen, k + 1)
                pool.wait_ge(lx_ready, k + 1)
                nc.gpsimd.tensor_tensor(SC[:, a], SC[:, a], TMP[:, a], ALU.mult).then_inc(weighed, 1)
            for c in range(NC):
                t = slice(c * CT, (c + 1) * CT)
                pool.wait_ge(lo_copied, c + 1)
                nc.gpsimd.tensor_tensor(SLO[:, t], REST[0:EXPERTS, t], SLO[:, t], ALU.subtract).then_inc(lo_ready, 1)
            whole = [TOK, NIMG, GRID]
            nc.gpsimd.tensor_tensor(H, H, LNB[:].unsqueeze(1).broadcast_to(whole), ALU.add).then_inc(hl_ready, 1)
            nc.gpsimd.tensor_tensor(SC, Y[:, :, 0, :], OB[:].unsqueeze(1).broadcast_to(whole), ALU.add).then_inc(ob_ready, 1)
            pool.wait_ge(hl_ready, 1)
            for k in range(LK):
                square(2, k)
                if k < LK - 1:
                    a = slice(k * LB, (k + 1) * LB)
                    pool.wait_ge(ln_ready, k + 1)
                    nc.gpsimd.tensor_tensor(TMP[:, a], TMP[:, a], LNG[:].unsqueeze(1).broadcast_to([TOK, LB, GRID]), ALU.mult
                                            ).then_inc(scaled, 1)
                    pool.wait_ge(scaled, k + 1)
                    nc.gpsimd.tensor_tensor(TMP[:, a], TMP[:, a], H[:, a], ALU.add).then_inc(out_ready, 1)

        def tail_vector(dve):
            steps = [0]

            def link(ins):
                steps[0] += 1
                ins.then_inc(dve_step, 1)
                dve.wait_ge(dve_step, steps[0])

            def over(x, n=LB):
                return x.unsqueeze(2).broadcast_to([TOK, n, GRID])

            def rows(x, n):
                return x.unsqueeze(1).broadcast_to([TOK, n, GRID])

            def centre(src, k):
                a = slice(k * LB, (k + 1) * LB)
                link(nc.vector.reduce_sum(st[:, 0, a], src[:, a], AX.X))
                link(nc.vector.tensor_scalar(st[:, 0, a], st[:, 0, a], 1.0 / GRID, None, ALU.mult))
                nc.vector.tensor_tensor(TMP[:, a], src[:, a], over(st[:, 0, a]), ALU.subtract).then_inc(centred, 1)

            def deviations(squares, n, k):
                a = slice(k * LB, (k + 1) * LB)
                dve.wait_ge(squared, n * LK + k + 1)
                link(nc.vector.reduce_sum(st[:, 1, a], squares[:, a], AX.X))
                nc.vector.tensor_scalar(st[:, 1, a], st[:, 1, a], 1.0 / GRID, EPS, ALU.mult, ALU.add).then_inc(var_ready, 1)
                dve.wait_ge(dev_ready, n * LK + k + 1)
                link(nc.vector.reciprocal(st[:, 3, a], st[:, 2, a]))
                return a

            dve.wait_ge(tail_w, 16 * TAIL_LOADS)
            dve.wait_ge(h_in, 32)
            for k in range(LK + 1):
                if k == LK - 1:
                    dve.wait_ge(last_h_in, 16)
                if k < LK:
                    centre(H, k)
                if k:
                    a = deviations(Y[:, :, 1, :], 0, k - 1)
                    nc.vector.tensor_tensor(Y[:, a, 0, :], TMP[:, a], over(st[:, 3, a]), ALU.mult).then_inc(y_ready, 1)
            nc.vector.memset(V[:, :, :, HD:VH], 1.0).then_inc(ones_set, 1)
            for c in range(NC):
                heads = lambda x: x.rearrange("p b (h e) -> p b h e", h=HEADS)
                dve.wait_ge(v_full, c + 1)
                nc.vector.tensor_tensor(V[:, c * BC:(c + 1) * BC, :, 0:HD],
                                        heads(PS[4][0:TOK, 0:BC * GRID].rearrange("p (b d) -> p b d", b=BC)),
                                        heads(rows(BV[:], BC)), ALU.add).then_inc(v_ready, 1)

            def attended(c):
                a = slice(c * BC, (c + 1) * BC)
                heads = lambda x: x.rearrange("p b (h e) -> p (b h) e", h=HEADS)
                sums = PS[6][0:TOK, 0:BC * HEADS * VH].rearrange("p (n e) -> p n e", e=VH)
                inverse = rden[:, a, :].rearrange("p b h -> p (b h)")
                dve.wait_ge(o_full, (c + 1) * BC)
                nc.vector.reciprocal(inverse.unsqueeze(2), sums[:, :, HD:VH])
                dve.wait_ge(nw_ready, c + 1)
                link(nc.vector.tensor_tensor(heads(O[:, a, :]), sums[:, :, 0:HD], heads(NV[:, a, :]), ALU.subtract))
                nc.vector.tensor_tensor(heads(O[:, a, :]), heads(O[:, a, :]),
                                        inverse.unsqueeze(2).broadcast_to([TOK, BC * HEADS, HD]), ALU.mult).then_inc(o_ready, 1)

            def residual(c):
                a = slice(c * BC, (c + 1) * BC)
                dve.wait_ge(pj_full, c + 1)
                if c == 0:
                    dve.wait_ge(hb_ready, 1)
                nc.vector.tensor_tensor(H[:, a, :], PS[7][0:TOK, 0:BC * GRID].rearrange("p (b d) -> p b d", b=BC),
                                        H[:, a, :], ALU.add).then_inc(pj_ready, 1)

            for i in range(LN_STEP + (LK - 1) * LB + 3):
                if i < NIMG:
                    dve.wait_ge(s_full, i + 1)
                    if i >= 4:
                        dve.wait_ge(pt_full, i - 3)
                    nc.vector.tensor_tensor(
                        PR[:, i % 4].rearrange("p (a h) t -> p a (h t)", a=2), SPR[i % 2][0:TOK],
                        BAND4[:].unsqueeze(1).broadcast_to([TOK, 2, 4 * TOK]), ALU.mult).then_inc(s_ready, 1)
                    dve.wait_ge(s_ready, i + 1)
                    nc.vector.reduce_max(smx[:, i, :], PR[:, i % 4], AX.X).then_inc(max_ready, 1)
                if LAG + 1 <= i <= NIMG + LAG and (i - LAG - 1) % BC == BC - 1:
                    attended((i - LAG - 1) // BC)
                if LAG + 2 < i < NIMG + LAG + 3 and (i - LAG - 3) % BC == BC - 1:
                    residual((i - LAG - 3) // BC)
                if i >= LN_STEP and (i - LN_STEP) % LB == 0:
                    k = (i - LN_STEP) // LB
                    dve.wait_ge(pj_ready, (k + 1) * LB // BC)
                    centre(H, k)
                if i >= LN_STEP + 2 and (i - LN_STEP - 2) % LB == 0:
                    k = (i - LN_STEP - 2) // LB
                    a = deviations(Y[:, :, 1, :], 1, k)
                    nc.vector.tensor_tensor(Y[:, a], TMP[:, a].unsqueeze(2).broadcast_to([TOK, LB, 2, GRID]),
                                            st[:, 3, a].unsqueeze(2).unsqueeze(3).broadcast_to([TOK, LB, 2, GRID]), ALU.mult
                                            ).then_inc(y_ready, 1)
            link(nc.vector.memset(LG[:, :, EXPERTS:LW], SENTINEL))

            def choose(k):
                a = slice(k * LB, (k + 1) * LB)
                dve.wait_ge(lg_ready, (k + 1) * LB // BC)
                for b in range(k * LB, (k + 1) * LB):
                    m = nc.vector.max(M8[:, b, :], LG[:, b, 0:EXPERTS])
                link(m)
                link(nc.vector.tensor_tensor(SC[:, a], LG[:, a, 0:EXPERTS],
                                             M8[:, a, 0:1].broadcast_to([TOK, LB, EXPERTS]), ALU.subtract))
                dve.sem_inc(le_ready, 1)
                link(nc.vector.memset(M8[:, a, TOPK:8], SENTINEL))
                for b in range(k * LB, (k + 1) * LB):
                    m = nc.vector.match_replace(LR[:, b, :], M8[:, b, :], LG[:, b, :], -SENTINEL)
                link(m)
                nc.vector.tensor_tensor(TMP[:, a], LR[:, a, 0:EXPERTS], LG[:, a, 0:EXPERTS], ALU.not_equal).then_inc(chosen, 1)

            def expert_scores(k):
                a = slice(k * LB, (k + 1) * LB)
                dve.wait_ge(weighed, k + 1)
                link(nc.vector.reduce_sum(st[:, 0, a], SC[:, a], AX.X))
                link(nc.vector.reciprocal(st[:, 3, a], st[:, 0, a]))
                for b in range(k * LB, (k + 1) * LB, BC):
                    a, twice = slice(b, b + BC), [TOK, BC, 2, EXPERTS]
                    nc.vector.tensor_tensor(SC2[:, a], SC[:, a].unsqueeze(2).broadcast_to(twice),
                                            st[:, 3, a].unsqueeze(2).unsqueeze(3).broadcast_to(twice), ALU.mult).then_inc(sc_ready, 1)

            def high_and_middle(k):
                for c in range(k * LB // BC, (k + 1) * LB // BC):
                    t = slice(c * CT, (c + 1) * CT)
                    dve.wait_ge(high_ready, c + 1)
                    nc.vector.tensor_tensor(REST[:, t], PS[6 + c % 2][:, 0:CT], SHM[:, t], ALU.subtract).then_inc(rest_ready, 1)
                    dve.wait_ge(rest_ready, c + 1)
                    nc.vector.tensor_copy(SHM[64:128, t], REST[64:128, t]).then_inc(mid_ready, 1)

            for k in range(LK + 2):
                if k < LK:
                    choose(k)
                if 1 <= k <= LK:
                    expert_scores(k - 1)
                if k >= 2:
                    high_and_middle(k - 2)
            F = SC

            def add_projection(c):
                a = slice(c * BC, (c + 1) * BC)
                if c == 0:
                    dve.wait_ge(ob_ready, 1)
                dve.wait_ge(f_full, c + 1)
                nc.vector.tensor_tensor(F[:, a, :], PS[6 + c % 2][0:TOK, 0:BC * GRID].rearrange("p (b d) -> p b d", b=BC),
                                        F[:, a, :], ALU.add).then_inc(f_ready, 1)

            def centre_last(k):
                dve.wait_ge(f_ready, (k + 1) * LB // BC)
                centre(F, k)

            def finish_last(k):
                a = deviations(SQ, 2, k)
                nc.vector.tensor_tensor(TMP[:, a], TMP[:, a], over(st[:, 3, a]), ALU.mult).then_inc(ln_ready, 1)

            for n in range(NZ * PAIRS):
                z = n // PAIRS
                dve.wait_ge(bc_full, n + 1)
                if n >= ZR and n % 2 == 0:
                    dve.wait_ge(zx_used, (n - ZR) // 2 + 1)
                nc.vector.tensor_tensor(ZX[:, n % ZR, :], PS[n % 4][:, 0:ZT], YT[:, z * ZT:(z + 1) * ZT], ALU.mult
                                        ).then_inc(zx_ready, 1)
                if n in ADD_AT:
                    add_projection(ADD_AT.index(n))
                if n in CENTRE_AT:
                    centre_last(CENTRE_AT.index(n))
                if n in FINISH_AT:
                    finish_last(FINISH_AT.index(n))
            for c in range(len(ADD_AT), NC):
                add_projection(c)
            centre_last(LK - 1)
            finish_last(LK - 1)
            a = slice(NIMG - LB, NIMG)
            dve.wait_ge(ln_ready, LK)
            link(nc.vector.tensor_tensor(TMP[:, a], TMP[:, a], rows(LNG[:], LB), ALU.mult))
            nc.vector.tensor_tensor(TMP[:, a], TMP[:, a], H[:, a], ALU.add).then_inc(last_ready, 1)

        block = ctx.enter_context(nc.Block())

        @block.sync
        def _(sp):
            half = PIX // 2
            sp.dma_start(ident[:], ident_in).then_inc(first_consts, 16)
            sp.dma_start(XALL[:, 0:half], xall[:, 0:half]).then_inc(input_in[0], 16)
            sp.dma_start(DW[:], dft_w).then_inc(first_consts, 16)
            sp.dma_start(XALL[:, half:], xall[:, half:]).then_inc(input_in[1], 16)
            for dst, src in [(DH, dft_h), (EH[0:KOUT], idft_h), (EH[64:64 + KOUT], idft_h),
                             (EW, idft_w), (CWALL, conv_wb), (W1, fc1_w), (B1, fc1_b), (W2, fc2_w), (B2, fc2_b)]:
                sp.dma_start(dst[:], src).then_inc(consts, 16)
            sp.wait_ge(ring_zeroed, 1)
            for c in stored:
                sp.sem_inc(c.sem, c.credit)
            turn, passes = Turns(sp, "layer", LAYER_COUNTS), Turns(sp, "pass", PASS_COUNTS)

            def load_piece(kyg, layer):
                slot = SLOT[kyg]
                if slot == RING:
                    turn.wait(cleared, CLEARS)
                elif slot in SLOT[:kyg]:
                    turn.wait(piece_used, SLOT.index(slot) + 1)
                else:
                    turn.wait(piece_used, KYG - SLOT[::-1].index(slot) - KYG)
                for j in range(B4):
                    sp.dma_start(pieces[slot][j * CH:(j + 1) * CH, j, :],
                                 spec_w[bass.ds(layer, 1), kyg, j].rearrange("l c n -> (l c) n")
                                 ).then_inc(piece_in[slot].sem, 16)

            def layer(p, l, first):
                if first:
                    sp.dma_start(W0[:], fc0_all[:, bass.ds(p * NG, NG), :]).then_inc(w0_in.sem, 16)
                for kyg in range(RING):
                    load_piece(kyg, l)
                if first:
                    passes.wait(pass_done, 1)
                    sp.dma_start(W0T, fc0_t[:, bass.ds(p * NG, NG), :]).then_inc(w0t_in.sem, 16)
                    sp.dma_start(XALL, xall).then_inc(co_in.sem, 16)
                load_piece(RING, l)
                modes = spec_scr.rearrange("k r b (y o) -> (k r) y b o", y=MODES)

                def load_modes(n, ky, count):
                    r = 64 * (n % 2)
                    for b in range(B4):
                        sp.dma_start(MODE[r:r + KOUT, ky].rearrange("p y (b o) -> p y b o", b=B4)[:, :, b],
                                     modes[:, ky, n * B4 + b]).then_inc(count.sem, 16)

                def load_part(i):
                    turn.wait(stored[i], 1)
                    load_modes(0, slice(4 * PARTS[i][0], 4 * PARTS[i][1]), loaded_first[i])

                for d in range(KYG):
                    if RING + 1 + d < KYG:
                        load_piece(RING + 1 + d, l)
                    turn.wait(mix_ready, -(-(d + 1) * KXD // 4))
                    sp.dma_start(
                        spec_scr.rearrange("(x q) r b (y n) -> (q r b) x y n", q=B4, y=KYG)[:, :, d],
                        MIXED[:, d * MODES * CH:(d + 1) * MODES * CH].rearrange("p (x n) -> p x n", x=KXD)
                    ).then_inc(stored[int(d >= PARTS[1][0])].sem, 16)
                for i in range(len(PARTS)):
                    load_part(i)
                for n in range(1, NG):
                    if n >= 2:
                        turn.wait(g_full, (n - 1) * N_G)
                    load_modes(n, slice(0, MODES), loaded[n])

            with sp.Fori(0, PASSES) as p:
                layer(p, 0, True)
                turn.next()
                with sp.Fori(1, LAYERS) as l:
                    layer(p, l, False)
                    turn.next()
                for n in range(NG):
                    passes.wait(fc2_ready, 4 * (n + 1))
                    for tile in range(4):
                        qp, pr = tile // 2, tile % 2
                        sp.dma_start(
                            hid_scr[bass.ds(p, 1), n, pr].rearrange("o b (d q n) -> q (o b) d n", d=4, q=2)[qp],
                            HO[32 * tile:32 * tile + 2]).then_inc(ho_out.sem, 16)
                passes.next()
            sp.wait_ge(ho_out.sem, PASSES * NG * 64)
            tail_sync(sp)

        @block.tensor
        def _(pe):
            pe.wait_ge(first_consts, 32)
            pe.wait_ge(psum_zeroed, 1)
            pe.wait_ge(credits, 1)
            pe.sem_inc(t1_full.sem, t1_full.credit - N_XT)
            for c in (tr_full, sp_full, piece_used, gt_full, x_full):
                pe.sem_inc(c.sem, c.credit)

            def transpose_x(bank, x, q):
                for i in range(4):
                    c = q * BANK + i * 128
                    m = pe.transpose(bank[:, i * 128:(i + 1) * 128], x[:, c:c + 128], ident[:])
                m.then_inc(xt_full.sem, 1)

            def dft_columns(k):
                for i in range(4):
                    m = pe.matmul(t1_bank[k % 2][:, i * H2 * KOUT:(i + 1) * H2 * KOUT],
                                  XT[:, k % 2, i * 128:(i + 1) * 128], DW[:], start=True, stop=True)
                m.then_inc(t1_full.sem, 1)

            for j in range(N_XT + 1):
                if j < N_XT:
                    if j % (N_XT // 2) == 0:
                        pe.wait_ge(input_in[j // (N_XT // 2)], 16)
                    if j >= 2:
                        pe.wait_ge(xt_ready.sem(j), 1 + j // 2)
                    transpose_x(xt_bank[j % 2], XALL, j)
                if j:
                    pe.wait_ge(xt_ready.sem(j - 1), 2 + (j - 1) // 2)
                    if j >= 3:
                        pe.wait_ge(t1_ready.sem, j - 2)
                    dft_columns(j - 1)
            pe.wait_ge(t1_ready.sem, N_XT)
            pe.wait_ge(consts, 16 * CONST_LOADS)

            turn, cols, passes = Turns(pe, "layer", LAYER_COUNTS), Turns(pe, "cols", COLUMN_COUNTS), Turns(pe, "pass", PASS_COUNTS)

            def fc0_pointwise():
                turn.wait(cw_set, 1)
                passes.wait(w0t_in, 1)
                for n in range(NG):
                    m = pe.matmul(xt_bank[0][:, n * 128:(n + 1) * 128], W0T[:, n, :], CW[:, 0:128], start=True, stop=True)
                m.then_inc(w0c_full.sem, 1)

            def transpose(k):
                if k < 2:
                    turn.wait(x_ready, k - 3)
                cols.wait_job(xt_ready, k - 2)
                transpose_x(xt_bank[k % 2], X[:, k // N_XT, :], k % N_XT)

            def columns(k):
                cols.wait_job(xt_ready, k)
                if k < 2:
                    turn.wait(x_ready, k - 1)
                else:
                    cols.wait(t1_ready, k - 1)
                dft_columns(k)

            def rows_onto_partitions(n, j, first):
                m0 = n * N_TR + j
                if m0 < 2:
                    turn.wait(gt_ready, m0 - 1)
                else:
                    turn.wait_job(tr_ready, m0 - 2)
                if m0 == 0 and first:
                    passes.wait(w0_in, 1)
                elif j == 0 and not first:
                    cols.wait(t1_ready, (n + 1) * N_XT)
                for i in range(4):
                    ky = 4 * j + i
                    dst = tr_bank[m0 % 2][:, i * 128:(i + 1) * 128]
                    if first:
                        m = pe.matmul(dst, T1C[:, RI * ky:RI * (ky + 1), :].rearrange("p r h -> p (r h)"),
                                      W0[:, n, :], start=True, stop=True)
                    else:
                        m = pe.transpose(dst, T1[:, n % 2, RI * ky:RI * (ky + 1), :].rearrange("p r h -> p (r h)"), ident[:])
                m.then_inc(tr_full.sem, 1)

            def dft_rows(n, kyg):
                j, ki = kyg // SPK, kyg % SPK
                turn.wait_job(tr_ready, n * N_TR + kyg)
                if ki == 0:
                    if n:
                        turn.wait(sp_ready, (n - 1) * N_F + j + 1)
                    else:
                        turn.wait(g_ready, j - 1)
                for b in range(B4):
                    m = pe.matmul(sp_bank[j][:, (ki * B4 + b) * KOUT:(ki * B4 + b + 1) * KOUT],
                                  TR[:, n % 2, b, 4 * kyg:4 * kyg + 4, :].rearrange("p k c -> p (k c)"), DH[:],
                                  start=True, stop=True)
                if ki == SPK - 1 or kyg == KYG - 1:
                    m.then_inc(sp_full.sem, 1)

            def mix():
                for blk in range(MIXB):
                    kyg, kxd, job = blk // KXD, blk % KXD, blk // 4
                    if blk == 0:
                        turn.wait(sp_ready, (NG - 1) * N_F + 1)
                    if blk == SPK * KXD:
                        turn.wait(sp_ready, NG * N_F)
                    if kxd == 0:
                        turn.wait(piece_in[SLOT[kyg]], SLOT[:kyg + 1].count(SLOT[kyg]))
                    if blk % 4 == 0 and job >= 2:
                        turn.wait(mix_ready, job - 1)
                    for q in range(B4):
                        c = (4 * kxd + q) * CH
                        m = pe.matmul(mix_bank[job % 2][32 * q:32 * q + RI * GIMG, (blk % 4) * 128:(blk % 4 + 1) * 128],
                                      SPEC[:, kyg, 4 * kxd + q, :], pieces[SLOT[kyg]][:, :, c:c + CH],
                                      start=True, stop=True, tile_position=(0, 32 * q))
                    if kxd == KXD - 1:
                        m.then_inc(piece_used.sem, 1)
                    if blk % 4 == 3 or blk == MIXB - 1:
                        if kxd == KXD - 1:
                            m = pe.matmul(mix_bank[job % 2][32 * q:32 * q + RI * GIMG, (blk % 4) * 128:(blk % 4 + 1) * 128],
                                          SPEC[:, kyg, 4 * kxd + q, :], pieces[SLOT[kyg]][:, :, c:c + CH],
                                          start=True, stop=True, tile_position=(0, 32 * q))
                        m.then_inc(mix_full.sem, 1)

            def pointwise(u, first):
                if u == 0:
                    turn.wait(cw_set, 1)
                    if first:
                        passes.wait(w0c_ready, 1)
                        passes.wait(co_in, 1)
                elif u == 2:
                    turn.wait(mix_ready, N_MIX)
                elif u >= 4:
                    turn.wait(x_ready, u + 1 - 4)
                n, q = u // N_X, u % N_X
                pe.matmul(x_bank[u % 4][:, :], W0C[:, n, :] if first else CW[:, 0:128],
                          (XALL if first else X[:, n])[:, q * BANK:(q + 1) * BANK],
                          start=True, stop=True, skip_group_check=True)

            def inverse_rows(n, j):
                m0, r = n * N_G + j, 64 * (n % 2)
                if n == 0:
                    for i, part in enumerate(PARTS):
                        if j == part[0]:
                            turn.wait(loaded_first[i], 1)
                elif j == 0:
                    turn.wait(loaded[n], 1)
                if m0 >= 2:
                    turn.wait(g_ready, m0 - 1)
                for i in range(4):
                    m = pe.matmul(g_bank[m0 % 2][:, i * 128:(i + 1) * 128], MODE[r:r + KOUT, 4 * j + i, :],
                                  EH[r:r + KOUT, :], start=True, stop=True)
                m.then_inc(g_full.sem, 1)

            def turn_back(u):
                n, q = u // N_X, u % N_X
                if q == 0:
                    turn.wait(g_ready, (n + 1) * N_G)
                if u >= 2:
                    turn.wait(gt_ready, u - 1)
                for i in range(4):
                    hh = 4 * q + i
                    m = pe.transpose(gt_bank[u % 2][0:H2 * KOUT, i * 128:(i + 1) * 128],
                                     G[:, n % 2, H2 * RI * hh:H2 * RI * (hh + 1), :].rearrange("p a b -> p (a b)"), ident[:])
                m.then_inc(gt_full.sem, 1)

            def inverse_columns(u):
                turn.wait(gt_ready, u + 1)
                for i in range(4):
                    m = pe.matmul(x_bank[u % 4][:, i * 128:(i + 1) * 128], GT[:, u % 4, i, :], EW[:],
                                  start=False, stop=True, skip_group_check=True)
                m.then_inc(x_full.sem, 1)

            def layer(first):
                for stage, k in FIRST_FORWARD if first else FORWARD:
                    if stage == "transpose":
                        transpose(k)
                    elif stage == "columns":
                        columns(k)
                    elif stage == "turn":
                        rows_onto_partitions(*k, first)
                    elif stage == "rows":
                        dft_rows(*k)
                if first:
                    fc0_pointwise()
                mix()
                for stage, u in INVERSE:
                    if stage == "pointwise":
                        pointwise(u, first)
                    elif stage == "modes":
                        inverse_rows(*u)
                    elif stage == "turn_back":
                        turn_back(u)
                    else:
                        inverse_columns(u)

            with pe.Fori(0, PASSES) as p:
                layer(True)
                turn.next()
                with pe.Fori(1, LAYERS) as l:
                    layer(False)
                    turn.next()
                    cols.next()
                turn.wait(x_ready, 0)
                turn.wait(gt_ready, 0)
                turn.wait(g_ready, 0)
                for m0 in range(NP // 2 + 1):
                    if m0 < NP // 2:
                        for i in range(FB):
                            k = FB * m0 + i
                            u, pr = k // 2, k % 2
                            if k >= 4:
                                passes.wait(fc1_ready, k - 3)
                            pe.matmul(PS[4 + k % 4][:, :], W1[:, pr, :], X[:, u // N_X, u % N_X * BANK:(u % N_X + 1) * BANK],
                                      start=True, stop=True).then_inc(fc1_full.sem, 1)
                    if m0:
                        if m0 >= 3:
                            passes.wait(fc2_ready, m0 - 2)
                        passes.wait(fc1_ready, FB * m0)
                        for i in range(FB):
                            m = pe.matmul(PS[(m0 - 1) % 2][32 * i:32 * i + 32, :], W2[:], FH[:, (m0 - 1) % 2 * FB + i, :],
                                          start=True, stop=True, tile_position=(0, 32 * i))
                        m.then_inc(fc2_full.sem, 1)
                passes.wait(fc2_ready, NP // 2)
                passes.next()
            tail_tensor(pe)

        @block.scalar
        def _(act):
            act.sem_inc(xt_ready.sem(1), 1)
            act.sem_inc(tr_ready.sem(1), 1)
            for c in (gt_ready, x_ready):
                act.sem_inc(c.sem, c.credit)
            for j in range(1, N_XT, 2):
                act.wait_ge(xt_full.sem, j + 1)
                if j >= 2:
                    act.wait_ge(t1_full.sem, 2 + j - 1)
                nc.scalar.copy(XT[:, j % 2, :], xt_bank[j % 2][:, :]).then_inc(xt_ready.sem(1), 1)
            act.wait_ge(consts, 16 * CONST_LOADS)
            turn, cols, passes = Turns(act, "layer", LAYER_COUNTS), Turns(act, "cols", COLUMN_COUNTS), Turns(act, "pass", PASS_COUNTS)

            def transposed(k):
                cols.wait(xt_full, k + 1)
                cols.wait(t1_full, k - 1)
                nc.scalar.copy(XT[:, k % 2, :], xt_bank[k % 2][:, :]).then_inc(xt_ready.sem(1), 1)

            def turned(n, j):
                m = n * N_TR + j
                turn.wait(tr_full, m + 1)
                turn.wait(sp_full, (n - 1) * N_F)
                nc.scalar.copy(TR[:, n % 2, :, 4 * j:4 * j + 4, :].rearrange("p b k c -> p k b c"),
                               tr_bank[m % 2][:, :].rearrange("p (k b c) -> p k b c", k=4, b=B4)
                               ).then_inc(tr_ready.sem(1), 1)

            def spectrum(n, j):
                turn.wait(sp_full, n * N_F + j + 1)
                ks = min(SPK, KYG - SPK * j)
                nc.scalar.copy(
                    SPEC[:, SPK * j:SPK * j + ks].rearrange("p k x (r b) -> p k (x r) b", r=RI)[:, :, :, n * B4:(n + 1) * B4],
                    sp_bank[j][:, 0:ks * B4 * KOUT].rearrange("p (k b n) -> p k n b", k=ks, b=B4)
                ).then_inc(sp_ready.sem, 1)

            def mixed():
                for j in range(N_MIX):
                    turn.wait(mix_full, j + 1)
                    if j == 0:
                        turn.wait_both(stored[0], 0, stored[1], 0)
                    w = min(BANK, MIXB * 128 - j * BANK)
                    nc.scalar.copy(MIXED[:, j * BANK:j * BANK + w], mix_bank[j % 2][:, 0:w]).then_inc(mix_ready.sem, 1)

            def turned_back(u):
                turn.wait(gt_full, u + 1)
                turn.wait(x_full, u + 1 - 4)
                nc.scalar.copy(GT[:, u % 4].rearrange("p h n -> p (h n)"),
                               gt_bank[u % 2][0:H2 * KOUT, :]).then_inc(gt_ready.sem, 1)

            def activated(u):
                turn.wait(x_full, u + 1)
                nc.scalar.activation(X[:, u // N_X, u % N_X * BANK:(u % N_X + 1) * BANK], x_bank[u % 4][:, :],
                                     ACT.Gelu, bias=CW[:, 128:129]).then_inc(x_ready.sem, 1)

            def layer(first):
                for stage, k in FIRST_FORWARD if first else FORWARD:
                    if stage == "transpose" and k % 2:
                        transposed(k)
                    elif stage == "turn" and (k[0] * N_TR + k[1]) % 2:
                        turned(*k)
                    elif stage == "rows" and (k[1] % SPK == SPK - 1 or k[1] == KYG - 1):
                        spectrum(k[0], k[1] // SPK)
                mixed()
                turn.wait(cw_set, 1)
                for stage, u in INVERSE:
                    if stage == "turn_back":
                        turned_back(u)
                    elif stage == "inverse":
                        activated(u)

            with act.Fori(0, PASSES) as p:
                layer(True)
                turn.next()
                with act.Fori(1, LAYERS) as l:
                    layer(False)
                    turn.next()
                    cols.next()
                for k in range(NF):
                    passes.wait(fc1_full, k + 1)
                    if k >= 2 * FB and k % FB == 0:
                        passes.wait(fc2_full, k // FB - 1)
                    nc.scalar.activation(FH[:, k % (2 * FB), :], PS[4 + k % 4][:, :], ACT.Gelu, bias=B1[:, 0:1]
                                         ).then_inc(fc1_ready.sem, 1)
                passes.next()
            tail_scalar(act)

        @block.vector
        def _(dve):
            for i in range(8):
                z = nc.vector.memset(PS[i], 0.0)
            z.then_inc(psum_zeroed, 1)
            dve.sem_inc(credits, 1)
            dve.sem_inc(xt_ready.sem(0), 1)
            dve.sem_inc(tr_ready.sem(0), 1)
            dve.sem_inc(g_ready.sem, g_ready.credit)

            def columns_out(j, q, dst):
                nc.vector.tensor_copy(dst[:, :, 8 * q:8 * q + 8],
                                      t1_bank[j % 2][:, 0:8 * KOUT].rearrange("p (h k) -> p k h", k=KOUT)
                                      ).then_inc(t1_ready.sem, 1)

            for j in range(N_XT + 1):
                if j < N_XT and j % 2 == 0:
                    dve.wait_ge(xt_full.sem, j + 1)
                    if j >= 2:
                        dve.wait_ge(t1_full.sem, 2 + j - 1)
                    nc.vector.tensor_copy(XT[:, 0, :], xt_bank[0][:, :]).then_inc(xt_ready.sem(0), 1)
                if j:
                    dve.wait_ge(t1_full.sem, 2 + j)
                    columns_out(j - 1, j - 1, T1C)
            dve.sem_inc(pass_done.sem, 1)
            dve.wait_ge(consts, 16 * CONST_LOADS)
            turn, cols, passes = Turns(dve, "layer", LAYER_COUNTS), Turns(dve, "cols", COLUMN_COUNTS), Turns(dve, "pass", PASS_COUNTS)

            def transposed(k):
                cols.wait(xt_full, k + 1)
                cols.wait(t1_full, k - 1)
                nc.vector.tensor_copy(XT[:, 0, :], xt_bank[0][:, :]).then_inc(xt_ready.sem(0), 1)

            def transformed(k):
                n, q = k // N_XT, k % N_XT
                cols.wait(t1_full, k + 1)
                if q == 0:
                    turn.wait(tr_full, (n - 1) * N_TR)
                columns_out(k, q, T1[:, n % 2])

            def turned(n, j):
                m = n * N_TR + j
                turn.wait(tr_full, m + 1)
                turn.wait(sp_full, (n - 1) * N_F)
                nc.vector.tensor_copy(TR[:, n % 2, :, 4 * j:4 * j + 4, :].rearrange("p b k c -> p k b c"),
                                      tr_bank[m % 2][:, :].rearrange("p (k b c) -> p k b c", k=4, b=B4)
                                      ).then_inc(tr_ready.sem(0), 1)

            def inverse_rows_out(n, j):
                m = n * N_G + j
                turn.wait(g_full, m + 1)
                if j == 0 and n >= 2:
                    turn.wait(gt_full, (n - 1) * N_X)
                nc.vector.tensor_copy(G[:, n % 2, :, 4 * j:4 * j + 4], g_bank[m % 2][:, :].rearrange("p (k r) -> p r k", k=4)
                                      ).then_inc(g_ready.sem, 1)

            def clear(j):
                if j == 0:
                    turn.wait(tr_full, (NG - 1) * N_TR)
                nc.vector.memset(pieces[RING][:, j * B4 // CLEARS, :], 0.0).then_inc(cleared.sem, 1)

            def layer(l, first):
                for stage, k in FIRST_FORWARD if first else FORWARD:
                    if stage == "transpose" and k % 2 == 0:
                        transposed(k)
                    elif stage == "columns":
                        transformed(k)
                    elif stage == "turn" and (k[0] * N_TR + k[1]) % 2 == 0:
                        turned(*k)
                    elif stage == "clear":
                        clear(k)
                turn.wait(x_ready, 0)
                nc.vector.tensor_copy(CW[:], CWALL[:, bass.ds(l, 1), :].rearrange("p o n -> p (o n)")).then_inc(cw_set.sem, 1)
                if first:
                    passes.wait(w0c_full, 1)
                    nc.vector.tensor_copy(XT[:, 1, :], xt_bank[0][:, :]).then_inc(w0c_ready.sem, 1)
                for stage, k in INVERSE:
                    if stage == "modes":
                        inverse_rows_out(*k)

            with dve.Fori(0, PASSES) as p:
                layer(0, True)
                turn.next()
                with dve.Fori(1, LAYERS) as l:
                    layer(l, False)
                    turn.next()
                    cols.next()
                turn.wait(gt_full, 0)
                for m in range(NP // 2):
                    if m % 4 == 0 and m:
                        passes.wait(ho_out, m // 4)
                    passes.wait(fc2_full, m + 1)
                    nc.vector.tensor_scalar(HO[:, m % 4, :], PS[m % 2], B2[:, 0:1], None, ALU.add
                                            ).then_inc(fc2_ready.sem, 1)
                passes.wait(ho_out, NG)
                dve.sem_inc(pass_done.sem, 1)
                passes.next()
            tail_vector(dve)

        @block.gpsimd
        def _(pool):
            nc.gpsimd.memset(SW[:], 0.0).then_inc(ring_zeroed, 1)
            pool.wait_ge(ring_zeroed, 1)
            for dst, src in [(WQKV, w_qkv), (BQK, b_qk), (BV, b_v), (WP, w_proj), (BP, b_proj), (GATE, gate_w),
                             (WO, out_w), (OB, out_b), (LNG, ln_g), (LNB, ln_b), (HM, head_mask),
                             (OUTSIDE, outside), (BAND4, band4)]:
                pool.dma_start(dst[:], src).then_inc(tail_w, 16)
            tail_pool(pool)


def constants():
    import numpy as np
    w = np.arange(GRID)
    k = np.arange(MODES)
    th = 2 * np.pi * np.outer(w, k) / GRID
    cos, sin = np.cos(th) / 8, np.sin(th) / 8
    fw = np.stack([cos, -sin], 2).reshape(GRID, KOUT)
    dft_w = np.zeros((H2, GRID, H2, KOUT))
    for i in range(H2):
        dft_w[i, :, i] = fw
    dft_h = np.zeros((RI, GRID, MODES, RI))
    dft_h[0, :, :, 0], dft_h[1, :, :, 0] = cos, sin
    dft_h[0, :, :, 1], dft_h[1, :, :, 1] = -sin, cos
    idft_h = np.zeros((MODES, RI, GRID, RI))
    idft_h[:, 0, :, 0], idft_h[:, 1, :, 0] = cos.T, -sin.T
    idft_h[:, 0, :, 1], idft_h[:, 1, :, 1] = sin.T, cos.T
    twice = np.where(k == 0, 1.0, 2.0)[:, None]
    bw = np.stack([twice * cos.T, -twice * sin.T], 0).reshape(KOUT, GRID)
    idft_w = np.zeros((H2, KOUT, H2, GRID))
    for i in range(H2):
        idft_w[i, :, i] = bw
    f = np.float32
    band = (np.abs(np.subtract.outer(np.arange(TOK), np.arange(TOK))) <= RADIUS).astype(f)
    return {
        "dft_w": dft_w.reshape(128, H2 * KOUT).astype(f), "dft_h": dft_h.reshape(128, KOUT).astype(f),
        "idft_h": idft_h.reshape(KOUT, GRID * RI).astype(f),
        "head_mask": np.kron(np.eye(HEADS, dtype=f), np.ones((HD, 1), f)),
        "outside": 1 - band, "band4": np.tile(band * f(HD ** -0.5), (1, 4)),
        "idft_w": idft_w.reshape(H2 * KOUT, H2 * GRID).astype(f), "ident": np.eye(128, dtype=f),
    }


def block_diagonal(w, n):
    import numpy as np
    k, m = w.shape
    out = np.zeros((n * k, n * m), w.dtype)
    for i in range(n):
        out[i * k:(i + 1) * k, i * m:(i + 1) * m] = w
    return out


def layout(inputs):
    import numpy as np
    a = {k: np.asarray(v) for k, v in inputs.items()}
    tok = {k[len("L0_tok_"):]: v for k, v in a.items() if k.startswith("L0_tok_")}
    d = constants()
    xa = np.ones((NIMG, 4, PIX), np.float32)
    xa[:, 0:3] = a["x"].reshape(NIMG, PIX, 3).transpose(0, 2, 1)
    d["xall"] = xa.reshape(128, PIX)
    w0a = np.zeros((NIMG, 4, NIMG // B4, B4, CH), np.float32)
    for b in range(NIMG):
        w0a[b, 0:3, b // B4, b % B4], w0a[b, 3, b // B4, b % B4] = tok["fc0_w"], tok["fc0_b"]
    d["fc0_all"] = w0a.reshape(128, NIMG // B4, 128)
    d["fc0_t"] = d["fc0_all"].transpose(2, 1, 0)
    sw = np.stack([tok[f"sw{i}"] for i in range(LAYERS)])
    sw = sw.reshape(LAYERS, CH, CH, MODES, KYG, B4)
    d["spec_w"] = sw.transpose(0, 4, 5, 1, 3, 2).reshape(LAYERS, KYG, B4, CH, MODES * CH)
    d["conv_wb"] = np.stack([np.concatenate([block_diagonal(tok[f"cw{i}"].T, B4), np.tile(tok[f"cb{i}"], B4)[:, None]], 1)
                             for i in range(LAYERS)], 1)
    w1 = np.zeros((2, 2, CH, 2, 2, FC), np.float32)
    for pr in range(2):
        for b in range(2):
            w1[pr, b, :, pr, b] = tok["fc1_w"]
    d["fc1_w"] = w1.reshape(128, 2, 128)
    d["fc1_b"] = np.tile(tok["fc1_b"], 2)[:, None]
    w2 = np.zeros((128, CH), np.float32)
    w2[0:FC, 0], w2[FC:128, 1] = tok["fc2_w"][:, 0], tok["fc2_w"][:, 0]
    d["fc2_w"] = w2
    d["fc2_b"] = np.repeat(tok["fc2_b"], 128)[:, None]
    att = {k[len("L0_attn_"):]: v for k, v in a.items() if k.startswith("L0_attn_")}
    ffn = {k[len("L0_ffn_"):]: v for k, v in a.items() if k.startswith("L0_ffn_")}
    d["w_qkv"], d["w_proj"] = att["w_qkv"], att["w_proj"]
    d["b_qk"] = att["b_qkv"][0:2 * GRID].reshape(2, GRID).T
    every = lambda v: np.tile(v, (TOK, 1))
    d["b_v"], d["b_proj"] = every(att["b_qkv"][2 * GRID:]), every(att["b_proj"])
    d["gate_w"], d["out_w"] = ffn["gate_w"].T, np.tile(ffn["out_w"].T, (2, 1))
    d["w_expert"] = ffn["lattice_weights"].reshape(EXPERTS // 2, 128, GRID).transpose(1, 0, 2)
    d["out_b"], d["ln_g"], d["ln_b"] = every(ffn["out_b"]), every(ffn["ln_g"]), every(ffn["ln_b"])
    d["cls_rows"] = np.tile(a["cls_tok"].reshape(1, 1, GRID), (1, NIMG, 1))
    return {k: np.ascontiguousarray(v) for k, v in d.items()}


INS = ["xall", "fc0_all", "fc0_t", "spec_w", "conv_wb", "fc1_w", "fc1_b", "fc2_w", "fc2_b",
       "w_qkv", "b_qk", "b_v", "w_proj", "b_proj", "gate_w", "w_expert", "out_w", "out_b", "ln_g", "ln_b", "cls_rows",
       "head_mask", "outside", "band4", "dft_w", "dft_h", "idft_h", "idft_w", "ident"]


def program(nc, arrays):
    args = [nc.dram_tensor(f"in_{n}", arrays[n].shape, F32, kind="ExternalInput").ap() for n in INS]
    args.append(nc.dram_tensor("spec_scr", (MODES, RI, GIMG, MODES * CH), F32).ap())
    args.append(nc.dram_tensor("hid_scr", (PASSES, NG, 2, 2, PIX), F32).ap())
    args.append(nc.dram_tensor("out", (NIMG, TOK, GRID), F32, kind="ExternalOutput").ap())
    vit_kernel(nc, *args)


def kernel(**inputs):
    import concourse.bacc as bacc
    from concourse.bass_utils import run_bass_kernel_spmd
    nc = bacc.Bacc("TRN2", target_bir_lowering=False, num_devices=1)
    arrays = layout(inputs)
    program(nc, arrays)
    r = run_bass_kernel_spmd(nc, [{f"in_{n}": arrays[n] for n in INS}], core_ids=[0])
    return r.results[0]["out"]
```
